# Optimizing a Trainium2 kernel written in Bass

```python
import numpy as np
import jax
import jax.numpy as jnp

def _softmax(x, axis=-1):
    return jax.nn.softmax(x, axis=axis)

def _gelu(x):
    return jax.nn.gelu(x, approximate=True)

def _silu(x):
    return jax.nn.silu(x)

def _sigmoid(x):
    return jax.nn.sigmoid(x)

def _layernorm(x, axis=-1, eps=1e-05):
    m = jnp.mean(x, axis=axis, keepdims=True)
    v = jnp.var(x, axis=axis, keepdims=True)
    return (x - m) / jnp.sqrt(v + eps)

def _scatter_add(tgt, idx, src, axis=0):
    return tgt.at[idx].add(src)

def _segment_sum(src, seg, n):
    return jax.ops.segment_sum(src, seg, n)
kernel_name = 'mk_metaformer_d4_conv_nhwc256_r4_af5ec4'

def setup_inputs(seed: int=0):
    np.random.seed(seed)
    _w = jnp.asarray

    def _rec_inputs():
        import jax
        import jax.numpy as jnp
        _gk = jax.random.key(seed)
        x = -0.0005207 + 1.001 * jax.random.normal(jax.random.fold_in(_gk, 1), (8, 32, 32, 64), jnp.float32)
        return x
    x = _rec_inputs()

    def _L0_conv_setup():
        import jax, jax.numpy as jnp
        import numpy as np
        D_MODEL = 64
        NB = 2
        D_STATE = 16
        D_CONV = 4
        D_INNER = 2 * D_MODEL
        HEADDIM = 16
        NHEADS = D_INNER // HEADDIM
        CONV_DIM = D_INNER + 2 * D_STATE
        D_IN_PROJ = 2 * D_INNER + 2 * D_STATE + NHEADS
        EPS = 1e-05

        def _mamba2_block(h, wi, cw, cb, dtb, a_log, d_skip, nw, wo):
            B, L, _ = h.shape
            zxbcdt = jnp.einsum('blc,pc->blp', h, wi)
            z = zxbcdt[..., :D_INNER]
            xBC = zxbcdt[..., D_INNER:D_INNER + CONV_DIM]
            dt = jax.nn.softplus(zxbcdt[..., -NHEADS:] + dtb)
            xBC = jax.lax.conv_general_dilated(xBC.swapaxes(1, 2), cw, window_strides=(1,), padding=[(D_CONV - 1, 0)], dimension_numbers=('NCH', 'OIH', 'NCH'), feature_group_count=CONV_DIM)
            xBC = jax.nn.silu((xBC + cb[None, :, None]).swapaxes(1, 2))
            xs = xBC[..., :D_INNER].reshape(B, L, NHEADS, HEADDIM)
            Bm = xBC[..., D_INNER:D_INNER + D_STATE]
            Cm = xBC[..., D_INNER + D_STATE:]
            A = -jnp.exp(a_log)
            dA = jnp.exp(dt * A)

            def step(s, inp):
                dA_t, dt_t, x_t, B_t, C_t = inp
                s = s * dA_t[:, :, None, None] + (dt_t[:, :, None] * x_t)[..., None] * B_t[:, None, None, :]
                y = jnp.einsum('bhps,bs->bhp', s, C_t)
                return (s, y)
            s0 = jnp.zeros((B, NHEADS, HEADDIM, D_STATE), dtype=h.dtype)
            _, ys = jax.lax.scan(step, s0, (dA.swapaxes(0, 1), dt.swapaxes(0, 1), xs.swapaxes(0, 1), Bm.swapaxes(0, 1), Cm.swapaxes(0, 1)))
            y = ys.swapaxes(0, 1) + d_skip[:, None] * xs
            y = y.reshape(B, L, D_INNER) * jax.nn.silu(z)
            y = y * jax.lax.rsqrt(jnp.mean(y * y, axis=-1, keepdims=True) + EPS) * nw
            return jnp.einsum('bld,cd->blc', y, wo)
        key = jax.random.key(seed)
        ks = jax.random.split(key, 10)
        x = jax.random.normal(ks[0], (8, 32, 32, D_MODEL), dtype=jnp.float32)
        in_proj_w = jax.random.normal(ks[1], (NB, D_IN_PROJ, D_MODEL), dtype=jnp.float32) * 0.02
        conv_w = jax.random.normal(ks[2], (NB, CONV_DIM, 1, D_CONV), dtype=jnp.float32) * 0.2
        conv_b = jax.random.normal(ks[3], (NB, CONV_DIM), dtype=jnp.float32) * 0.02
        dt_bias = jax.random.normal(ks[4], (NB, NHEADS), dtype=jnp.float32) * 0.5
        A_log = jnp.log(jax.random.uniform(ks[5], (NB, NHEADS), minval=1.0, maxval=16.0, dtype=jnp.float32))
        D = jax.random.normal(ks[6], (NB, NHEADS), dtype=jnp.float32) * 0.1 + 1.0
        norm_w = jnp.ones((NB, D_INNER), dtype=jnp.float32)
        out_proj_w = jax.random.normal(ks[7], (NB, D_MODEL, D_INNER), dtype=jnp.float32) * 0.02
        return {'x': x, 'in_proj_w': in_proj_w, 'conv_w': conv_w, 'conv_b': conv_b, 'dt_bias': dt_bias, 'A_log': A_log, 'D': D, 'norm_w': norm_w, 'out_proj_w': out_proj_w}
    _L0_conv_all = _L0_conv_setup()
    _L0_conv_in = {k: v for k, v in _L0_conv_all.items() if k in ('in_proj_w', 'conv_w', 'conv_b', 'dt_bias', 'A_log', 'D', 'norm_w', 'out_proj_w')}
    del _L0_conv_all

    def _L0_ffn_setup():
        import jax, jax.numpy as jnp
        import numpy as np
        BN_EPS = 0.001

        def _bn(h, g, b, m, v):
            return g * (h - m) * jax.lax.rsqrt(v + BN_EPS) + b
        key = jax.random.key(seed)
        ks = jax.random.split(key, 8)
        B, F, Df = (64, 16, 64)
        E, H, D = (8, 64, 64)
        s1 = 1.0 / np.sqrt(Df)
        s2 = 1.0 / np.sqrt(H)
        return {'x': jax.random.normal(ks[0], (B, F, Df), jnp.float32), 'Wr': jax.random.normal(ks[1], (Df, E), jnp.float32) * s1, 'br': jnp.zeros((E,), jnp.float32), 'W1': jax.random.normal(ks[2], (E, Df, H), jnp.float32) * s1, 'b1': jnp.zeros((E, H), jnp.float32), 'g1': jnp.ones((E, H), jnp.float32), 'be1': jnp.zeros((E, H), jnp.float32), 'm1': jnp.zeros((E, H), jnp.float32), 'v1': jnp.ones((E, H), jnp.float32), 'W2': jax.random.normal(ks[3], (E, H, H), jnp.float32) * s2, 'b2': jnp.zeros((E, H), jnp.float32), 'g2': jnp.ones((E, H), jnp.float32), 'be2': jnp.zeros((E, H), jnp.float32), 'm2': jnp.zeros((E, H), jnp.float32), 'v2': jnp.ones((E, H), jnp.float32), 'Wo': jax.random.normal(ks[4], (E, H, D), jnp.float32) * s2, 'bo': jnp.zeros((E, D), jnp.float32)}
    _L0_ffn_all = _L0_ffn_setup()
    _L0_ffn_in = {k: v for k, v in _L0_ffn_all.items() if k in ('Wr', 'br', 'W1', 'b1', 'g1', 'be1', 'm1', 'v1', 'W2', 'b2', 'g2', 'be2', 'm2', 'v2', 'Wo', 'bo')}
    del _L0_ffn_all

    def _L1_conv_setup():
        import jax, jax.numpy as jnp
        import numpy as np
        B, V, H, CIN, S = (32, 32, 32, 64, 64)
        key = jax.random.key(seed)
        k1, k2 = jax.random.split(key)
        x = jax.random.normal(k1, (B, V, H, CIN), dtype=jnp.float32)
        accumulators = jax.random.uniform(k2, (V, H, CIN, S), dtype=jnp.float32, minval=0.1, maxval=1.1)
        return {'x': x, 'accumulators': accumulators}
    _L1_conv_all = _L1_conv_setup()
    _L1_conv_in = {k: v for k, v in _L1_conv_all.items() if k in ('accumulators',)}
    del _L1_conv_all

    def _L1_ffn_setup():
        import jax, jax.numpy as jnp
        import numpy as np
        B, T, D, H, E = (16, 1024, 64, 128, 8)
        key = jax.random.key(seed)
        ks = jax.random.split(key, 5)
        x = jax.random.normal(ks[0], (B, T, D), dtype=jnp.float32)
        gate_w = jax.random.normal(ks[1], (D, E), dtype=jnp.float32) * 0.02
        gate_b = jnp.zeros((E,), dtype=jnp.float32)
        W1 = jax.random.normal(ks[2], (E, D, H), dtype=jnp.float32) * 0.02
        b1 = jnp.zeros((E, H), dtype=jnp.float32)
        W2 = jax.random.normal(ks[3], (E, H, D), dtype=jnp.float32) * 0.02
        b2 = jnp.zeros((E, D), dtype=jnp.float32)
        return {'x': x, 'gate_w': gate_w, 'gate_b': gate_b, 'W1': W1, 'b1': b1, 'W2': W2, 'b2': b2}
    _L1_ffn_all = _L1_ffn_setup()
    _L1_ffn_in = {k: v for k, v in _L1_ffn_all.items() if k in ('gate_w', 'gate_b', 'W1', 'b1', 'W2', 'b2')}
    del _L1_ffn_all

    def _L2_conv_setup():
        import jax, jax.numpy as jnp
        import numpy as np
        B, V, H, CIN, S = (32, 32, 32, 64, 64)
        key = jax.random.key(seed)
        k1, k2 = jax.random.split(key)
        x = jax.random.normal(k1, (B, V, H, CIN), dtype=jnp.float32)
        accumulators = jax.random.uniform(k2, (V, H, CIN, S), dtype=jnp.float32, minval=0.1, maxval=1.1)
        return {'x': x, 'accumulators': accumulators}
    _L2_conv_all = _L2_conv_setup()
    _L2_conv_in = {k: v for k, v in _L2_conv_all.items() if k in ('accumulators',)}
    del _L2_conv_all

    def _L2_ffn_setup():
        import jax, jax.numpy as jnp
        import numpy as np
        from jax import lax
        key = jax.random.key(seed)
        B, T, I, H = (16, 512, 64, 64)
        ks = jax.random.split(key, 13)
        s = 1.0 / np.sqrt(H)

        def w(k, shape):
            return jax.random.uniform(k, shape, jnp.float32, -s, s)
        return {'x': jax.random.normal(ks[0], (B, T, I), jnp.float32), 'U_i': w(ks[1], (I, H)), 'V_i': w(ks[2], (H, H)), 'b_i': w(ks[3], (H,)), 'U_f': w(ks[4], (I, H)), 'V_f': w(ks[5], (H, H)), 'b_f': w(ks[6], (H,)), 'U_c': w(ks[7], (I, H)), 'V_c': w(ks[8], (H, H)), 'b_c': w(ks[9], (H,)), 'U_o': w(ks[10], (I, H)), 'V_o': w(ks[11], (H, H)), 'b_o': w(ks[12], (H,))}
    _L2_ffn_all = _L2_ffn_setup()
    _L2_ffn_in = {k: v for k, v in _L2_ffn_all.items() if k in ('U_i', 'V_i', 'b_i', 'U_f', 'V_f', 'b_f', 'U_c', 'V_c', 'b_c', 'U_o', 'V_o', 'b_o')}
    del _L2_ffn_all

    def _L3_conv_setup():
        import jax, jax.numpy as jnp
        import numpy as np
        from jax import lax
        B, H, W, C = (4, 16, 16, 64)
        D_ATTN = 64
        KH = KW = 7
        BN_EPS = 1e-05
        key = jax.random.key(seed)
        ks = jax.random.split(key, 7)
        s = 0.02
        return {'x': jax.random.normal(ks[0], (B, H, W, C), jnp.float32), 'dw_kernel': jax.random.normal(ks[1], (KH, KW, C, 1), jnp.float32) * s, 'bn_gamma': jnp.ones((C,), jnp.float32), 'bn_beta': jnp.zeros((C,), jnp.float32), 'bn_mean': jnp.zeros((C,), jnp.float32), 'bn_var': jnp.ones((C,), jnp.float32), 'wq': jax.random.normal(ks[2], (C, D_ATTN), jnp.float32) * s, 'wk': jax.random.normal(ks[3], (C, D_ATTN), jnp.float32) * s, 'wv': jax.random.normal(ks[4], (C, D_ATTN), jnp.float32) * s, 'wo': jax.random.normal(ks[5], (D_ATTN, C), jnp.float32) * s, 'attn_scale': jnp.ones((), jnp.float32)}
    _L3_conv_all = _L3_conv_setup()
    _L3_conv_in = {k: v for k, v in _L3_conv_all.items() if k in ('dw_kernel', 'bn_gamma', 'bn_beta', 'bn_mean', 'bn_var', 'wq', 'wk', 'wv', 'wo', 'attn_scale')}
    del _L3_conv_all

    def _L3_ffn_setup():
        import jax, jax.numpy as jnp
        import numpy as np
        NUM_EXPERTS = 8
        TOP_K = 2
        B, S, D = (8, 2048, 64)

        def _moe(tokens, router_w, w1, b1, w2, b2):
            N = tokens.shape[0]
            E = router_w.shape[0]
            logits = tokens.astype(jnp.float32) @ router_w.astype(jnp.float32).T
            probs = jax.nn.softmax(logits, axis=-1)
            rw, re = jax.lax.top_k(probs, TOP_K)
            if TOP_K > 1:
                rw = rw / jnp.maximum(rw.sum(-1, keepdims=True), 1e-12)
            rw = rw.astype(tokens.dtype)
            combine = jnp.zeros((N, E), tokens.dtype).at[jnp.arange(N)[:, None], re].set(rw)
            out = tokens
            for e in range(E):
                h = jax.nn.gelu(tokens @ w1[e] + b1[e], approximate=False)
                y = h @ w2[e] + b2[e]
                out = out + combine[:, e:e + 1] * y
            return out
        key = jax.random.key(seed)
        ks = jax.random.split(key, 4)
        scale = 1.0 / np.sqrt(D).astype(np.float32)
        return {'input_embeddings': jax.random.normal(ks[0], (B, S, D), jnp.float32), 'router_w': jax.random.normal(ks[1], (NUM_EXPERTS, D), jnp.float32) * scale, 'w1': jax.random.normal(ks[2], (NUM_EXPERTS, D, D), jnp.float32) * scale, 'b1': jnp.zeros((NUM_EXPERTS, D), jnp.float32), 'w2': jax.random.normal(ks[3], (NUM_EXPERTS, D, D), jnp.float32) * scale, 'b2': jnp.zeros((NUM_EXPERTS, D), jnp.float32)}
    _L3_ffn_all = _L3_ffn_setup()
    _L3_ffn_in = {k: v for k, v in _L3_ffn_all.items() if k in ('router_w', 'w1', 'b1', 'w2', 'b2')}
    del _L3_ffn_all
    return {'x': x, 'L0_conv_in_proj_w': _L0_conv_in['in_proj_w'], 'L0_conv_conv_w': _L0_conv_in['conv_w'], 'L0_conv_conv_b': _L0_conv_in['conv_b'], 'L0_conv_dt_bias': _L0_conv_in['dt_bias'], 'L0_conv_A_log': _L0_conv_in['A_log'], 'L0_conv_D': _L0_conv_in['D'], 'L0_conv_norm_w': _L0_conv_in['norm_w'], 'L0_conv_out_proj_w': _L0_conv_in['out_proj_w'], 'L0_ffn_Wr': _L0_ffn_in['Wr'], 'L0_ffn_br': _L0_ffn_in['br'], 'L0_ffn_W1': _L0_ffn_in['W1'], 'L0_ffn_b1': _L0_ffn_in['b1'], 'L0_ffn_g1': _L0_ffn_in['g1'], 'L0_ffn_be1': _L0_ffn_in['be1'], 'L0_ffn_m1': _L0_ffn_in['m1'], 'L0_ffn_v1': _L0_ffn_in['v1'], 'L0_ffn_W2': _L0_ffn_in['W2'], 'L0_ffn_b2': _L0_ffn_in['b2'], 'L0_ffn_g2': _L0_ffn_in['g2'], 'L0_ffn_be2': _L0_ffn_in['be2'], 'L0_ffn_m2': _L0_ffn_in['m2'], 'L0_ffn_v2': _L0_ffn_in['v2'], 'L0_ffn_Wo': _L0_ffn_in['Wo'], 'L0_ffn_bo': _L0_ffn_in['bo'], 'L1_conv_accumulators': _L1_conv_in['accumulators'], 'L1_ffn_gate_w': _L1_ffn_in['gate_w'], 'L1_ffn_gate_b': _L1_ffn_in['gate_b'], 'L1_ffn_W1': _L1_ffn_in['W1'], 'L1_ffn_b1': _L1_ffn_in['b1'], 'L1_ffn_W2': _L1_ffn_in['W2'], 'L1_ffn_b2': _L1_ffn_in['b2'], 'L2_conv_accumulators': _L2_conv_in['accumulators'], 'L2_ffn_U_i': _L2_ffn_in['U_i'], 'L2_ffn_V_i': _L2_ffn_in['V_i'], 'L2_ffn_b_i': _L2_ffn_in['b_i'], 'L2_ffn_U_f': _L2_ffn_in['U_f'], 'L2_ffn_V_f': _L2_ffn_in['V_f'], 'L2_ffn_b_f': _L2_ffn_in['b_f'], 'L2_ffn_U_c': _L2_ffn_in['U_c'], 'L2_ffn_V_c': _L2_ffn_in['V_c'], 'L2_ffn_b_c': _L2_ffn_in['b_c'], 'L2_ffn_U_o': _L2_ffn_in['U_o'], 'L2_ffn_V_o': _L2_ffn_in['V_o'], 'L2_ffn_b_o': _L2_ffn_in['b_o'], 'L3_conv_dw_kernel': _L3_conv_in['dw_kernel'], 'L3_conv_bn_gamma': _L3_conv_in['bn_gamma'], 'L3_conv_bn_beta': _L3_conv_in['bn_beta'], 'L3_conv_bn_mean': _L3_conv_in['bn_mean'], 'L3_conv_bn_var': _L3_conv_in['bn_var'], 'L3_conv_wq': _L3_conv_in['wq'], 'L3_conv_wk': _L3_conv_in['wk'], 'L3_conv_wv': _L3_conv_in['wv'], 'L3_conv_wo': _L3_conv_in['wo'], 'L3_conv_attn_scale': _L3_conv_in['attn_scale'], 'L3_ffn_router_w': _L3_ffn_in['router_w'], 'L3_ffn_w1': _L3_ffn_in['w1'], 'L3_ffn_b1': _L3_ffn_in['b1'], 'L3_ffn_w2': _L3_ffn_in['w2'], 'L3_ffn_b2': _L3_ffn_in['b2']}

def reference(x, L0_conv_in_proj_w, L0_conv_conv_w, L0_conv_conv_b, L0_conv_dt_bias, L0_conv_A_log, L0_conv_D, L0_conv_norm_w, L0_conv_out_proj_w, L0_ffn_Wr, L0_ffn_br, L0_ffn_W1, L0_ffn_b1, L0_ffn_g1, L0_ffn_be1, L0_ffn_m1, L0_ffn_v1, L0_ffn_W2, L0_ffn_b2, L0_ffn_g2, L0_ffn_be2, L0_ffn_m2, L0_ffn_v2, L0_ffn_Wo, L0_ffn_bo, L1_conv_accumulators, L1_ffn_gate_w, L1_ffn_gate_b, L1_ffn_W1, L1_ffn_b1, L1_ffn_W2, L1_ffn_b2, L2_conv_accumulators, L2_ffn_U_i, L2_ffn_V_i, L2_ffn_b_i, L2_ffn_U_f, L2_ffn_V_f, L2_ffn_b_f, L2_ffn_U_c, L2_ffn_V_c, L2_ffn_b_c, L2_ffn_U_o, L2_ffn_V_o, L2_ffn_b_o, L3_conv_dw_kernel, L3_conv_bn_gamma, L3_conv_bn_beta, L3_conv_bn_mean, L3_conv_bn_var, L3_conv_wq, L3_conv_wk, L3_conv_wv, L3_conv_wo, L3_conv_attn_scale, L3_ffn_router_w, L3_ffn_w1, L3_ffn_b1, L3_ffn_w2, L3_ffn_b2):
    import jax
    import jax.numpy as jnp

    def _L0_conv_ref(x, in_proj_w, conv_w, conv_b, dt_bias, A_log, D, norm_w, out_proj_w):
        import jax, jax.numpy as jnp
        import numpy as np
        D_MODEL = 64
        NB = 2
        D_STATE = 16
        D_CONV = 4
        D_INNER = 2 * D_MODEL
        HEADDIM = 16
        NHEADS = D_INNER // HEADDIM
        CONV_DIM = D_INNER + 2 * D_STATE
        D_IN_PROJ = 2 * D_INNER + 2 * D_STATE + NHEADS
        EPS = 1e-05

        def _mamba2_block(h, wi, cw, cb, dtb, a_log, d_skip, nw, wo):
            B, L, _ = h.shape
            zxbcdt = jnp.einsum('blc,pc->blp', h, wi)
            z = zxbcdt[..., :D_INNER]
            xBC = zxbcdt[..., D_INNER:D_INNER + CONV_DIM]
            dt = jax.nn.softplus(zxbcdt[..., -NHEADS:] + dtb)
            xBC = jax.lax.conv_general_dilated(xBC.swapaxes(1, 2), cw, window_strides=(1,), padding=[(D_CONV - 1, 0)], dimension_numbers=('NCH', 'OIH', 'NCH'), feature_group_count=CONV_DIM)
            xBC = jax.nn.silu((xBC + cb[None, :, None]).swapaxes(1, 2))
            xs = xBC[..., :D_INNER].reshape(B, L, NHEADS, HEADDIM)
            Bm = xBC[..., D_INNER:D_INNER + D_STATE]
            Cm = xBC[..., D_INNER + D_STATE:]
            A = -jnp.exp(a_log)
            dA = jnp.exp(dt * A)

            def step(s, inp):
                dA_t, dt_t, x_t, B_t, C_t = inp
                s = s * dA_t[:, :, None, None] + (dt_t[:, :, None] * x_t)[..., None] * B_t[:, None, None, :]
                y = jnp.einsum('bhps,bs->bhp', s, C_t)
                return (s, y)
            s0 = jnp.zeros((B, NHEADS, HEADDIM, D_STATE), dtype=h.dtype)
            _, ys = jax.lax.scan(step, s0, (dA.swapaxes(0, 1), dt.swapaxes(0, 1), xs.swapaxes(0, 1), Bm.swapaxes(0, 1), Cm.swapaxes(0, 1)))
            y = ys.swapaxes(0, 1) + d_skip[:, None] * xs
            y = y.reshape(B, L, D_INNER) * jax.nn.silu(z)
            y = y * jax.lax.rsqrt(jnp.mean(y * y, axis=-1, keepdims=True) + EPS) * nw
            return jnp.einsum('bld,cd->blc', y, wo)
        B, H, W, C = x.shape
        h = x.reshape(B, H * W, C)
        for i in range(NB):
            h = _mamba2_block(h, in_proj_w[i], conv_w[i], conv_b[i], dt_bias[i], A_log[i], D[i], norm_w[i], out_proj_w[i])
        return h.reshape(B, H, W, C)

    def _L0_ffn_ref(x, Wr, br, W1, b1, g1, be1, m1, v1, W2, b2, g2, be2, m2, v2, Wo, bo):
        import jax, jax.numpy as jnp
        import numpy as np
        BN_EPS = 0.001

        def _bn(h, g, b, m, v):
            return g * (h - m) * jax.lax.rsqrt(v + BN_EPS) + b
        feat = jnp.mean(x, axis=0)
        w = jax.nn.softmax(feat @ Wr + br, axis=-1)
        h = jnp.einsum('bfd,edh->bfeh', x, W1) + b1
        h = jax.nn.relu(_bn(h, g1, be1, m1, v1))
        h = jnp.einsum('bfeh,ehk->bfek', h, W2) + b2
        h = jax.nn.relu(_bn(h, g2, be2, m2, v2))
        y = jnp.einsum('bfeh,ehd->bfed', h, Wo) + bo
        return jnp.einsum('bfed,fe->bfd', y, w)

    def _L1_conv_ref(x, accumulators):
        import jax, jax.numpy as jnp
        import numpy as np
        B, V, H, CIN, S = (32, 32, 32, 64, 64)
        log_w = jax.nn.log_softmax(jnp.log(accumulators), axis=2)
        xs = jnp.transpose(x, (1, 2, 0, 3))
        x_max = jnp.max(xs, axis=-1, keepdims=True)
        w_max = jnp.max(log_w, axis=2, keepdims=True)
        prod = jnp.einsum('vhbk,vhks->vhbs', jnp.exp(xs - x_max), jnp.exp(log_w - w_max))
        out_scopes_first = jnp.log(prod) + x_max + w_max
        return jnp.transpose(out_scopes_first, (2, 0, 1, 3))

    def _L1_ffn_ref(x, gate_w, gate_b, W1, b1, W2, b2):
        import jax, jax.numpy as jnp
        import numpy as np
        B, T, D, H, E = (16, 1024, 64, 128, 8)
        Bb, Tt, Dd = x.shape
        Ee = gate_w.shape[1]
        xf = x.reshape(-1, Dd)
        N = xf.shape[0]
        logits = xf @ gate_w + gate_b
        probs = jax.nn.softmax(logits, axis=-1)
        top2_vals, top2_idx = jax.lax.top_k(probs, 2)
        cw = jnp.zeros((N, Ee), dtype=xf.dtype).at[jnp.arange(N)[:, None], top2_idx].add(top2_vals)

        def step(acc, params):
            w1, bb1, w2, bb2, we = params
            h = jax.nn.gelu(xf @ w1 + bb1, approximate=False)
            y = h @ w2 + bb2
            return (acc + we[:, None] * y, None)
        out, _ = jax.lax.scan(step, jnp.zeros_like(xf), (W1, b1, W2, b2, cw.T))
        return out.reshape(Bb, Tt, Dd)

    def _L2_conv_ref(x, accumulators):
        import jax, jax.numpy as jnp
        import numpy as np
        B, V, H, CIN, S = (32, 32, 32, 64, 64)
        log_w = jax.nn.log_softmax(jnp.log(accumulators), axis=2)
        xs = jnp.transpose(x, (1, 2, 0, 3))
        x_max = jnp.max(xs, axis=-1, keepdims=True)
        w_max = jnp.max(log_w, axis=2, keepdims=True)
        prod = jnp.einsum('vhbk,vhks->vhbs', jnp.exp(xs - x_max), jnp.exp(log_w - w_max))
        out_scopes_first = jnp.log(prod) + x_max + w_max
        return jnp.transpose(out_scopes_first, (2, 0, 1, 3))

    def _L2_ffn_ref(x, U_i, V_i, b_i, U_f, V_f, b_f, U_c, V_c, b_c, U_o, V_o, b_o):
        import jax, jax.numpy as jnp
        import numpy as np
        from jax import lax
        B, T, _ = x.shape
        H = U_i.shape[1]
        xt = jnp.swapaxes(x, 0, 1)
        xi = xt @ U_i + b_i
        xf = xt @ U_f + b_f
        xg = xt @ U_c + b_c
        xo = xt @ U_o + b_o
        h0 = jnp.zeros((B, H), x.dtype)
        c0 = jnp.zeros((B, H), x.dtype)

        def step(carry, xs):
            h, c = carry
            xi_t, xf_t, xg_t, xo_t = xs
            i_t = jax.nn.sigmoid(xi_t + h @ V_i)
            f_t = jax.nn.sigmoid(xf_t + h @ V_f)
            g_t = jnp.tanh(xg_t + h @ V_c)
            o_t = jax.nn.sigmoid(xo_t + h @ V_o)
            c_new = h * c + i_t * g_t
            h_new = o_t * jnp.tanh(c_new)
            return ((h_new, c_new), h_new)
        (_, _), hs = lax.scan(step, (h0, c0), (xi, xf, xg, xo))
        return jnp.swapaxes(hs, 0, 1)

    def _L3_conv_ref(x, dw_kernel, bn_gamma, bn_beta, bn_mean, bn_var, wq, wk, wv, wo, attn_scale):
        import jax, jax.numpy as jnp
        import numpy as np
        from jax import lax
        B, H, W, C = (4, 16, 16, 64)
        D_ATTN = 64
        KH = KW = 7
        BN_EPS = 1e-05
        b, h, w, c = x.shape
        kern = jnp.transpose(dw_kernel, (0, 1, 3, 2))
        y = lax.conv_general_dilated(x, kern, window_strides=(1, 1), padding='SAME', dimension_numbers=('NHWC', 'HWIO', 'NHWC'), feature_group_count=c)
        y = jax.nn.relu(y)
        y = (y - bn_mean) * (bn_gamma / jnp.sqrt(bn_var + BN_EPS)) + bn_beta
        q = jnp.einsum('bhwc,cd->bhwd', y, wq).reshape(b, h * w, -1)
        k = jax.nn.relu(jnp.einsum('bhwc,cd->bhwd', y, wk)).reshape(b, h * w, -1)
        v = jnp.einsum('bhwc,cd->bhwd', y, wv).reshape(b, h * w, -1)
        scores = jnp.einsum('bqd,bkd->bqk', q, k) * attn_scale
        attn = jax.nn.softmax(scores, axis=-1)
        out = jnp.einsum('bqk,bkd->bqd', attn, v).reshape(b, h, w, -1)
        return jnp.einsum('bhwd,dc->bhwc', out, wo)

    def _L3_ffn_ref(input_embeddings, router_w, w1, b1, w2, b2):
        import jax, jax.numpy as jnp
        import numpy as np
        NUM_EXPERTS = 8
        TOP_K = 2
        B, S, D = (8, 2048, 64)

        def _moe(tokens, router_w, w1, b1, w2, b2):
            N = tokens.shape[0]
            E = router_w.shape[0]
            logits = tokens.astype(jnp.float32) @ router_w.astype(jnp.float32).T
            probs = jax.nn.softmax(logits, axis=-1)
            rw, re = jax.lax.top_k(probs, TOP_K)
            if TOP_K > 1:
                rw = rw / jnp.maximum(rw.sum(-1, keepdims=True), 1e-12)
            rw = rw.astype(tokens.dtype)
            combine = jnp.zeros((N, E), tokens.dtype).at[jnp.arange(N)[:, None], re].set(rw)
            out = tokens
            for e in range(E):
                h = jax.nn.gelu(tokens @ w1[e] + b1[e], approximate=False)
                y = h @ w2[e] + b2[e]
                out = out + combine[:, e:e + 1] * y
            return out
        b, s, d = input_embeddings.shape
        tokens = input_embeddings.reshape(b * s, d)
        return _moe(tokens, router_w, w1, b1, w2, b2).reshape(b, s, d)

    def _gn(v, G=32, eps=1e-05):
        B_, H_, W_, C_ = v.shape
        g = v.reshape(B_, H_, W_, G, C_ // G)
        m = jnp.mean(g, axis=(1, 2, 4), keepdims=True)
        s = jnp.var(g, axis=(1, 2, 4), keepdims=True)
        return ((g - m) / jnp.sqrt(s + eps)).reshape(v.shape)

    def _ln_c(v, eps=1e-06):
        m = jnp.mean(v, axis=-1, keepdims=True)
        s = jnp.var(v, axis=-1, keepdims=True)
        return (v - m) / jnp.sqrt(s + eps)

    def _ln_t(v, eps=1e-05):
        m = jnp.mean(v, axis=-1, keepdims=True)
        s = jnp.var(v, axis=-1, keepdims=True)
        return (v - m) / jnp.sqrt(s + eps)

    def _to_tokens(v):
        B_, H_, W_, C_ = v.shape
        return v.reshape(B_, H_ * W_, C_)

    def _from_tokens(t, like):
        return t.reshape(like.shape)
    x = x + _L0_conv_ref(_ln_c(x), L0_conv_in_proj_w, L0_conv_conv_w, L0_conv_conv_b, L0_conv_dt_bias, L0_conv_A_log, L0_conv_D, L0_conv_norm_w, L0_conv_out_proj_w)
    t = _to_tokens(x)
    t = t + _L0_ffn_ref(_ln_t(t), L0_ffn_Wr, L0_ffn_br, L0_ffn_W1, L0_ffn_b1, L0_ffn_g1, L0_ffn_be1, L0_ffn_m1, L0_ffn_v1, L0_ffn_W2, L0_ffn_b2, L0_ffn_g2, L0_ffn_be2, L0_ffn_m2, L0_ffn_v2, L0_ffn_Wo, L0_ffn_bo)
    x = _from_tokens(t, x)
    x = x + _L1_conv_ref(_ln_c(x), L1_conv_accumulators)
    t = _to_tokens(x)
    t = t + _L1_ffn_ref(_ln_t(t), L1_ffn_gate_w, L1_ffn_gate_b, L1_ffn_W1, L1_ffn_b1, L1_ffn_W2, L1_ffn_b2)
    x = _from_tokens(t, x)
    x = x + _L2_conv_ref(_ln_c(x), L2_conv_accumulators)
    t = _to_tokens(x)
    t = t + _L2_ffn_ref(_ln_t(t), L2_ffn_U_i, L2_ffn_V_i, L2_ffn_b_i, L2_ffn_U_f, L2_ffn_V_f, L2_ffn_b_f, L2_ffn_U_c, L2_ffn_V_c, L2_ffn_b_c, L2_ffn_U_o, L2_ffn_V_o, L2_ffn_b_o)
    x = _from_tokens(t, x)
    x = x + _L3_conv_ref(_ln_c(x), L3_conv_dw_kernel, L3_conv_bn_gamma, L3_conv_bn_beta, L3_conv_bn_mean, L3_conv_bn_var, L3_conv_wq, L3_conv_wk, L3_conv_wv, L3_conv_wo, L3_conv_attn_scale)
    t = _to_tokens(x)
    t = t + _L3_ffn_ref(_ln_t(t), L3_ffn_router_w, L3_ffn_w1, L3_ffn_b1, L3_ffn_w2, L3_ffn_b2)
    x = _from_tokens(t, x)
    return x

_drawn_inputs = setup_inputs


def setup_inputs(seed=0):
    import zlib

    import numpy as np

    out = dict(_drawn_inputs(seed))
    spreads = {'L0_conv_norm_w': (1.0, 0.6),
     'L0_ffn_br': (0.0, 0.1),
     'L0_ffn_b1': (0.0, 0.1),
     'L0_ffn_g1': (1.0, 0.2),
     'L0_ffn_be1': (0.0, 0.1),
     'L0_ffn_m1': (0.0, 0.1),
     'L0_ffn_v1': (1.0, 0.2),
     'L0_ffn_b2': (0.0, 0.1),
     'L0_ffn_g2': (1.0, 0.2),
     'L0_ffn_be2': (0.0, 0.1),
     'L0_ffn_m2': (0.0, 0.1),
     'L0_ffn_v2': (1.0, 0.567),
     'L0_ffn_bo': (0.0, 0.1),
     'L1_ffn_gate_b': (0.0, 0.364),
     'L1_ffn_b1': (0.0, 0.8),
     'L1_ffn_b2': (0.0, 0.1),
     'L3_conv_bn_gamma': (1.0, 0.6),
     'L3_conv_bn_beta': (0.0, 0.8),
     'L3_conv_bn_mean': (0.0, 0.78),
     'L3_conv_bn_var': (1.0, 0.6),
     'L3_ffn_b1': (0.0, 0.377),
     'L3_ffn_b2': (0.0, 0.344)}
    factors = {'L0_conv_in_proj_w': 3.078,
     'L0_conv_conv_w': 3.131,
     'L0_conv_conv_b': 3.343,
     'L0_conv_dt_bias': 8.0,
     'L0_conv_A_log': 8.0,
     'L0_conv_D': 8.0,
     'L0_conv_out_proj_w': 3.311,
     'L1_ffn_W1': 5.682,
     'L1_ffn_W2': 5.497,
     'L2_ffn_V_i': 5.924,
     'L2_ffn_b_i': 5.421,
     'L2_ffn_V_o': 5.921,
     'L2_ffn_b_o': 5.917,
     'L3_conv_dw_kernel': 8.0,
     'L3_conv_wq': 8.0,
     'L3_conv_wk': 8.0,
     'L3_conv_wv': 4.384,
     'L3_conv_wo': 5.569}
    for name, (base, spread) in spreads.items():
        noise = np.random.default_rng([zlib.crc32(name.encode()), seed]).standard_normal(out[name].shape)
        drawn = base * np.exp(spread * noise) if base else spread * noise
        out[name] = jnp.asarray(drawn.astype(out[name].dtype))
    for name, factor in factors.items():
        out[name] = (out[name] * factor).astype(out[name].dtype)
    return out
```

```python
from contextlib import ExitStack

import numpy as np

import concourse.bass as bass
from concourse import mybir

P = 128
B, IMG, C = 8, 32, 64
NT = IMG
TT = IMG
J, B4 = 2, 4
NB, DI, DS, NH, HD = 2, 128, 16, 8, 16
ZD = DI + NH
XBC = DI + 2 * DS
PROJ = ZD + XBC
E = 8
KT = 7
PADI = IMG + KT - 1
LB = 8
NEG = -1.0

F32 = mybir.dt.float32
ALU = mybir.AluOpType
ACT = mybir.ActivationFunctionType
AX = mybir.AxisListType.X


PACK = [
    ("ident", 128, 128), ("triblk", 128, 128), ("strictblk", 128, 128), ("indblk", 128, 128),
    ("tri32", 128, 32), ("maskb", 128, 4), ("ones", 1, 128),
]
for _b in range(NB):
    PACK += [(f"wzd{_b}", 64, ZD), (f"wxbc{_b}", 128, XBC), (f"taps{_b}", 128, 2 * XBC), (f"bias{_b}", 1, PROJ),
             (f"alog{_b}", 128, NH), (f"dskip{_b}", 128, NH), (f"normw{_b}", 128, 1), (f"wout{_b}", 128, 2 * C)]
PACK += [("wr", 64, E), ("br", 1, E), ("f0w1", 64, E * 64), ("f0w2", 128, 512), ("f0wo", 128, 512), ("f0bo", 1, 512)]
PACK += [(f"f0{_n}{_l}", 128, 4) for _l in (1, 2) for _n in ("b", "g", "be", "m", "v")]
PACK += [("m1gate", 64, E), ("m1gateb", 1, E), ("m1w1", 64, E * 128), ("m1b1", 128, 8), ("m1w2", 128, 512), ("m1b2", 1, 512)]
PACK += [("ugo", 65, 128), ("ui", 65, 64), ("vgo", 64, 128), ("vi", 64, 64)]
PACK += [("dw", 128, KT * KT), ("bng", 128, 1), ("bnb", 128, 1), ("bnm", 128, 1), ("bnv", 128, 1),
         ("wq", 64, 64), ("wk", 64, 64), ("wvT", 64, 64), ("wo3", 64, 64), ("ascale", 128, 1)]
PACK += [("m2gate", 64, E), ("m2gateb", 1, E), ("m2w1", 64, E * 64), ("m2b1", 128, 4), ("m2w2", 128, 512), ("m2b2", 1, 512)]
COL = {}
_at = 0
for _n, _r, _c in PACK:
    COL[_n] = (_r, _at, _c)
    _at += _c
NPACK = _at

DVE_A = 19


class Steps:

    def __init__(self, eng, sem, tile, per_tile):
        self.eng, self.sem, self.base, self.per, self.n = eng, sem, tile * per_tile, per_tile, 0

    def did(self, ins):
        ins.then_inc(self.sem, 1)
        self.n += 1

    def wait(self):
        self.eng.wait_ge(self.sem, self.base + self.n)

    def end(self):
        assert self.n == self.per, (self.sem, self.n, self.per)


def bc(ap, axis, n):
    ap = ap.unsqueeze(axis)
    shape = list(ap.shape)
    shape[axis] = n
    return ap.broadcast_to(shape)


def build(nc, x_in, pack_in, acc1_in, acc2_in, out, upto="all", dump=None):
    with ExitStack() as ctx:
        def resident(name, *shape):
            return ctx.enter_context(nc.sbuf_tensor(name, list(shape), F32))

        sems = {}
        phase = [""]

        def sem(name):
            if name not in sems:
                sems[name] = nc.alloc_semaphore(name=f"{phase[0]}{name}")
            return sems[name]

        def next_phase():
            nc.all_engine_barrier()
            nc.clear_and_free_semaphores(list(sems.values()))
            nc.all_engine_barrier()
            sems.clear()
            phase[0] += "n_"

        X = resident("X", P, NT, J, C)
        W = resident("W", P, NPACK)
        ident = W[:, COL["ident"][1]:COL["ident"][1] + 128]

        def w(name, c0=0, c1=None):
            r, at, c = COL[name]
            return W[0:r, at + c0:at + (c if c1 is None else c1)]

        wpair = resident("wpair", P, NB, 2, XBC)
        aneg = resident("aneg", P, NB, J, NH)
        dhalf = resident("dhalf", P, NB, J, NH)
        wout = resident("wout", P, NB, 2 * C)
        bn0s = resident("bn0s", P, 2, 4)
        bn0b = resident("bn0b", P, 2, 4)
        lwgo = resident("lwgo", 65, 128)
        lwi = resident("lwi", 65, 64)
        lvgo = resident("lvgo", 64, 128)
        lvi = resident("lvi", 64, 64)
        wr8 = resident("wr8", 64, E)
        bn3s = resident("bn3s", P, 1)
        bn3b = resident("bn3b", P, 1)
        wqs = resident("wqs", 64, 64)
        wvo = resident("wvo", 64, 64)
        epst = resident("epst", P, 4)
        tmp0 = resident("tmp0", P, 64)
        epss = resident("epss", P, J, 2)

        psA = ctx.enter_context(nc.psum_tensor("psA", [P, 2, 512], F32))
        psB = ctx.enter_context(nc.psum_tensor("psB", [P, 2, 512], F32))
        psC = ctx.enter_context(nc.psum_tensor("psC", [P, 2, 512], F32))
        psL = ctx.enter_context(nc.psum_tensor("psL", [P, 2, 512], F32))

        img = resident("img", P, B4, PADI, PADI)
        x6d = nc.dram_tensor("x6d", [B, IMG * IMG, C], F32)
        phase1 = ctx.enter_context(ExitStack())

        def sb(name, *shape):
            return phase1.enter_context(nc.sbuf_tensor(name, list(shape), F32))

        a_st = sb("a_st", P, J, 6); a_mv = sb("a_mv", P, J, 2); a_rs = sb("a_rs", P, J)
        a_xn = sb("a_xn", P, J, 2, C)
        hb = sb("hb", P, NB, 2, B, TT)
        hh = sb("hh", P, NB, B, 3)
        a_abs = sb("a_abs", P, J, NH); a_rx = sb("a_rx", P, J, NH); a_u = sb("a_u", P, J, NH)
        a_t = sb("a_t", P, 3, J, NH)
        a_dt = sb("a_dt", P, J, NH); a_a = sb("a_a", P, J, NH); a_dth = sb("a_dth", P, J, NH)
        a_T = sb("a_T", P, J, PROJ); a_S = sb("a_S", P, J, PROJ)
        a_bc = sb("a_bc", P, J, 2, B4, DS)
        a_xd = sb("a_xd", P, J, DI)
        a_R = sb("a_R", P, J * NH, TT); a_E = sb("a_E", P, J * NH, TT); a_ex = sb("a_ex", P, 3, J, NH)
        a_bct = sb("a_bct", 64, J, 2, P)
        a_xw = sb("a_xw", P, J, NH, HD); a_xe = sb("a_xe", P, J, NH, HD)
        a_G = sb("a_G", P, J, P)
        a_M = sb("a_M", P, J * NH, P)
        state = sb("state", 64, NB, J, DI); a_sd = sb("a_sd", 64, J, DI)
        a_y = sb("a_y", P, J, DI); a_sq = sb("a_sq", P, J, DI); a_ss = sb("a_ss", P, J); a_r2 = sb("a_r2", P, J)
        a_yT = sb("a_yT", P, J * P)

        def lnbuf(k):
            return dict(st=sb(f"{k}_st", P, J, 6), mv=sb(f"{k}_mv", P, J, 2), rs=sb(f"{k}_rs", P, J),
                        xn=sb(f"{k}_xn", P, J, C))

        f_ln = lnbuf("f"); f_xT = sb("f_xT", 64, B, TT); f_ft = sb("f_ft", 64, TT); f_fr = sb("f_fr", 64, B4, TT)
        f_w = sb("f_w", P, 5, E); f_s = sb("f_s", P, 4)
        f_h1 = sb("f_h1", P, 4, 256); f_h2 = sb("f_h2", P, 4, 256)
        f_big = sb("f_big", P, J, E, C); f_red = sb("f_red", P, J, C)
        c_ln = [lnbuf("c1"), lnbuf("c2")]
        c_mx = [sb(f"c_mx{k}", P, 2, J) for k in (0, 1)]
        c_e = [sb(f"c_e{k}", P, J, 2, C) for k in (0, 1)]
        c_eT = [sb(f"c_eT{k}", P, B + 1, TT) for k in (0, 1)]
        c_r = [sb(f"c_r{k}", 64, J, 16) for k in (0, 1)]
        c_q = [sb(f"c_q{k}", 64, B, TT) for k in (0, 1)]
        c_l = [sb(f"c_l{k}", P, J, C) for k in (0, 1)]
        accb = [sb(f"accb{k}", P, 16, C) for k in (0, 1)]
        def moe_bufs(m, make, nch):
            return dict(ln={n: make(f"{m}_{n}", *sh) for n, sh in (("st", (P, J, 6)), ("mv", (P, J, 2)), ("rs", (P, J)), ("xn", (P, J, C)))},
                        xT=make(f"{m}_xT", 64, J * P), g=make(f"{m}_g", P, J, 14), mx=make(f"{m}_mx", P, J), sm=make(f"{m}_sm", P, J),
                        d=make(f"{m}_d", P, J, E), top=make(f"{m}_top", P, J, 8), rep=make(f"{m}_rep", P, J, 8),
                        rest=make(f"{m}_rest", P, J, 14), cw=make(f"{m}_cw", P, J, E), h=make(f"{m}_h", P, nch, 256),
                        big=make(f"{m}_big", P, J, E, C), red=make(f"{m}_red", P, J, C))

        mix1 = moe_bufs("m0", sb, 8)
        r_ln = lnbuf("r"); r_xT = sb("r_xT", 65, B, TT)
        r_wk = sb("r_wk", 64, 96); r_c3 = sb("r_c3", 64, 2, 24); r_tc = sb("r_tc", 64, LB)
        r_h = sb("r_h", 64, TT + 1, LB); r_hT = sb("r_hT", 64, B, TT)
        p_ln = lnbuf("p")

        pow_m = epst[:, 0:2]
        EPS = {1e-5: 0, 1e-6: 1}

        block_ctx = nc.Block()
        block = block_ctx.__enter__()


        def settle(eng):
            eng.sem_inc(sem("apart"), 1)

        def ln_vector(dve, k, buf, src, i1, dup=False, out=None):
            settle(dve)
            for j in range(J):
                last = nc.vector.bn_stats(buf["st"][:, j, :], src[:, j, :])
            last.then_inc(sem(k + "_stats"), 1)
            dve.wait_ge(sem(k + "_stats"), i1)
            settle(dve)
            for j in range(J):
                last = nc.vector.bn_aggr(buf["mv"][:, j, :], buf["st"][:, j, :])
            last.then_inc(sem(k + "_var"), 1)
            yield
            dve.wait_ge(sem(k + "_rstd"), i1)
            for j in range(J):
                o = buf["xn"][:, j] if out is None else out[:, j]
                s = src[:, j, :]
                if dup:
                    s = bc(s, 1, 2)
                last = nc.vector.tensor_scalar(o, s, buf["mv"][:, j, 0:1], buf["rs"][:, j:j + 1], ALU.subtract, ALU.mult)
            last.then_inc(sem(k + "_xn"), 1)

        def ln_pool(pool, k, buf, eps, i1):
            pool.wait_ge(sem(k + "_var"), i1)
            nc.gpsimd.tensor_tensor(buf["rs"][:, :], buf["mv"][:, :, 1], epss[:, :, EPS[eps]], ALU.add).then_inc(sem(k + "_vare"), 1)
            pool.wait_ge(sem(k + "_vare"), i1)
            nc.gpsimd.tensor_tensor(buf["rs"][:, :], buf["rs"][:, :], pow_m, ALU.pow).then_inc(sem(k + "_rstd"), 1)

        a_ln = dict(st=a_st, mv=a_mv, rs=a_rs)
        EXC, EXS, EXT = 0, 1, 2

        def mamba_pe(pe, i):
            for k in range(NB):
                n = i * 2 + (k + 1)
                if k == 0:
                    pe.wait_ge(sem("a_xn"), i + 1)
                    pe.wait_ge(sem("x1_done"), i + 1)
                    for j in range(J):
                        last = nc.tensor.transpose(psA[:, 0, j * P:(j + 1) * P], a_xn[:, j].rearrange("p d c -> p (d c)"), ident)
                    last.then_inc(sem("a_feed"), 1)
                yield
                pe.wait_ge(sem("a_htop"), n)
                pe.wait_ge(sem("a_hbot"), n)
                pe.wait_ge(sem("a_halo"), n)
                pe.wait_ge(sem("a_hh"), n)
                for j in range(J):
                    hfl = hb[:, k].rearrange("p s b t -> p s (b t)")
                    nc.tensor.matmul(psA[:, j, 0:PROJ], w("ones"), w(f"bias{k}"), start=True, stop=False)
                    nc.tensor.matmul(psA[:, j, 0:ZD], hfl[0:64, 0, j * P:(j + 1) * P], w(f"wzd{k}"), start=False, stop=False)
                    nc.tensor.matmul(psA[:, j, ZD:PROJ], hfl[:, 0, j * P:(j + 1) * P], wpair[:, k, 0, :], start=False, stop=False)
                    last = nc.tensor.matmul(psA[:, j, ZD:PROJ], hfl[:, 1, j * P:(j + 1) * P], wpair[:, k, 1, :], start=False, stop=True)
                last.then_inc(sem("a_zx"), 1)
                yield
                pe.wait_ge(sem("a_R"), n)
                pe.wait_ge(sem("a_S"), n)
                nc.tensor.matmul(psA[:, 0, :], w("strictblk"), a_R[:].rearrange("p h t -> p (h t)"), start=True, stop=True)
                av = a_a[:].rearrange("p j h -> p (j h)")
                nc.tensor.matmul(psA[:, 1, 0:16], w("triblk"), av, start=True, stop=True)
                nc.tensor.matmul(psA[:, 1, 16:32], w("strictblk"), av, start=True, stop=True)
                nc.tensor.matmul(psA[:, 1, 32:48], w("indblk"), av, start=True, stop=True).then_inc(sem("a_seg"), 1)
                yield
                pe.wait_ge(sem("a_bc"), n)
                pe.wait_ge(sem("a_ex"), n)
                settle(pe)
                for j in range(J):
                    for q in range(2):
                        last = nc.tensor.transpose(psA[0:64, 1, (2 * j + q) * P:(2 * j + q + 1) * P],
                                                   a_bc[:, j, q].rearrange("p b n -> p (b n)"), ident)
                last.then_inc(sem("a_bct"), 1)
                yield
                pe.wait_ge(sem("a_bcts"), n)
                for j in range(J):
                    last = nc.tensor.matmul(psA[:, 0, j * P:(j + 1) * P], a_bct[:, j, 0], a_bct[:, j, 1], start=True, stop=True)
                last.then_inc(sem("a_G"), 1)
                for j in range(J):
                    nc.tensor.matmul(psA[:, 1, j * P:(j + 1) * P], a_bct[:, j, 1], state[:, k, j], start=True, stop=True)
                yield
                pe.wait_ge(sem("a_Gm"), n)
                for j in range(J):
                    last = nc.tensor.matmul(psA[0:64, 0, j * P:(j + 1) * P], a_bc[:, j, 0].rearrange("p b n -> p (b n)"),
                                            a_xe[:, j].rearrange("p h d -> p (h d)"), start=True, stop=True)
                last.then_inc(sem("a_st"), 1)
                yield
                pe.wait_ge(sem("a_Md"), n)
                pe.wait_ge(sem("a_Mp"), n)
                for j in range(J):
                    for h in range(NH):
                        last = nc.tensor.matmul(psA[:, 1, 256 + j * P + h * HD:256 + j * P + (h + 1) * HD],
                                                a_M[:, j * NH + h], a_xw[:, j, h], start=True, stop=True)
                last.then_inc(sem("a_Y"), 1)
                yield
                pe.wait_ge(sem("a_yn"), n)
                for j in range(J):
                    last = nc.tensor.transpose(psA[:, 0, j * P:(j + 1) * P], a_y[:, j], ident)
                last.then_inc(sem("a_yT"), 1)
                yield
                pe.wait_ge(sem("a_yTs"), n)
                if k == 0:
                    nc.tensor.matmul(psA[:, 1, 0:256], wout[:, k], a_yT[:], start=True, stop=True).then_inc(sem("a_feed"), 1)
                else:
                    for j in range(J):
                        last = nc.tensor.matmul(psA[:, 1, j * C:(j + 1) * C], a_yT[:, j * P:(j + 1) * P], wout[:, k, 0:C],
                                                start=True, stop=True)
                    last.then_inc(sem("a_mo"), 1)
                yield

        def mamba_act(act, i):
            for k in range(NB):
                n = i * 2 + (k + 1)
                act.wait_ge(sem("a_feed"), n)
                fd = psA[0:64, k, 0:256].rearrange("p (b t) -> p b t", b=B)
                nc.scalar.activation(hb[0:64, k, 0], fd, ACT.Copy)
                nc.scalar.activation(hb[0:64, k, 1, :, 2:TT], fd[:, :, 0:TT - 2], ACT.Copy).then_inc(sem("a_htop"), 1)
                yield
                act.wait_ge(sem("a_rx"), n)
                nc.scalar.activation(a_u[:], a_abs[:], ACT.Exp).then_inc(sem("a_u"), 1)
                nc.scalar.activation(a_T[:], psA[:, :, 0:PROJ], ACT.Tanh, scale=0.5).then_inc(sem("a_T"), 1)
                yield
                act.wait_ge(sem("a_seg"), n)
                nc.scalar.activation(a_E[:].rearrange("p h t -> p (h t)"), psA[:, 0, :], ACT.Exp)
                nc.scalar.activation(a_ex[:].rearrange("p s j h -> p (s j h)"), psA[:, 1, 0:48], ACT.Exp).then_inc(sem("a_ex"), 1)
                yield
                act.wait_ge(sem("a_bct"), n)
                nc.scalar.activation(a_bct[:].rearrange("p j q t -> p (j q t)"), psA[0:64, 1, :], ACT.Copy).then_inc(sem("a_bcts"), 1)
                yield
                act.wait_ge(sem("a_y"), n)
                for j in range(J):
                    last = nc.scalar.activation(a_sq[:, j], a_y[:, j], ACT.Square, accum_out=a_ss[:, j:j + 1])
                last.then_inc(sem("a_ss"), 1)
                yield
                act.wait_ge(sem("a_yT"), n)
                nc.scalar.activation(a_yT[:], psA[:, 0, 0:256], ACT.Copy).then_inc(sem("a_yTs"), 1)
                yield

        def mamba_dve(dve, i):
            xi = X[:, i]
            dve.wait_ge(sem("x1_done"), i + 1)
            yield from ln_vector(dve, "a", a_ln, xi, i + 1, dup=True, out=a_xn)
            yield
            for k in range(NB):
                n = i * 2 + (k + 1)
                st = Steps(dve, sem("a_steps"), i * 2 + k, DVE_A)
                v = nc.vector
                dve.wait_ge(sem("a_feed"), n)
                dve.wait_ge(sem("a_halo"), n)
                fd = psA[:, k, 0:256].rearrange("p (b t) -> p b t", b=B)
                v.tensor_copy(hb[64:128, k, 0, :, 1:TT], fd[64:128, :, 0:TT - 1])
                v.tensor_copy(hb[64:128, k, 1, :, 3:TT], fd[64:128, :, 0:TT - 3]).then_inc(sem("a_hbot"), 1)
                dve.wait_ge(sem("a_htop"), n)
                v.tensor_copy(hh[:, k], fd[:, :, TT - 3:TT]).then_inc(sem("a_hh"), 1)
                yield
                dve.wait_ge(sem("a_zx"), n)
                raw = psA[:, :, DI:ZD]
                st.did(v.tensor_scalar(a_rx[:], raw, 0.0, None, ALU.max)); st.wait()
                v.scalar_tensor_tensor(a_abs[:], a_rx[:], -2.0, raw, ALU.mult, ALU.add).then_inc(sem("a_rx"), 1)
                dve.wait_ge(sem("a_hh"), n)
                v.tensor_copy(hb[64:128, k, 0, :, 0:1], hh[64:128, k, :, 2:3])
                v.tensor_copy(hb[0:64, k, 1, :, 0:2], hh[0:64, k, :, 1:3])
                v.tensor_copy(hb[64:128, k, 1, :, 0:3], hh[64:128, k, :, 0:3]).then_inc(sem("a_halo"), 1)
                yield
                dve.wait_ge(sem("a_u"), n)
                s_, s2, pq = a_t[:, 0], a_t[:, 1], a_t[:, 2]
                st.did(v.tensor_scalar(s2, a_u[:], 2.0, None, ALU.add)); st.wait()
                st.did(v.reciprocal(pq, s2)); st.wait()
                st.did(v.tensor_tensor(s_, a_u[:], pq, ALU.mult)); st.wait()
                st.did(v.tensor_tensor(s2, s_, s_, ALU.mult)); st.wait()
                st.did(v.tensor_scalar(pq, s2, 1.0 / 13, None, ALU.mult)); st.wait()
                for d in (11, 9, 7, 5, 3):
                    st.did(v.scalar_tensor_tensor(pq, pq, 1.0 / d, s2, ALU.add, ALU.mult)); st.wait()
                st.did(v.scalar_tensor_tensor(pq, pq, 1.0, s_, ALU.add, ALU.mult)); st.wait()
                st.did(v.scalar_tensor_tensor(a_dt[:], pq, 2.0, a_rx[:], ALU.mult, ALU.add)); st.wait()
                st.did(v.tensor_tensor(a_a[:], a_dt[:], aneg[:, k], ALU.mult))
                st.did(v.tensor_scalar(a_dth[:], a_dt[:], 0.5, None, ALU.mult)); st.wait()
                v.tensor_tensor(a_R[:], bc(w("tri32"), 1, J * NH), bc(a_a[:].rearrange("p j h -> p (j h)"), 2, TT), ALU.mult)\
                    .then_inc(sem("a_R"), 1)
                yield
                dve.wait_ge(sem("a_T"), n)
                v.scalar_tensor_tensor(a_S[:], a_T[:], 1.0, psA[:, :, 0:PROJ], ALU.add, ALU.mult).then_inc(sem("a_S"), 1)
                yield
                dve.wait_ge(sem("a_S"), n)
                xs = a_S[:, :, ZD:ZD + DI].rearrange("p j (h d) -> p j h d", h=NH)
                st.did(v.tensor_tensor(a_xw[:], xs, bc(a_dth[:], 3, HD), ALU.mult)); st.wait()
                dve.wait_ge(sem("a_ex"), n)
                v.tensor_tensor(a_xe[:], a_xw[:], bc(a_ex[:, EXS], 3, HD), ALU.mult)
                yield
                dve.wait_ge(sem("a_G"), n)
                v.tensor_tensor(a_G[:], psA[:, 0, 0:256].rearrange("p (j t) -> p j t", j=J), bc(w("triblk"), 1, J), ALU.mult)\
                    .then_inc(sem("a_Gm"), 1)
                dve.wait_ge(sem("a_Gm"), n)
                for b in range(B4 - 1):
                    last = m_product(v, b)
                last.then_inc(sem("a_Md"), 1)
                yield
                dve.wait_ge(sem("a_st"), n)
                dve.wait_ge(sem("a_sd"), n)
                v.tensor_tensor(state[:, k], a_sd[:], psA[0:64, 0, 0:256].rearrange("p (j d) -> p j d", j=J), ALU.add)
                yield
                dve.wait_ge(sem("a_Y"), n)
                yv = a_y[:].rearrange("p j (h d) -> p j h d", h=NH)
                st.did(v.tensor_tensor(yv, psA[:, 1, 0:256].rearrange("p (j h d) -> p j h d", j=J, h=NH), bc(a_ex[:, EXC], 3, HD), ALU.mult))
                st.wait()
                dve.wait_ge(sem("a_xd"), n)
                yf = a_y[:].rearrange("p j d -> p (j d)")
                st.did(v.tensor_tensor(yf, yf, a_xd[:].rearrange("p j d -> p (j d)"), ALU.add)); st.wait()
                st.did(v.tensor_tensor(yf, yf, psA[:, 1, 256:512], ALU.add)); st.wait()
                v.tensor_tensor(a_y[:], a_y[:], a_S[:, :, 0:DI], ALU.mult).then_inc(sem("a_y"), 1)
                yield
                dve.wait_ge(sem("a_r2"), n)
                for j in range(J):
                    last = v.tensor_scalar(a_y[:, j], a_y[:, j], a_r2[:, j:j + 1], None, ALU.mult)
                last.then_inc(sem("a_yn"), 1)
                st.end()
                yield
            dve.wait_ge(sem("a_mo"), i + 1)
            nc.vector.tensor_tensor(X[:, i], X[:, i], psA[:, 1, 0:P].rearrange("p (j c) -> p j c", j=J), ALU.add)\
                .then_inc(sem("x1_done"), 1)

        def m_product(eng, b):
            r = slice(32 * b, 32 * b + 32)
            return eng.tensor_tensor(a_M[r, :, r].rearrange("p (j h) t -> p j h t", j=J),
                                     a_E[r].rearrange("p (j h) t -> p j h t", j=J), bc(a_G[r, :, r], 2, NH), ALU.mult)

        def mamba_pool(pool, i):
            ln_pool(pool, "a", a_ln, 1e-6, i + 1)
            yield
            for k in range(NB):
                n = i * 2 + (k + 1)
                g = nc.gpsimd
                pool.wait_ge(sem("a_S"), n)
                for j in range(J):
                    last = g.tensor_tensor(a_bc[:, j], bc(bc(w("maskb"), 1, 2), 3, DS),
                                           bc(a_S[:, j, ZD + DI:PROJ].rearrange("p (q n) -> p q n", q=2), 2, B4), ALU.mult)
                last.then_inc(sem("a_bc"), 1)
                g.tensor_tensor(a_xd[:].rearrange("p j (h d) -> p j h d", h=NH),
                                a_S[:, :, ZD:ZD + DI].rearrange("p j (h d) -> p j h d", h=NH), bc(dhalf[:, k], 3, HD), ALU.mult)\
                    .then_inc(sem("a_xd"), 1)
                yield
                pool.wait_ge(sem("a_ex"), n)
                g.tensor_tensor(a_sd[:].rearrange("p j (h d) -> p j h d", h=NH), state[:, k].rearrange("p j (h d) -> p j h d", h=NH),
                                bc(a_ex[0:64, EXT], 3, HD), ALU.mult).then_inc(sem("a_sd"), 1)
                yield
                pool.wait_ge(sem("a_sd"), n)
                pool.wait_ge(sem("a_Gm"), n)
                m_product(g, B4 - 1).then_inc(sem("a_Mp"), 1)
                yield
                pool.wait_ge(sem("a_ss"), n)
                settle(pool)
                g.tensor_scalar(a_r2[:], a_ss[:], 1.0 / DI, 4e-5, ALU.mult, ALU.add).then_inc(sem("a_r2e"), 1)
                pool.wait_ge(sem("a_r2e"), n)
                g.tensor_tensor(a_r2[:], a_r2[:], pow_m, ALU.pow).then_inc(sem("a_r2"), 1)
                yield

        def ffn0_pe(pe, i):
            i1 = i + 1
            pe.wait_ge(sem("f_xn"), i1)
            pe.wait_ge(sem("x3_done"), i1)
            settle(pe)
            for j in range(J):
                last = nc.tensor.transpose(psB[0:64, 0, j * P:(j + 1) * P], f_ln["xn"][:, j], ident)
            last.then_inc(sem("f_xT"), 1)
            yield
            pe.wait_ge(sem("f_xTs"), i1)
            for q in range(4):
                nc.tensor.matmul(psB[:, q // 2, (q % 2) * 256:(q % 2 + 1) * 256], w("f0w1", q * P, (q + 1) * P),
                                 f_xT[:].rearrange("p b t -> p (b t)"), start=True, stop=True).then_inc(sem("f_mm1"), 1)
            yield
            for q in range(4):
                pe.wait_ge(sem("f_h1"), i1)
                nc.tensor.matmul(psB[:, q // 2, (q % 2) * 256:(q % 2 + 1) * 256], w("f0w2", q * P, (q + 1) * P), f_h1[:, q],
                                 start=True, stop=True).then_inc(sem("f_mm2"), 1)
            yield
            pe.wait_ge(sem("f_feat"), i1)
            pe.wait_ge(sem("f_h2"), i1)
            nc.tensor.matmul(psB[:, 0, 0:E], w("ones"), w("br"), start=True, stop=False)
            nc.tensor.matmul(psB[:, 0, 0:E], f_fr[:].rearrange("p b t -> p (b t)"), wr8[:], start=False, stop=True).then_inc(sem("f_lg"), 1)
            yield
            pe.wait_ge(sem("f_w"), i1)
            for j in range(J):
                nc.tensor.matmul(psB[:, j, :], w("ones"), w("f0bo"), start=True, stop=False)
                for q in range(4):
                    last = nc.tensor.matmul(psB[:, j, q * P:(q + 1) * P], f_h2[:, q, j * P:(j + 1) * P], w("f0wo", q * P, (q + 1) * P),
                                            start=False, stop=(q == 3))
            last.then_inc(sem("f_y"), 1)
            yield

        def ffn0_act(act, i):
            i1 = i + 1
            act.wait_ge(sem("f_xT"), i1)
            nc.scalar.activation(f_xT[:].rearrange("p b t -> p (b t)"), psB[0:64, 0, 0:256], ACT.Copy).then_inc(sem("f_xTs"), 1)
            yield
            act.wait_ge(sem("f_mm1"), i * 4 + 4)
            for q in range(4):
                last = nc.scalar.activation(f_h1[:, q], psB[:, q // 2, (q % 2) * 256:(q % 2 + 1) * 256], ACT.Relu,
                                            bias=bn0b[:, 0, q:q + 1], scale=bn0s[:, 0, q:q + 1])
            last.then_inc(sem("f_h1"), 1)
            yield
            act.wait_ge(sem("f_mm2"), i * 4 + 4)
            for q in range(4):
                last = nc.scalar.activation(f_h2[:, q], psB[:, q // 2, (q % 2) * 256:(q % 2 + 1) * 256], ACT.Relu,
                                            bias=bn0b[:, 1, q:q + 1], scale=bn0s[:, 1, q:q + 1])
            last.then_inc(sem("f_h2"), 1)
            yield
            act.wait_ge(sem("f_ld"), i1)
            nc.scalar.activation(f_w[:, 1], f_w[:, 0], ACT.Exp, accum_out=f_s[:, 1:2]).then_inc(sem("f_le"), 1)
            yield

        def ffn0_dve(dve, i):
            i1 = i + 1
            v = nc.vector
            dve.wait_ge(sem("x1_done"), i + 2)
            yield from ln_vector(dve, "f", f_ln, X[:, i], i1)
            yield
            dve.wait_ge(sem("f_xTs"), i1)
            st = Steps(dve, sem("f_steps"), i, 5)
            st.did(v.tensor_reduce(f_ft[:], f_xT[:].rearrange("p b t -> p t b"), AX, ALU.add)); st.wait()
            v.tensor_copy(f_fr[:], bc(f_ft[:], 1, B4)).then_inc(sem("f_feat"), 1)
            yield
            dve.wait_ge(sem("f_lg"), i1)
            st.did(v.tensor_reduce(f_s[:, 0:1], psB[:, 0, 0:E], AX, ALU.max)); st.wait()
            v.tensor_scalar(f_w[:, 0], psB[:, 0, 0:E], f_s[:, 0:1], None, ALU.subtract).then_inc(sem("f_ld"), 1)
            dve.wait_ge(sem("f_le"), i1)
            st.did(v.reciprocal(f_s[:, 2:3], f_s[:, 1:2])); st.wait()
            v.tensor_scalar(f_w[:, 2], f_w[:, 1], f_s[:, 2:3], None, ALU.mult).then_inc(sem("f_w"), 1)
            yield
            dve.wait_ge(sem("f_y"), i1)
            st.did(v.tensor_tensor(f_big[:], psB[:].rearrange("p j (e c) -> p j e c", e=E), bc(bc(f_w[:, 2], 1, J), 3, C), ALU.mult)); st.wait()
            yield
            st.did(v.tensor_reduce(f_red[:], f_big[:].rearrange("p j e c -> p j c e"), AX, ALU.add)); st.wait()
            st.end()
            v.tensor_tensor(X[:, i], X[:, i], f_red[:], ALU.add).then_inc(sem("x2_done"), 1)

        def prod_pe(pe, i, k, ps):
            i1, c = i + 1, f"c{k}"
            pe.wait_ge(sem(c + "_e"), i1)
            if k == 1:
                pe.wait_ge(sem("x4_done"), i + 2)
            else:
                pe.wait_ge(sem("x2_done"), i1)
            for j in range(J):
                last = nc.tensor.transpose(ps[:, 0, j * P:(j + 1) * P], c_e[k][:, j].rearrange("p d c -> p (d c)"), ident)
            last.then_inc(sem(c + "_et"), 1)
            yield
            pe.wait_ge(sem(c + "_ets"), i1)
            pe.wait_ge(sem(c + "_acc"), i * 16 + 16)
            settle(pe)
            for h in range(2):
                r = slice(64 * h, 64 * h + 64)
                for t in range(16):
                    last = nc.tensor.matmul(ps[0:64, h, 0:144].rearrange("p (b t) -> p b t", t=16)[:, :, t],
                                            accb[k][r, t], c_eT[k][r, :, h * 16 + t], start=True, stop=True)
                if h == 0:
                    yield
            last.then_inc(sem(c + "_mm"), 1)
            yield
            pe.wait_ge(sem(c + "_q"), i1)
            settle(pe)
            for j in range(J):
                last = nc.tensor.transpose(ps[:, 0, j * C:(j + 1) * C],
                                           c_q[k][:, j * B4:(j + 1) * B4].rearrange("p b t -> p (b t)"), ident[0:64, 0:64])
            last.then_inc(sem(c + "_qT"), 1)
            yield

        def prod_act(act, i, k, ps):
            i1, c = i + 1, f"c{k}"
            act.wait_ge(sem(c + "_mx"), i1)
            for j in range(J):
                last = nc.scalar.activation(c_e[k][:, j], bc(c_ln[k]["xn"][:, j], 1, 2), ACT.Exp, bias=c_mx[k][:, 1, j:j + 1])
            last.then_inc(sem(c + "_e"), 1)
            yield
            act.wait_ge(sem(c + "_et"), i1)
            nc.scalar.activation(c_eT[k][:, 0:B, :].rearrange("p b t -> p (b t)"), ps[:, 0, 0:256], ACT.Copy).then_inc(sem(c + "_ets"), 1)
            yield
            act.wait_ge(sem(c + "_qT"), i1)
            nc.scalar.activation(c_l[k][:].rearrange("p j c -> p (j c)"), ps[:, 0, 0:P], ACT.Ln).then_inc(sem(c + "_l"), 1)
            yield

        def prod_dve(dve, i, k, ps, before, done):
            i1, c = i + 1, f"c{k}"
            v = nc.vector
            dve.wait_ge(sem(before), i + (1 + k))
            yield from ln_vector(dve, c, c_ln[k], X[:, i], i1)
            dve.wait_ge(sem(c + "_xn"), i1)
            st = Steps(dve, sem(c + "_steps"), i, 2)
            st.did(v.tensor_reduce(c_mx[k][:, 0], c_ln[k]["xn"][:], AX, ALU.max)); st.wait()
            v.tensor_scalar(c_mx[k][:, 1], c_mx[k][:, 0], -1.0, None, ALU.mult).then_inc(sem(c + "_mx"), 1)
            yield
            dve.wait_ge(sem(c + "_mm"), i1)
            pv = ps[0:64, :, 0:144].rearrange("p h (b t) -> p h b t", b=B + 1)
            st.did(v.reciprocal(c_r[k][:], pv[:, :, B])); st.wait()
            st.end()
            v.tensor_tensor(c_q[k][:].rearrange("p b (h t) -> p h b t", h=2), pv[:, :, 0:B], bc(c_r[k][:], 2, B), ALU.mult)\
                .then_inc(sem(c + "_q"), 1)
            yield
            dve.wait_ge(sem(c + "_l"), i1)
            for j in range(J):
                last = v.scalar_tensor_tensor(X[:, i, j], c_l[k][:, j], c_mx[k][:, 0, j:j + 1], X[:, i, j], ALU.add, ALU.add)
            last.then_inc(sem(done), 1)

        def x6_store(sp, i):
            sp.wait_ge(sem("x6_done"), i + 1)
            for j in range(J):
                sp.dma_start(x6d[j * B4:(j + 1) * B4, bass.ts(i, TT), :], X[:, i, j]).then_inc(sem("x6_out"), 16)

        def acc_load(sp, i, k, src):
            sp.dma_start(accb[k][:], src[i]).then_inc(sem(f"c{k}_acc"), 16)

        def moe_pe(pe, i, m, u, ps, nch, names, before):
            i1 = i + 1
            gate, gateb, w1, w2, b2 = names
            hw = 512 // nch
            pe.wait_ge(sem(m + "_xn"), i1)
            pe.wait_ge(*before)
            settle(pe)
            for j in range(J):
                last = nc.tensor.transpose(ps[0:64, 0, j * P:(j + 1) * P], u["ln"]["xn"][:, j], ident)
            last.then_inc(sem(m + "_xT"), 1)
            yield
            pe.wait_ge(sem(m + "_xTs"), i1)
            for j in range(J):
                nc.tensor.matmul(ps[:, 1, j * E:(j + 1) * E], w("ones"), w(gateb), start=True, stop=False)
                last = nc.tensor.matmul(ps[:, 1, j * E:(j + 1) * E], u["xT"][:, j * P:(j + 1) * P], w(gate), start=False, stop=True)
            last.then_inc(sem(m + "_lg"), 1)
            yield
            pe.wait_ge(sem(m + "_ld"), i1)
            for r in range(nch // 4):
                if r:
                    pe.wait_ge(sem(m + "_h"), i * (nch // 4) + r)
                for q in range(4):
                    e = r * 4 + q
                    last = nc.tensor.matmul(ps[:, q // 2, (q % 2) * 256:(q % 2 + 1) * 256], w(w1, e * P, (e + 1) * P), u["xT"][:],
                                            start=True, stop=True)
                last.then_inc(sem(m + "_mm1"), 1)
                yield
            pe.wait_ge(sem(m + "_h"), (i + 1) * (nch // 4))
            for j in range(J):
                nc.tensor.matmul(ps[:, j, :], w("ones"), w(b2), start=True, stop=False)
                for e in range(nch):
                    last = nc.tensor.matmul(ps[:, j, e * hw:(e + 1) * hw], u["h"][:, e, j * P:(j + 1) * P], w(w2, e * hw, (e + 1) * hw),
                                            start=False, stop=(e == nch - 1))
                if j == 0:
                    yield
            last.then_inc(sem(m + "_y"), 1)
            yield

        def moe_act(act, i, m, u, ps, nch, b1):
            i1 = i + 1
            act.wait_ge(sem(m + "_xT"), i1)
            nc.scalar.activation(u["xT"][:], ps[0:64, 0, 0:256], ACT.Copy).then_inc(sem(m + "_xTs"), 1)
            yield
            act.wait_ge(sem(m + "_ld"), i1)
            nc.scalar.activation(u["g"][:, :, 0:E], u["d"][:], ACT.Exp).then_inc(sem(m + "_p"), 1)
            yield
            for r in range(nch // 4):
                act.wait_ge(sem(m + "_mm1"), i * (nch // 4) + (r + 1))
                for q in range(4):
                    e = r * 4 + q
                    last = nc.scalar.activation(u["h"][:, e], ps[:, q // 2, (q % 2) * 256:(q % 2 + 1) * 256], ACT.Gelu, bias=w(b1, e, e + 1))
                last.then_inc(sem(m + "_h"), 1)
                yield

        def moe_dve(dve, i, m, u, ps, x, before, done, renorm):
            i1 = i + 1
            v = nc.vector
            if before:
                dve.wait_ge(*before)
            yield from ln_vector(dve, m, u["ln"], x, i1)
            yield
            dve.wait_ge(sem(m + "_lg"), i1)
            st = Steps(dve, sem(m + "_steps"), i, 15 if renorm else 10)
            lg = ps[:, 1, 0:J * E].rearrange("p (j e) -> p j e", j=J)
            st.did(v.tensor_reduce(u["mx"][:], lg, AX, ALU.max)); st.wait()
            v.tensor_tensor(u["d"][:], lg, bc(u["mx"][:], 2, E), ALU.subtract).then_inc(sem(m + "_ld"), 1)
            yield
            dve.wait_ge(sem(m + "_p"), i1)
            p_ = u["g"][:, :, 0:E]
            st.did(v.tensor_reduce(u["sm"][:], p_, AX, ALU.add)); st.wait()
            st.did(v.reciprocal(u["sm"][:], u["sm"][:])); st.wait()
            st.did(v.tensor_tensor(p_, p_, bc(u["sm"][:], 2, E), ALU.mult)); st.wait()
            settle(dve)
            for j in range(J):
                last = v.max(u["top"][:, j], u["g"][:, j])
            st.did(last); st.wait()
            st.did(v.tensor_copy(u["rep"][:, :, 0:2], u["top"][:, :, 0:2])); st.wait()
            settle(dve)
            for j in range(J):
                last = v.match_replace(u["rest"][:, j], u["rep"][:, j], u["g"][:, j], 0.0)
            st.did(last); st.wait()
            st.did(v.tensor_tensor(u["cw"][:], p_, u["rest"][:, :, 0:E], ALU.subtract)); st.wait()
            if renorm:
                st.did(v.tensor_reduce(u["sm"][:], u["cw"][:], AX, ALU.add)); st.wait()
                st.did(v.tensor_scalar(u["sm"][:], u["sm"][:], 1e-12, None, ALU.max)); st.wait()
                st.did(v.reciprocal(u["mx"][:], u["sm"][:])); st.wait()
                st.did(v.tensor_tensor(u["cw"][:], u["cw"][:], bc(u["mx"][:], 2, E), ALU.mult)); st.wait()
            yield
            dve.wait_ge(sem(m + "_y"), i1)
            st.did(v.tensor_tensor(u["big"][:], ps[:].rearrange("p j (e c) -> p j e c", e=E), bc(u["cw"][:], 3, C), ALU.mult)); st.wait()
            yield
            st.did(v.tensor_reduce(u["red"][:], u["big"][:].rearrange("p j e c -> p j c e"), AX, ALU.add)); st.wait()
            if renorm:
                st.did(v.tensor_tensor(u["red"][:], u["red"][:], u["ln"]["xn"][:], ALU.add)); st.wait()
            st.end()
            v.tensor_tensor(x, x, u["red"][:], ALU.add).then_inc(sem(done), 1)

        def xproj_pe(pe, i):
            i1 = i + 1
            pe.wait_ge(sem("r_xn"), i1)
            pe.wait_ge(sem("x5_done"), i + 2)
            settle(pe)
            for j in range(J):
                last = nc.tensor.transpose(psC[0:64, 0, j * P:(j + 1) * P], r_ln["xn"][:, j], ident)
            last.then_inc(sem("r_xT"), 1)
            yield
            pe.wait_ge(sem("r_xTs"), i1)
            ps = psL[:, 0, :].rearrange("p (t q b) -> p t q b", q=2, b=LB)
            xv = r_xT[:].rearrange("p b t -> p t b")
            nc.tensor.matmul(ps[:, :, 0], lwgo[:], xv, start=True, stop=False, skip_group_check=True)
            nc.tensor.matmul(ps[0:64, :, 1], lwi[:], xv, start=False, stop=False, skip_group_check=True).then_inc(sem("r_xp"), 1)
            yield

        def xproj_act(act, i):
            act.wait_ge(sem("r_xT"), i + 1)
            nc.scalar.activation(r_xT[0:64].rearrange("p b t -> p (b t)"), psC[0:64, 0, 0:256], ACT.Copy).then_inc(sem("r_xTs"), 1)
            yield

        def xproj_dve(dve, i):
            dve.wait_ge(sem("x5_done"), i + 2)
            yield from ln_vector(dve, "r", r_ln, X[:, i], i + 1)
            yield

        TO = r_wk[:, 58:82:3]

        def lstm_pe(pe, i):
            pe.wait_ge(sem("r_xp"), i + 1)
            for t in range(TT):
                pe.wait_ge(sem("r_hr"), i * TT + (t + 1))
                h = r_h[:, t if t else TT]
                c = t * 2 * LB
                nc.tensor.matmul(psL[:, 0, c:c + LB], lvgo[:], h, start=False, stop=False, skip_group_check=True)
                nc.tensor.matmul(psL[0:64, 0, c + LB:c + 2 * LB], lvi[:], h, start=False, stop=False, skip_group_check=True)\
                    .then_inc(sem("r_z"), 1)
                yield

        def lstm_act(act, i):
            for t in range(TT):
                n = i * TT + (t + 1)
                c = t * 2 * LB
                act.wait_ge(sem("r_z"), n)
                o = r_wk[:, 2:2 + 84].rearrange("p (g x) -> p g x", x=28)[:, 0:2, 0:24:3]
                nc.scalar.activation(o, psL[0:64, 0, c:c + 2 * LB].rearrange("p (g b) -> p g b", b=LB), ACT.Tanh).then_inc(sem("r_gi"), 1)
                nc.scalar.activation(TO, psL[64:128, 0, c:c + LB], ACT.Tanh)
                act.wait_ge(sem("r_c"), n)
                nc.scalar.activation(r_tc[:], r_c3[:, t % 2, 2::3], ACT.Tanh, scale=0.5).then_inc(sem("r_tc"), 1)
                yield

        def lstm_dve(dve, i):
            v = nc.vector
            for t in range(TT):
                n = i * TT + (t + 1)
                hp = r_h[:, t if t else TT]
                dve.wait_ge(sem("r_hr"), n)
                v.scalar_tensor_tensor(r_wk[:, 32:56:3], hp, 0.5, r_c3[:, (t - 1) % 2, 2::3], ALU.mult, ALU.mult).then_inc(sem("r_hc"), 1)
                dve.wait_ge(sem("r_hc"), n)
                dve.wait_ge(sem("r_gi"), n)
                v.tensor_tensor_scan(r_c3[:, t % 2, :], r_wk[:, 0:24], r_wk[:, 30:54], 0.0, ALU.mult, ALU.add).then_inc(sem("r_c"), 1)
                dve.wait_ge(sem("r_tc"), n)
                v.scalar_tensor_tensor(r_h[:, t + 1], TO, 1.0, r_tc[:], ALU.add, ALU.mult).then_inc(sem("r_hr"), 1)
                yield

        def post_pe(pe, i):
            i1 = i + 1
            pe.wait_ge(sem("r_hT"), i1)
            settle(pe)
            for j in range(J):
                last = nc.tensor.transpose(psB[:, 0, j * C:(j + 1) * C], r_hT[:, j * B4:(j + 1) * B4].rearrange("p b t -> p (b t)"),
                                           ident[0:64, 0:64])
            last.then_inc(sem("p_hT"), 1)
            yield
            pe.wait_ge(sem("p_xn"), i1)
            nc.tensor.transpose(psB[:, 1, 0:P], p_ln["xn"][:].rearrange("p j c -> p (j c)"), ident).then_inc(sem("p_xT"), 1)
            yield

        def post_dve(dve, i):
            dve.wait_ge(sem("p_hT"), i + 1)
            for j in range(J):
                last = nc.vector.scalar_tensor_tensor(X[:, i, j], psB[:, 0, j * C:(j + 1) * C], 0.5, X[:, i, j], ALU.mult, ALU.add)
            last.then_inc(sem("x6_done"), 1)
            dve.wait_ge(sem("x6_done"), i + 1)
            yield from ln_vector(dve, "p", p_ln, X[:, i], i + 1)
            yield

        def post_pool(pool, i):
            pool.wait_ge(sem("r_hr"), (i + 1) * TT + 1)
            settle(pool)
            nc.gpsimd.tensor_copy(r_hT[:].rearrange("p b t -> p t b"), r_h[:, 1:TT + 1]).then_inc(sem("r_hT"), 1)

        def post_act(act, i):
            act.wait_ge(sem("p_xT"), i + 1)
            nc.scalar.activation(img[:, :, i + 3, 3:3 + IMG], psB[:, 1, 0:P].rearrange("p (b t) -> p b t", b=B4), ACT.Copy)\
                .then_inc(sem("x6_free"), 1)
            yield

        def run(*gens):
            for g in gens:
                for _ in g:
                    pass

        NP_ = NT
        stages = dict(mamba=1, ffn0=2, prod0=3, moe1=4, prod1=5, lstm=6, all=9)[upto]
        CREDIT = ["x1_done", "x3_done", "x4_done", "x5_done", "x6_free", "r_hr"]
        M1 = ("m1gate", "m1gateb", "m1w1", "m1w2", "m1b2")
        M2 = ("m2gate", "m2gateb", "m2w1", "m2w2", "m2b2")

        @block.sync
        def _(sp):
            sp.dma_start(W[:], pack_in).then_inc(sem("w_in"), 16)
            sp.dma_start(X[:], x_in).then_inc(sem("x_in"), 16)
            sp.wait_ge(sem("setup"), 1)
            if stages >= 3:
                acc_load(sp, 0, 0, acc1_in)
                acc_load(sp, 0, 1, acc2_in)
                with sp.Fori(1, NT) as i:
                    sp.wait_ge(sem("c0_mm"), i)
                    acc_load(sp, i, 0, acc1_in)
                    if stages >= 5:
                        sp.wait_ge(sem("c1_mm"), i)
                        acc_load(sp, i, 1, acc2_in)
                    if stages >= 9:
                        x6_store(sp, i - 1)
                if stages >= 9:
                    x6_store(sp, NT - 1)
                    sp.wait_ge(sem("x6_out"), NT * 32)
            if stages < 9:
                sp.wait_ge(sem({1: "x1_done", 2: "x2_done", 3: "x3_done", 4: "x4_done", 5: "x5_done", 6: "x6_done"}[stages]),
                           NT + (0 if stages in (2, 6) else 1))
                sp.dma_start(dump, X[:]).then_inc(sem("out"), 16)
                sp.wait_ge(sem("out"), 16)

        @block.gpsimd
        def _(pool):
            g = nc.gpsimd
            pool.wait_ge(sem("zeroed"), 2)
            pool.wait_ge(sem("w_in"), 16)
            for l in (1, 2):
                g.tensor_scalar(bn0s[:, l - 1], w(f"f0v{l}"), 1.0, 1e-3, ALU.mult, ALU.add)
            g.tensor_scalar(bn3s[:], w("bnv"), 1.0, 1e-5, ALU.mult, ALU.add).then_inc(sem("pool_bn"), 1)
            pool.wait_ge(sem("pool_bn"), 1)
            for l in (1, 2):
                g.tensor_tensor(bn0s[:, l - 1], bn0s[:, l - 1], epst[:, 0:4], ALU.pow)
            g.tensor_tensor(bn3s[:], bn3s[:], epst[:, 0:1], ALU.pow).then_inc(sem("pool_bn"), 1)
            with pool.Fori(0, NT) as i:
                run(mamba_pool(pool, i))
                if stages >= 2: ln_pool(pool, "f", f_ln, 1e-5, i + 1)
                if stages >= 3: ln_pool(pool, "c0", c_ln[0], 1e-6, i + 1)
                if stages >= 4: ln_pool(pool, "m0", mix1["ln"], 1e-5, i + 1)
                if stages >= 5: ln_pool(pool, "c1", c_ln[1], 1e-6, i + 1)
                if stages >= 6:
                    ln_pool(pool, "r", r_ln, 1e-5, i + 1)
                    post_pool(pool, i)
                    ln_pool(pool, "p", p_ln, 1e-6, i + 1)

        @block.scalar
        def _(act):
            act.wait_ge(sem("w_in"), 16)
            for k in range(NB):
                for j in range(J):
                    nc.scalar.activation(aneg[:, k, j], w(f"alog{k}"), ACT.Exp)
            nc.scalar.activation(tmp0[:, 0:1], w("normw0"), ACT.Copy).then_inc(sem("act_setup"), 1)
            act.wait_ge(sem("setup"), 1)
            with act.Fori(0, NT) as i:
                run(mamba_act(act, i))
                if stages >= 2: run(ffn0_act(act, i))
                if stages >= 3: run(prod_act(act, i, 0, psB))
                if stages >= 4: run(moe_act(act, i, "m0", mix1, psC, 8, "m1b1"))
                if stages >= 5: run(prod_act(act, i, 1, psC))
                if stages >= 6: run(xproj_act(act, i), lstm_act(act, i), post_act(act, i))

        @block.vector
        def _(dve):
            v = nc.vector
            v.memset(epst[:], -0.5)
            v.memset(epss[:, :, 0], 1e-5)
            v.memset(epss[:, :, 1], 1e-6)
            v.memset(hb[:], 0.0)
            v.memset(hh[:], 0.0)
            v.memset(a_M[:], 0.0)
            v.memset(state[:], 0.0)
            for k in (0, 1):
                v.memset(c_eT[k][:, B, :], 1.0)
            v.memset(r_xT[64:65], 1.0)
            v.memset(mix1["g"][:], NEG)
            v.memset(mix1["rep"][:], NEG)
            v.memset(r_c3[:], 0.0)
            v.memset(r_h[:], 0.0)
            v.memset(img[:], 0.0)
            v.memset(r_wk[:], 0.0).then_inc(sem("zeroed"), 1)
            dve.wait_ge(sem("zeroed"), 1)
            v.memset(r_wk[:, 1:24:3], 1.0)
            v.memset(r_wk[:, 31:54:3], 1.0).then_inc(sem("zeroed"), 1)
            dve.wait_ge(sem("zeroed"), 2)
            dve.wait_ge(sem("w_in"), 16)
            dve.wait_ge(sem("x_in"), 16)
            dve.wait_ge(sem("act_setup"), 1)
            dve.wait_ge(sem("pool_bn"), 2)
            for k in range(NB):
                for q in range(2):
                    v.tensor_tensor(wpair[:, k, q], w(f"wxbc{k}"), w(f"taps{k}", q * XBC, (q + 1) * XBC), ALU.mult)
                v.tensor_scalar(wout[:, k], w(f"wout{k}"), w(f"normw{k}"), None, ALU.mult)
                for j in range(J):
                    v.tensor_scalar(dhalf[:, k, j], w(f"dskip{k}"), 0.5, None, ALU.mult)
            v.tensor_scalar(aneg[:].rearrange("p k j h -> p (k j h)"), aneg[:].rearrange("p k j h -> p (k j h)"), -1.0, None, ALU.mult)
            v.tensor_scalar(wr8[:], w("wr"), 1.0 / B, None, ALU.mult)
            for l in (0, 1):
                v.tensor_tensor(bn0s[:, l], bn0s[:, l], w(f"f0g{l + 1}"), ALU.mult)
                v.tensor_tensor(bn0b[:, l], w(f"f0b{l + 1}"), w(f"f0m{l + 1}"), ALU.subtract)
            v.tensor_tensor(bn3s[:], bn3s[:], w("bng"), ALU.mult).then_inc(sem("dve_setup"), 1)
            dve.wait_ge(sem("dve_setup"), 1)
            v.tensor_tensor(bn0b[:].rearrange("p l q -> p (l q)"), bn0b[:].rearrange("p l q -> p (l q)"),
                            bn0s[:].rearrange("p l q -> p (l q)"), ALU.mult)
            v.tensor_tensor(bn3b[:], bn3s[:], w("bnm"), ALU.mult).then_inc(sem("dve_setup"), 1)
            dve.wait_ge(sem("dve_setup"), 2)
            for l in (0, 1):
                v.tensor_tensor(bn0b[:, l], bn0b[:, l], w(f"f0be{l + 1}"), ALU.add)
            v.tensor_tensor(bn3b[:], w("bnb"), bn3b[:], ALU.subtract)
            v.tensor_copy(lwgo[:, 0:64], w("ugo", 0, 64))
            v.tensor_scalar(lwgo[:, 64:128], w("ugo", 64, 128), 0.5, None, ALU.mult)
            v.tensor_scalar(lwi[:], w("ui"), 0.5, None, ALU.mult)
            v.tensor_scalar(lvgo[:, 0:64], w("vgo", 0, 64), 0.5, None, ALU.mult)
            v.tensor_scalar(lvgo[:, 64:128], w("vgo", 64, 128), 0.25, None, ALU.mult)
            v.tensor_scalar(lvi[:], w("vi"), 0.25, None, ALU.mult)
            v.tensor_scalar(wqs[:], w("wq"), w("ascale")[0:64], None, ALU.mult).then_inc(sem("dve_setup"), 1)
            dve.wait_ge(sem("dve_setup"), 3)
            for name in CREDIT:
                dve.sem_inc(sem(name), 1)
            dve.sem_inc(sem("a_halo"), 2)
            dve.sem_inc(sem("setup"), 1)
            with dve.Fori(0, NT) as i:
                run(mamba_dve(dve, i))
                if stages >= 2: run(ffn0_dve(dve, i))
                if stages >= 3: run(prod_dve(dve, i, 0, psB, "x2_done", "x3_done"))
                if stages >= 4: run(moe_dve(dve, i, "m0", mix1, psC, X[:, i], (sem("x3_done"), i + 2), "x4_done", False))
                if stages >= 5: run(prod_dve(dve, i, 1, psC, "x4_done", "x5_done"))
                if stages >= 6: run(xproj_dve(dve, i), lstm_dve(dve, i), post_dve(dve, i))

        @block.tensor
        def _(pe):
            pe.wait_ge(sem("setup"), 1)
            with pe.Fori(0, NT) as i:
                run(mamba_pe(pe, i))
                if stages >= 2: run(ffn0_pe(pe, i))
                if stages >= 3: run(prod_pe(pe, i, 0, psB))
                if stages >= 4: run(moe_pe(pe, i, "m0", mix1, psC, 8, M1, (sem("x5_done"), i + 1)))
                if stages >= 5: run(prod_pe(pe, i, 1, psC))
                if stages >= 6: run(xproj_pe(pe, i), lstm_pe(pe, i), post_pe(pe, i))

        block_ctx.__exit__(None, None, None)
        if stages < 9:
            return
        next_phase()
        phase1.close()

        NU = IMG * IMG // P
        XN = X[:].rearrange("p i j c -> p (i j) c")
        HALF = IMG * IMG // 2
        Y3 = resident("Y3", P, B4, IMG * IMG)
        conv = ExitStack()
        dg = conv.enter_context(nc.sbuf_tensor("dg", [P, KT * KT, P], F32))
        DVE_CHUNKS, PE_CHUNKS = range(0, 5), range(5, 8)

        def chunk(q):
            return Y3[:, q // 2, (q % 2) * HALF:(q % 2 + 1) * HALF]

        def window(q, ky, kx):
            r0 = (q % 2) * 16
            return img[:, q // 2, r0 + ky:r0 + ky + 16, kx:kx + IMG] if isinstance(ky, int) else \
                img[:, q // 2, bass.ds(ky + r0, 16), kx:kx + IMG]

        with nc.Block() as block:
            @block.sync
            def _(sp):
                sp.dma_start(XN, x6d[:, :, :].rearrange("b (u p) c -> p (b u) c", p=P)).then_inc(sem("xn_in"), 16)
                sp.wait_ge(sem("xn_in"), 16)

            @block.vector
            def _(dve):
                v = nc.vector
                v.tensor_tensor(dg[:], bc(ident, 1, KT * KT), bc(w("dw"), 2, P), ALU.mult).then_inc(sem("diag"), 1)
                nd = len(DVE_CHUNKS)
                for q in DVE_CHUNKS:
                    last = v.memset(chunk(q), 0.0)
                last.then_inc(sem("dw_zero"), 1)
                dve.wait_ge(sem("dw_zero"), 1)
                dve.wait_ge(sem("diag"), 1)
                with dve.Fori(0, KT) as ky:
                    for kx in range(KT):
                        if kx:
                            dve.wait_ge(sem("dw_tap"), ky * KT + kx)
                        for q in DVE_CHUNKS:
                            o = chunk(q).rearrange("p (r t) -> p r t", r=16)
                            last = v.scalar_tensor_tensor(o, window(q, ky, kx), w("dw")[:, bass.ds(ky * KT + kx, 1)], o, ALU.mult, ALU.add)
                        last.then_inc(sem("dw_tap"), 1)
                    dve.wait_ge(sem("dw_tap"), (ky + 1) * KT)
                for n, q in enumerate(DVE_CHUNKS):
                    v.tensor_scalar(chunk(q), chunk(q), 0.0, None, ALU.max).then_inc(sem("dw_relu"), 1)
                for n, q in enumerate(DVE_CHUNKS):
                    dve.wait_ge(sem("dw_relu"), n + 1)
                    v.tensor_scalar(chunk(q), chunk(q), bn3s[:], bn3b[:], ALU.mult, ALU.add).then_inc(sem("y3"), 1)
                for n, q in enumerate(PE_CHUNKS):
                    dve.wait_ge(sem("dw_pr"), n + 1)
                    v.tensor_scalar(chunk(q), chunk(q), bn3s[:], bn3b[:], ALU.mult, ALU.add).then_inc(sem("y3"), 1)

            @block.scalar
            def _(act):
                for n, q in enumerate(PE_CHUNKS):
                    act.wait_ge(sem("dw_mm"), n + 1)
                    nc.scalar.activation(chunk(q), psA[:, n % 2, :], ACT.Relu).then_inc(sem("dw_pr"), 1)
                act.wait_ge(sem("wvo"), 1)
                nc.scalar.activation(wvo[:], psB[0:64, 0, 0:64], ACT.Copy).then_inc(sem("wvos"), 1)

            @block.tensor
            def _(pe):
                pe.wait_ge(sem("diag"), 1)
                nc.tensor.matmul(psB[0:64, 0, 0:64], w("wvT"), w("wo3"), start=True, stop=True).then_inc(sem("wvo"), 1)
                for n, q in enumerate(PE_CHUNKS):
                    if n >= 2:
                        pe.wait_ge(sem("dw_pr"), n - 1)
                    for t in range(KT * KT):
                        last = nc.tensor.matmul(psA[:, n % 2, :].rearrange("p (r t) -> p r t", r=16), dg[:, t], window(q, t // KT, t % KT),
                                                start=(t == 0), stop=(t == KT * KT - 1))
                    last.then_inc(sem("dw_mm"), 1)

        next_phase()
        conv.close()

        def sb2(name, *shape):
            return ctx.enter_context(nc.sbuf_tensor(name, list(shape), F32))

        ys = sb2("ys", 64, 2, IMG * IMG)
        qs = sb2("qs", 64, 2, IMG * IMG); ks = sb2("ks", 64, 2, IMG * IMG); vs = sb2("vs", P, 2, NU, C)
        nmax = sb2("nmax", P, 2); rsum = sb2("rsum", P, 2); rinv = sb2("rinv", P, 2)
        at = sb2("at", P, 2, IMG * IMG); atT = sb2("atT", P, 2, NU, P)
        pss = [psA, psB]

        with nc.Block() as block:
            @block.sync
            def _(sp):
                for n in range(2):
                    sp.dma_start(ys[:, n], Y3[64 * n:64 * n + 64, 0, :]).then_inc(sem(f"ys{n}"), 16)
                with sp.Fori(1, B4) as b:
                    for n in range(2):
                        sp.wait_ge(sem("v_mm"), b * 2 + (n - 1))
                        sp.dma_start(ys[:, n], Y3[64 * n:64 * n + 64, b, :]).then_inc(sem(f"ys{n}"), 16)

            @block.tensor
            def _(pe):
                with pe.Fori(0, B4) as b:
                    for n in range(2):
                        m = b * 2 + (n + 1)
                        g0 = b * (2 * NU) + n * NU
                        pe.wait_ge(sem(f"ys{n}"), b * 16 + 16)
                        pe.wait_ge(sem("a_exp"), g0 + 2)
                        settle(pe)
                        for h in range(2):
                            nc.tensor.matmul(psA[0:64, h, :], wqs[:], ys[:, n, h * 512:(h + 1) * 512], start=True, stop=True)
                            last = nc.tensor.matmul(psB[0:64, h, :], w("wk"), ys[:, n, h * 512:(h + 1) * 512], start=True, stop=True)
                        last.then_inc(sem("qk_mm"), 1)
                        pe.wait_ge(sem("at_c0"), g0 + 2)
                        settle(pe)
                        for u in range(NU):
                            last = nc.tensor.matmul(psC[:, 0, u * C:(u + 1) * C], ys[:, n, u * P:(u + 1) * P], wvo[:], start=True, stop=True)
                        last.then_inc(sem("v_mm"), 1)
                        pe.wait_ge(sem("q_s"), m)
                        pe.wait_ge(sem("k_s"), m)

                        def scores(u):
                            pe.wait_ge(sem("a_exp"), g0 + (u + 1))
                            for h in range(2):
                                last = nc.tensor.matmul(pss[u % 2][:, h, :], qs[:, n, u * P:(u + 1) * P], ks[:, n, h * 512:(h + 1) * 512],
                                                        start=True, stop=True)
                            last.then_inc(sem("sc"), 1)

                        scores(0)
                        for u in range(NU):
                            if u + 1 < NU:
                                scores(u + 1)
                            pe.wait_ge(sem("a_exp"), g0 + (u + 3))
                            if u == 0:
                                pe.wait_ge(sem("v_s"), m)
                            for c in range(NU):
                                if c == 0:
                                    pe.wait_ge(sem("at_c0"), g0 + (u + 2))
                                if c == 4:
                                    pe.wait_ge(sem("at_c1"), g0 + (u + 2))
                                last = nc.tensor.transpose(psC[:, c // 4, (c % 4) * P:(c % 4 + 1) * P], at[:, u % 2, c * P:(c + 1) * P], ident)
                                if c == 3:
                                    last.then_inc(sem("aT0"), 1)
                            last.then_inc(sem("aT1"), 1)
                            pe.wait_ge(sem("xo"), g0 + (u + 1))
                            for c in range(NU):
                                if c == 0:
                                    pe.wait_ge(sem("at_c0"), g0 + (u + 3))
                                if c == 4:
                                    pe.wait_ge(sem("at_c1"), g0 + (u + 3))
                                last = nc.tensor.matmul(psL[:, u % 2, 0:C], atT[:, u % 2, c], vs[:, n, c], start=(c == 0), stop=(c == NU - 1))
                            last.then_inc(sem("av"), 1)

            @block.scalar
            def _(act):
                with act.Fori(0, B4) as b:
                    for n in range(2):
                        m = b * 2 + (n + 1)
                        g0 = b * (2 * NU) + n * NU
                        act.wait_ge(sem("qk_mm"), m)
                        nc.scalar.activation(qs[:, n].rearrange("p (h t) -> p h t", h=2), psA[0:64, :, :], ACT.Copy).then_inc(sem("q_s"), 1)
                        act.wait_ge(sem("v_mm"), m)
                        nc.scalar.activation(vs[:, n].rearrange("p u c -> p (u c)"), psC[:, 0, :], ACT.Copy).then_inc(sem("v_s"), 1)
                        for u in range(NU):
                            act.wait_ge(sem("nmax"), g0 + (u + 1))
                            act.wait_ge(sem("aT1"), g0 + (u + 1))
                            nc.scalar.activation(at[:, u % 2].rearrange("p (h t) -> p h t", h=2), pss[u % 2][:], ACT.Exp,
                                                 bias=nmax[:, u % 2:u % 2 + 1], accum_out=rsum[:, u % 2:u % 2 + 1]).then_inc(sem("a_exp"), 1)
                            act.wait_ge(sem("aT0"), g0 + (u + 1))
                            act.wait_ge(sem("av"), g0 + (u + 1))
                            nc.scalar.activation(atT[:, u % 2, 0:4].rearrange("p c q -> p (c q)"), psC[:, 0, :], ACT.Copy).then_inc(sem("at_c0"), 1)

            @block.vector
            def _(dve):
                v = nc.vector
                for name in ("a_exp", "at_c0", "at_c1", "aT1", "av", "xo"):
                    dve.sem_inc(sem(name), 2)
                with dve.Fori(0, B4) as b:
                    for n in range(2):
                        m = b * 2 + (n + 1)
                        g0 = b * (2 * NU) + n * NU
                        dve.wait_ge(sem("qk_mm"), m)
                        v.tensor_scalar(ks[:, n].rearrange("p (h t) -> p h t", h=2), psB[0:64, :, :], 0.0, None, ALU.max).then_inc(sem("k_s"), 1)
                        for u in range(NU + 1):
                            if u < NU:
                                dve.wait_ge(sem("sc"), g0 + (u + 1))
                                dve.wait_ge(sem("a_exp"), g0 + (u + 1))
                                v.tensor_reduce(nmax[:, u % 2:u % 2 + 1], pss[u % 2][:].rearrange("p h t -> p (h t)"), AX, ALU.max, negate=True)\
                                    .then_inc(sem("nmax"), 1)
                            if u:
                                r = (u - 1) % 2
                                dve.wait_ge(sem("aT1"), g0 + (u + 2))
                                dve.wait_ge(sem("av"), g0 + u)
                                v.tensor_copy(atT[:, r, 4:8].rearrange("p c q -> p (c q)"), psC[:, 1, :]).then_inc(sem("at_c1"), 1)
                                v.reciprocal(rinv[:, r:r + 1], rsum[:, r:r + 1]).then_inc(sem("rinv"), 1)
                                dve.wait_ge(sem("rinv"), g0 + u)
                                dve.wait_ge(sem("av"), g0 + (u + 2))
                                xo = XN[:, bass.ds(n * B4 * NU + b * NU + (u - 1), 1), :].rearrange("p o c -> p (o c)")
                                v.scalar_tensor_tensor(xo, psL[:, r, 0:C], rinv[:, r:r + 1], xo, ALU.mult, ALU.add).then_inc(sem("xo"), 1)

        next_phase()

        LANES = 4
        mixes = [moe_bufs(f"mix{k}", sb2, 4) for k in range(LANES)]
        banks = [psA, psB, psC, psL]
        M2 = ("m2gate", "m2gateb", "m2w1", "m2w2", "m2b2")
        o_v = out.rearrange("b (u p) c -> p (b u) c", p=P)
        XT = X[:]

        def side_by_side(gens):
            while gens:
                for g in list(gens):
                    if next(g, gens) is gens:
                        gens.remove(g)

        with nc.Block() as block:
            @block.sync
            def _(sp):
                with sp.Fori(0, NT // LANES) as i:
                    for k in range(LANES):
                        sp.wait_ge(sem(f"done{k}"), i + 2)
                        sp.dma_start(o_v[:, bass.ds(i * (2 * LANES) + 2 * k, 2), :], XN[:, bass.ds(i * (2 * LANES) + 2 * k, 2), :])\
                            .then_inc(sem("out"), 16)
                sp.wait_ge(sem("out"), NT * 16)

            @block.gpsimd
            def _(pool):
                with pool.Fori(0, NT // LANES) as i:
                    for k in range(LANES):
                        ln_pool(pool, f"m{k}", mixes[k]["ln"], 1e-5, i + 1)

            @block.scalar
            def _(act):
                with act.Fori(0, NT // LANES) as i:
                    side_by_side([moe_act(act, i, f"m{k}", mixes[k], banks[k], 4, "m2b1") for k in range(LANES)])

            @block.vector
            def _(dve):
                for k in range(LANES):
                    nc.vector.memset(mixes[k]["g"][:], NEG)
                    last = nc.vector.memset(mixes[k]["rep"][:], NEG)
                last.then_inc(sem("pad"), 1)
                dve.wait_ge(sem("pad"), 1)
                for k in range(LANES):
                    dve.sem_inc(sem(f"done{k}"), 1)
                with dve.Fori(0, NT // LANES) as i:
                    side_by_side([moe_dve(dve, i, f"m{k}", mixes[k], banks[k], XT[:, bass.ds(i * LANES + k, 1)].rearrange("p o j c -> p (o j) c"),
                                          None, f"done{k}", True) for k in range(LANES)])

            @block.tensor
            def _(pe):
                with pe.Fori(0, NT // LANES) as i:
                    side_by_side([moe_pe(pe, i, f"m{k}", mixes[k], banks[k], 4, M2, (sem(f"done{k}"), i + 1)) for k in range(LANES)])


UPTO = "all"


def kernel(**inputs):
    import concourse.bacc as bacc
    from concourse.bass_utils import run_bass_kernel_spmd

    a = {k: np.asarray(v) for k, v in inputs.items()}
    pack = np.zeros((P, NPACK), np.float32)

    def put(name, v):
        r, at, c = COL[name]
        pack[0:r, at:at + c] = np.asarray(v).reshape(r, c)

    def rows(v, n=P):
        return np.tile(np.asarray(v).reshape(1, -1), (n, 1))

    def pairs(v):
        o = np.zeros((P, 4, 2, v.shape[2]), np.float32)
        for e in range(E):
            o[64 * (e % 2):64 * (e % 2) + 64, e // 2, e % 2] = v[e]
        return o

    def pairv(v):
        return v.reshape(4, 2 * 64).T

    p = np.arange(P)
    same = (p[:, None] // TT) == (p[None, :] // TT)
    put("ident", np.eye(P))
    put("triblk", same & (p[:, None] <= p[None, :]))
    put("strictblk", same & (p[:, None] > p[None, :]))
    put("indblk", (p[:, None] // TT) == (p[None, :] // DS) % B4)
    put("tri32", (p[:, None] % TT) <= np.arange(TT)[None, :])
    put("maskb", 0.5 * ((p[:, None] // TT) == np.arange(B4)[None, :]))
    put("ones", np.ones(P))
    for k in range(NB):
        wi, cw = a["L0_conv_in_proj_w"][k], a["L0_conv_conv_w"][k][:, 0]
        put(f"wzd{k}", np.concatenate([wi[0:DI], wi[DI + XBC:]]).T)
        put(f"wxbc{k}", np.concatenate([wi[DI:DI + XBC].T] * 2))
        taps = np.concatenate([rows(cw[:, 3], 64), rows(cw[:, 2], 64)]), np.concatenate([rows(cw[:, 1], 64), rows(cw[:, 0], 64)])
        put(f"taps{k}", np.concatenate(taps, 1))
        put(f"bias{k}", np.concatenate([np.zeros(DI, np.float32), a["L0_conv_dt_bias"][k], a["L0_conv_conv_b"][k]]))
        put(f"alog{k}", rows(a["L0_conv_A_log"][k]))
        put(f"dskip{k}", rows(a["L0_conv_D"][k]))
        put(f"normw{k}", a["L0_conv_norm_w"][k])
        put(f"wout{k}", np.concatenate([a["L0_conv_out_proj_w"][k].T] * 2, 1))
    put("wr", a["L0_ffn_Wr"]); put("br", a["L0_ffn_br"])
    put("f0w1", a["L0_ffn_W1"].transpose(1, 0, 2)); put("f0w2", pairs(a["L0_ffn_W2"])); put("f0wo", pairs(a["L0_ffn_Wo"]))
    put("f0bo", a["L0_ffn_bo"])
    for l in (1, 2):
        for n, k in (("b", "b"), ("g", "g"), ("be", "be"), ("m", "m"), ("v", "v")):
            put(f"f0{n}{l}", pairv(a[f"L0_ffn_{k}{l}"]))
    put("m1gate", a["L1_ffn_gate_w"]); put("m1gateb", a["L1_ffn_gate_b"]); put("m1w1", a["L1_ffn_W1"].transpose(1, 0, 2))
    put("m1b1", a["L1_ffn_b1"].T); put("m1w2", a["L1_ffn_W2"].transpose(1, 0, 2)); put("m1b2", a["L1_ffn_b2"])
    u, v, bb = ({g: a[f"L2_ffn_{n}_{g}"] for g in "cio"} for n in "UVb")
    put("ugo", np.concatenate([np.concatenate([u["c"], bb["c"][None]]), np.concatenate([u["o"], bb["o"][None]])], 1))
    put("ui", np.concatenate([u["i"], bb["i"][None]]))
    put("vgo", np.concatenate([v["c"], v["o"]], 1)); put("vi", v["i"])
    put("dw", np.tile(a["L3_conv_dw_kernel"].reshape(KT * KT, C).T, (2, 1)))
    for n, k in (("bng", "gamma"), ("bnb", "beta"), ("bnm", "mean"), ("bnv", "var")):
        put(n, np.tile(a[f"L3_conv_bn_{k}"], 2))
    put("wq", a["L3_conv_wq"]); put("wk", a["L3_conv_wk"]); put("wvT", a["L3_conv_wv"].T); put("wo3", a["L3_conv_wo"])
    put("ascale", np.full(P, a["L3_conv_attn_scale"]))
    put("m2gate", a["L3_ffn_router_w"].T); put("m2gateb", np.zeros(E)); put("m2w1", a["L3_ffn_w1"].transpose(1, 0, 2))
    put("m2b1", pairv(a["L3_ffn_b1"])); put("m2w2", pairs(a["L3_ffn_w2"])); put("m2b2", a["L3_ffn_b2"])

    x = a["x"].reshape(J, B4, NT, TT, C).transpose(1, 3, 2, 0, 4).reshape(P, NT, J, C)
    accs = [a[f"L{l}_conv_accumulators"].reshape(NT, 2, 16, C, C).transpose(0, 1, 3, 2, 4).reshape(NT, P, 16, C) for l in (1, 2)]
    arrays = {"x_in": x, "pack_in": pack, "acc1_in": accs[0], "acc2_in": accs[1]}
    arrays = {k: np.ascontiguousarray(v) for k, v in arrays.items()}

    nc = bacc.Bacc("TRN2", target_bir_lowering=False, num_devices=1)
    args = [nc.dram_tensor(k, v.shape, F32, kind="ExternalInput").ap() for k, v in arrays.items()]
    shape = (P, NT, J, C) if UPTO != "all" else (B, IMG * IMG, C)
    o = nc.dram_tensor("out_x", shape, F32, kind="ExternalOutput").ap()
    build(nc, *args, o, upto=UPTO, dump=o)
    r = run_bass_kernel_spmd(nc, [arrays], core_ids=[0]).results[0]["out_x"]
    return np.asarray(r).reshape(B, IMG, IMG, C)
```

```python
from contextlib import ExitStack

import numpy as np

import concourse.bass as bass
from concourse import mybir

P = 128
B, IMG, C = 8, 32, 64
NT = IMG
TT = IMG
J, B4 = 2, 4
NB, DI, DS, NH, HD = 2, 128, 16, 8, 16
ZD = DI + NH
XBC = DI + 2 * DS
PROJ = ZD + XBC
E = 8
KT = 7
PADI = IMG + KT - 1
LB = 8
NEG = -1.0

F32 = mybir.dt.float32
BF16 = mybir.dt.bfloat16
ALU = mybir.AluOpType
ACT = mybir.ActivationFunctionType
AX = mybir.AxisListType.X


PACK = [
    ("ident", 128, 128), ("triblk", 128, 128), ("strictblk", 128, 128), ("indblk", 128, 128),
    ("tri32", 128, 32), ("maskb", 128, 4),
]
for _b in range(NB):
    PACK += [(f"wzd{_b}", 64, ZD), (f"wxbc{_b}", 128, XBC), (f"taps{_b}", 128, 2 * XBC), 
             (f"alog{_b}", 128, NH), (f"dskip{_b}", 128, NH), (f"normw{_b}", 128, 1), (f"wout{_b}", 128, 2 * C)]
PACK += [("wr", 64, E), ("f0w1", 64, E * 64), ("f0w2", 128, 512), ("f0wo", 128, 512)]
PACK += [(f"f0{_n}{_l}", 128, 4) for _l in (1, 2) for _n in ("b", "g", "be", "m", "v")]
PACK += [("m1gate", 64, E), ("m1w1", 64, E * 128), ("m1b1", 128, 8), ("m1w2", 128, 512)]
PACK += [("ugo", 65, 128), ("ui", 65, 64), ("vgo", 64, 128), ("vi", 64, 64)]
PACK += [("dw", 128, KT * KT), ("bng", 128, 1), ("bnb", 128, 1), ("bnm", 128, 1), ("bnv", 128, 1),
         ("wq", 64, 64), ("wk", 64, 64), ("wvT", 64, 64), ("wo3", 64, 64), ("ascale", 128, 1)]
PACK += [("m2gate", 64, E), ("m2w1", 64, E * 64), ("m2b1", 128, 4), ("m2w2", 128, 512)]
BIASES = [(f"bias{_b}", 1, PROJ) for _b in range(NB)] + [("br", 1, E), ("f0bo", 1, 512), ("m1gateb", 1, E), ("m1b2", 1, 512), ("m2gateb", 1, E), ("m2b2", 1, 512)]
PACK += BIASES
COL = {}
_at = 0
for _n, _r, _c in PACK:
    COL[_n] = (_r, _at, _c)
    _at += _c
NPACK = _at
BIAS0 = COL[BIASES[0][0]][1]
NBIAS = NPACK - BIAS0

DVE_A = 17


class Steps:

    def __init__(self, eng, sem, tile, per_tile):
        self.eng, self.sem, self.base, self.per, self.n = eng, sem, tile * per_tile, per_tile, 0

    def did(self, ins):
        ins.then_inc(self.sem, 1)
        self.n += 1

    def wait(self):
        self.eng.wait_ge(self.sem, self.base + self.n)

    def end(self):
        assert self.n == self.per, (self.sem, self.n, self.per)


def bc(ap, axis, n):
    ap = ap.unsqueeze(axis)
    shape = list(ap.shape)
    shape[axis] = n
    return ap.broadcast_to(shape)


def build(nc, x_in, pack_in, acc1_in, acc2_in, out):
    with ExitStack() as ctx:
        def resident(name, *shape):
            return ctx.enter_context(nc.sbuf_tensor(name, list(shape), F32))

        sems = {}
        phase = [""]

        def sem(name):
            if name not in sems:
                sems[name] = nc.alloc_semaphore(name=f"{phase[0]}{name}")
            return sems[name]

        def next_phase():
            nc.all_engine_barrier()
            nc.clear_and_free_semaphores(list(sems.values()))
            nc.all_engine_barrier()
            sems.clear()
            phase[0] += "n_"

        X = resident("X", P, NT, J, C)
        W = resident("W", P, NPACK)
        ident = W[:, COL["ident"][1]:COL["ident"][1] + 128]

        def w(name, c0=0, c1=None):
            r, at, c = COL[name]
            return W[0:r, at + c0:at + (c if c1 is None else c1)]

        def wb(name):
            r, at, c = COL[name]
            return bias3[:, at - BIAS0:at - BIAS0 + c]

        bias3 = ctx.enter_context(nc.sbuf_tensor("bias3", [65, NBIAS], BF16))
        ones3 = ctx.enter_context(nc.sbuf_tensor("ones3", [65, P], BF16))
        wpair = resident("wpair", P, NB, 2, XBC)
        aneg = resident("aneg", P, NB, J, NH)
        dhalf = resident("dhalf", P, NB, J, NH)
        wout = resident("wout", P, NB, 2 * C)
        bn0s = resident("bn0s", P, 2, 4)
        bn0b = resident("bn0b", P, 2, 4)
        lwgo = resident("lwgo", 65, 128)
        lwi = resident("lwi", 65, 64)
        lvgo = resident("lvgo", 64, 128)
        lvi = resident("lvi", 64, 64)
        wr8 = resident("wr8", 64, E)
        bn3s = resident("bn3s", P, 1)
        bn3b = resident("bn3b", P, 1)
        wqs = resident("wqs", 64, 64)
        wvo = resident("wvo", 64, 64)
        epst = resident("epst", P, 4)
        tmp0 = resident("tmp0", P, 64)
        epss = resident("epss", P, J, 2)

        psA = ctx.enter_context(nc.psum_tensor("psA", [P, 2, 512], F32))
        psB = ctx.enter_context(nc.psum_tensor("psB", [P, 2, 512], F32))
        psC = ctx.enter_context(nc.psum_tensor("psC", [P, 2, 512], F32))
        psL = ctx.enter_context(nc.psum_tensor("psL", [P, 2, 512], F32))

        img = resident("img", P, B4, PADI, PADI)
        x6d = nc.dram_tensor("x6d", [B, IMG * IMG, C], F32)
        phase1 = ctx.enter_context(ExitStack())

        def sb(name, *shape):
            return phase1.enter_context(nc.sbuf_tensor(name, list(shape), F32))

        bpart = phase1.enter_context(nc.sbuf_tensor("bpart", [1, 3, NBIAS], BF16))
        brest = sb("brest", 1, NBIAS)
        a_st = sb("a_st", P, J, 6); a_mv = sb("a_mv", P, J, 2); a_rs = sb("a_rs", P, J)
        a_xn = sb("a_xn", P, J, 2, C)
        hb = sb("hb", P, NB, 2, B, TT)
        hh = sb("hh", P, NB, B, 3)
        a_abs = sb("a_abs", P, J, NH); a_rx = sb("a_rx", P, J, NH); a_u = sb("a_u", P, J, NH)
        a_t = sb("a_t", P, 3, J, NH)
        a_dt = sb("a_dt", P, J, NH); a_a = sb("a_a", P, J, NH);
        a_T = sb("a_T", P, J, PROJ); a_S = sb("a_S", P, J, PROJ)
        a_bc = sb("a_bc", P, J, 2, B4, DS)
        a_xd = sb("a_xd", P, J, DI)
        a_R = sb("a_R", P, J * NH, TT); a_E = sb("a_E", P, J * NH, TT); a_ex = sb("a_ex", P, 3, J, NH)
        a_bct = sb("a_bct", 64, 2, J, P)
        a_xe = sb("a_xe", P, J, NH, HD)
        a_dtm = sb("a_dtm", P, J, NH, B4); a_de = sb("a_de", P, J, NH)
        a_xw = sb("a_xw", P, J, NH, B4, HD)
        a_G = sb("a_G", P, J, TT)
        a_M = sb("a_M", P, J * NH, TT)
        a_yi = sb("a_yi", P, J, DI)
        state = sb("state", 64, NB, J, DI); a_sd = sb("a_sd", 64, J, DI)
        a_y = sb("a_y", P, J, DI); a_sq = sb("a_sq", P, J, DI); a_ss = sb("a_ss", P, J); a_r2 = sb("a_r2", P, J)
        a_yT = sb("a_yT", P, J * P)

        def lnbuf(k):
            return dict(st=sb(f"{k}_st", P, J, 6), mv=sb(f"{k}_mv", P, J, 2), rs=sb(f"{k}_rs", P, J),
                        xn=sb(f"{k}_xn", P, J, C))

        f_ln = lnbuf("f"); f_xT = sb("f_xT", 64, B, TT); f_ft = sb("f_ft", 64, TT); f_fr = sb("f_fr", 64, B4, TT)
        f_w = sb("f_w", P, 5, E); f_s = sb("f_s", P, 4)
        f_h1 = sb("f_h1", P, 4, 256); f_h2 = sb("f_h2", P, 4, 256)
        f_big = sb("f_big", P, J, E, C); f_red = sb("f_red", P, J, C)
        c_ln = [lnbuf("c1"), lnbuf("c2")]
        c_mx = [sb(f"c_mx{k}", P, 2, J) for k in (0, 1)]
        c_e = [sb(f"c_e{k}", P, J, 2, C) for k in (0, 1)]
        c_eT = [sb(f"c_eT{k}", P, 2, B + 1, 16) for k in (0, 1)]
        c_r = [sb(f"c_r{k}", 64, J, 16) for k in (0, 1)]
        c_q = [sb(f"c_q{k}", 64, B, TT) for k in (0, 1)]
        c_l = [sb(f"c_l{k}", P, J, C) for k in (0, 1)]
        accb = [sb(f"accb{k}", P, 16, C) for k in (0, 1)]
        def moe_bufs(m, make, nch):
            return dict(ln={n: make(f"{m}_{n}", *sh) for n, sh in (("st", (P, J, 6)), ("mv", (P, J, 2)), ("rs", (P, J)), ("xn", (P, J, C)))},
                        xT=make(f"{m}_xT", 64, J * P), g=make(f"{m}_g", P, J, 14), mx=make(f"{m}_mx", P, J), sm=make(f"{m}_sm", P, J),
                        d=make(f"{m}_d", P, J, E), top=make(f"{m}_top", P, J, 8), rep=make(f"{m}_rep", P, J, 8),
                        rest=make(f"{m}_rest", P, J, 14), cw=make(f"{m}_cw", P, J, E), h=make(f"{m}_h", P, nch, 256),
                        big=make(f"{m}_big", P, J, E, C), red=make(f"{m}_red", P, J, C))

        mix1 = moe_bufs("m0", sb, 8)
        r_ln = lnbuf("r"); r_xT = sb("r_xT", 65, B, TT)
        r_wk = sb("r_wk", 64, 96); r_c3 = sb("r_c3", 64, 2, 24); r_tc = sb("r_tc", 64, LB)
        r_h = sb("r_h", 64, TT + 1, LB); r_hT = sb("r_hT", 64, B, TT)
        p_ln = lnbuf("p")

        pow_m = epst[:, 0:2]
        EPS = {1e-5: 0, 1e-6: 1}

        block_ctx = nc.Block()
        block = block_ctx.__enter__()


        def settle(eng):
            eng.sem_inc(sem("apart"), 1)

        def ln_vector(dve, k, buf, src, i1, s0, dup=False, out=None):
            yield s0
            settle(dve)
            for j in range(J):
                last = nc.vector.bn_stats(buf["st"][:, j, :], src[:, j, :])
            last.then_inc(sem(k + "_stats"), 1)
            dve.wait_ge(sem(k + "_stats"), i1)
            settle(dve)
            for j in range(J):
                last = nc.vector.bn_aggr(buf["mv"][:, j, :], buf["st"][:, j, :])
            last.then_inc(sem(k + "_var"), 1)
            yield s0 + 1
            dve.wait_ge(sem(k + "_rstd"), i1)
            for j in range(J):
                o = buf["xn"][:, j] if out is None else out[:, j]
                s = src[:, j, :]
                if dup:
                    s = bc(s, 1, 2)
                last = nc.vector.tensor_scalar(o, s, buf["mv"][:, j, 0:1], buf["rs"][:, j:j + 1], ALU.subtract, ALU.mult)
            last.then_inc(sem(k + "_xn"), 1)

        def ln_pool(pool, k, buf, eps, i1):
            pool.wait_ge(sem(k + "_var"), i1)
            nc.gpsimd.tensor_tensor(buf["rs"][:, :], buf["mv"][:, :, 1], epss[:, :, EPS[eps]], ALU.add).then_inc(sem(k + "_vare"), 1)
            pool.wait_ge(sem(k + "_vare"), i1)
            nc.gpsimd.tensor_tensor(buf["rs"][:, :], buf["rs"][:, :], pow_m, ALU.pow).then_inc(sem(k + "_rstd"), 1)

        a_ln = dict(st=a_st, mv=a_mv, rs=a_rs)
        EXC, EXS, EXT = 0, 1, 2

        def mamba_pe(pe, i):
            for k in range(NB):
                n = i * 2 + (k + 1)
                s0 = 16 * k
                if k == 0:
                    pe.wait_ge(sem("a_xn"), i + 1)
                    pe.wait_ge(sem("x1_done"), i + 1)
                    for j in range(J):
                        last = nc.tensor.transpose(psA[:, 0, j * P:(j + 1) * P], a_xn[:, j].rearrange("p d c -> p (d c)"), ident)
                    last.then_inc(sem("a_feed"), 1)
                yield s0 + 2
                pe.wait_ge(sem("a_htop"), n)
                pe.wait_ge(sem("a_hbot"), n)
                pe.wait_ge(sem("a_halo"), n)
                pe.wait_ge(sem("a_hh"), n)
                for j in range(J):
                    if j:
                        yield s0 + 3
                    hfl = hb[:, k].rearrange("p s b t -> p s (b t)")
                    nc.tensor.matmul(psA[:, j, 0:PROJ], ones3[:], wb(f"bias{k}"), start=True, stop=False)
                    nc.tensor.matmul(psA[:, j, 0:ZD], hfl[0:64, 0, j * P:(j + 1) * P], w(f"wzd{k}"), start=False, stop=False)
                    nc.tensor.matmul(psA[:, j, ZD:PROJ], hfl[:, 0, j * P:(j + 1) * P], wpair[:, k, 0, :], start=False, stop=False)
                    last = nc.tensor.matmul(psA[:, j, ZD:PROJ], hfl[:, 1, j * P:(j + 1) * P], wpair[:, k, 1, :], start=False, stop=True)
                last.then_inc(sem("a_zx"), 1)
                yield s0 + 6
                pe.wait_ge(sem("a_S"), n)
                pe.wait_ge(sem("a_bc"), n)
                for j in range(J):
                    last = nc.tensor.transpose(psA[:, 1, j * P:(j + 1) * P], a_bc[:, j].rearrange("p q b n -> p (q b n)"), ident)
                last.then_inc(sem("a_bct"), 1)
                yield s0 + 7
                pe.wait_ge(sem("a_R"), n)
                nc.tensor.matmul(psA[:, 0, :], w("strictblk"), a_R[:].rearrange("p h t -> p (h t)"), start=True, stop=True)\
                    .then_inc(sem("a_seg"), 1)
                yield s0 + 8
                pe.wait_ge(sem("a_bcts"), n)
                av = a_a[:].rearrange("p j h -> p (j h)")
                nc.tensor.matmul(psA[:, 1, 0:16], w("triblk"), av, start=True, stop=True)
                nc.tensor.matmul(psA[:, 1, 16:32], w("strictblk"), av, start=True, stop=True)
                nc.tensor.matmul(psA[:, 1, 32:48], w("indblk"), av, start=True, stop=True).then_inc(sem("a_sum"), 1)
                yield s0 + 9
                pe.wait_ge(sem("a_ex"), n)
                for j in range(J):
                    last = nc.tensor.matmul(psA[:, 0, j * P:(j + 1) * P], a_bct[:, 0, j], a_bct[:, 1, j], start=True, stop=True)
                last.then_inc(sem("a_G"), 1)
                for j in range(J):
                    last = nc.tensor.matmul(psA[:, 1, j * P:(j + 1) * P], a_bct[:, 1, j], state[:, k, j], start=True, stop=True)
                last.then_inc(sem("a_off"), 1)
                yield s0 + 10
                pe.wait_ge(sem("a_xe"), n)
                pe.wait_ge(sem("a_Gm"), n)
                for j in range(J):
                    last = nc.tensor.matmul(psA[0:64, 0, j * P:(j + 1) * P], a_bc[:, j, 0].rearrange("p b n -> p (b n)"),
                                            a_xe[:, j].rearrange("p h d -> p (h d)"), start=True, stop=True)
                last.then_inc(sem("a_st"), 1)
                yield s0 + 11
                pe.wait_ge(sem("a_M"), n)
                pe.wait_ge(sem("a_xw"), n)
                pe.wait_ge(sem("a_yo"), n)
                for j in range(J):
                    if j:
                        yield s0 + 12
                    for h in range(NH):
                        last = nc.tensor.matmul(psA[0:TT, j, h * B4 * HD:(h + 1) * B4 * HD], a_M[:, j * NH + h],
                                                a_xw[:, j, h].rearrange("p b d -> p (b d)"), start=True, stop=True)
                last.then_inc(sem("a_Y"), 1)
                yield s0 + 15
                pe.wait_ge(sem("a_yn"), n)
                for j in range(J):
                    last = nc.tensor.transpose(psA[:, 0, j * P:(j + 1) * P], a_y[:, j], ident)
                last.then_inc(sem("a_yT"), 1)
                yield s0 + 16
                pe.wait_ge(sem("a_yTs"), n)
                if k == 0:
                    nc.tensor.matmul(psA[:, 1, 0:256], wout[:, k], a_yT[:], start=True, stop=True).then_inc(sem("a_feed"), 1)
                else:
                    for j in range(J):
                        last = nc.tensor.matmul(psA[:, 1, j * C:(j + 1) * C], a_yT[:, j * P:(j + 1) * P], wout[:, k, 0:C],
                                                start=True, stop=True)
                    last.then_inc(sem("a_mo"), 1)
                yield s0 + 16

        def mamba_act(act, i):
            for k in range(NB):
                n = i * 2 + (k + 1)
                s0 = 16 * k
                yield s0 + 1
                act.wait_ge(sem("a_feed"), n)
                fd = psA[0:64, k, 0:256].rearrange("p (b t) -> p b t", b=B)
                nc.scalar.activation(hb[0:64, k, 0], fd, ACT.Copy)
                nc.scalar.activation(hb[0:64, k, 1, :, 2:TT], fd[:, :, 0:TT - 2], ACT.Copy).then_inc(sem("a_htop"), 1)
                yield s0 + 4
                act.wait_ge(sem("a_rx"), n)
                nc.scalar.activation(a_u[:], a_abs[:], ACT.Exp).then_inc(sem("a_u"), 1)
                nc.scalar.activation(a_T[:], psA[:, :, 0:PROJ], ACT.Tanh, scale=0.5).then_inc(sem("a_T"), 1)
                yield s0 + 7
                act.wait_ge(sem("a_bct"), n)
                for q in range(2):
                    last = nc.scalar.activation(a_bct[:, q].rearrange("p j t -> p (j t)"), psA[64 * q:64 * q + 64, 1, 0:2 * P], ACT.Copy)
                last.then_inc(sem("a_bcts"), 1)
                yield s0 + 8
                act.wait_ge(sem("a_seg"), n)
                nc.scalar.activation(a_E[:].rearrange("p h t -> p (h t)"), psA[:, 0, :], ACT.Exp)
                act.wait_ge(sem("a_sum"), n)
                nc.scalar.activation(a_ex[:].rearrange("p s j h -> p (s j h)"), psA[:, 1, 0:48], ACT.Exp).then_inc(sem("a_ex"), 1)
                yield s0 + 12
                act.wait_ge(sem("a_Y"), n)
                for b in range(B4):
                    last = nc.scalar.activation(a_yi[TT * b:TT * b + TT].rearrange("p j (h d) -> p (j h) d", h=NH),
                                                psA[0:TT].rearrange("p j (h b d) -> p (j h) b d", h=NH, b=B4)[:, :, b], ACT.Copy)
                last.then_inc(sem("a_yi"), 1)
                yield s0 + 14
                act.wait_ge(sem("a_y"), n)
                for j in range(J):
                    last = nc.scalar.activation(a_sq[:, j], a_y[:, j], ACT.Square, accum_out=a_ss[:, j:j + 1])
                last.then_inc(sem("a_ss"), 1)
                yield s0 + 15
                act.wait_ge(sem("a_yT"), n)
                nc.scalar.activation(a_yT[:], psA[:, 0, 0:256], ACT.Copy).then_inc(sem("a_yTs"), 1)
                yield s0 + 16

        def norm_dve(dve, i):
            yield 28
            if not (isinstance(i, int) and i == 0):
                dve.wait_ge(sem("a_feed"), i * 2)
            yield from ln_vector(dve, "a", a_ln, X[:, i], i + 1, 28, dup=True, out=a_xn)

        def mamba_dve(dve, i):
            for k in range(NB):
                n = i * 2 + (k + 1)
                s0 = 16 * k
                st = Steps(dve, sem("a_steps"), i * 2 + k, DVE_A)
                v = nc.vector
                yield s0 + 1
                dve.wait_ge(sem("a_feed"), n)
                dve.wait_ge(sem("a_halo"), n)
                fd = psA[:, k, 0:256].rearrange("p (b t) -> p b t", b=B)
                v.tensor_copy(hb[64:128, k, 0, :, 1:TT], fd[64:128, :, 0:TT - 1])
                v.tensor_copy(hb[64:128, k, 1, :, 3:TT], fd[64:128, :, 0:TT - 3]).then_inc(sem("a_hbot"), 1)
                dve.wait_ge(sem("a_htop"), n)
                v.tensor_copy(hh[:, k], fd[:, :, TT - 3:TT]).then_inc(sem("a_hh"), 1)
                yield s0 + 4
                dve.wait_ge(sem("a_zx"), n)
                raw = psA[:, :, DI:ZD]
                st.did(v.tensor_scalar(a_rx[:], raw, 0.0, None, ALU.max)); st.wait()
                v.scalar_tensor_tensor(a_abs[:], a_rx[:], -2.0, raw, ALU.mult, ALU.add).then_inc(sem("a_rx"), 1)
                dve.wait_ge(sem("a_hh"), n)
                v.tensor_copy(hb[64:128, k, 0, :, 0:1], hh[64:128, k, :, 2:3])
                v.tensor_copy(hb[0:64, k, 1, :, 0:2], hh[0:64, k, :, 1:3])
                v.tensor_copy(hb[64:128, k, 1, :, 0:3], hh[64:128, k, :, 0:3]).then_inc(sem("a_halo"), 1)
                yield s0 + 5
                dve.wait_ge(sem("a_T"), n)
                v.scalar_tensor_tensor(a_S[:], a_T[:], 1.0, psA[:, :, 0:PROJ], ALU.add, ALU.mult).then_inc(sem("a_S"), 1)
                dve.wait_ge(sem("a_u"), n)
                s_, s2, pq = a_t[:, 0], a_t[:, 1], a_t[:, 2]
                st.did(v.tensor_scalar(s2, a_u[:], 2.0, None, ALU.add)); st.wait()
                st.did(v.reciprocal(pq, s2)); st.wait()
                st.did(v.tensor_tensor(s_, a_u[:], pq, ALU.mult)); st.wait()
                st.did(v.tensor_tensor(s2, s_, s_, ALU.mult)); st.wait()
                st.did(v.tensor_scalar(pq, s2, 1.0 / 13, None, ALU.mult)); st.wait()
                yield s0 + 6
                for d in (11, 9, 7, 5, 3):
                    st.did(v.scalar_tensor_tensor(pq, pq, 1.0 / d, s2, ALU.add, ALU.mult)); st.wait()
                st.did(v.scalar_tensor_tensor(pq, pq, 1.0, s_, ALU.add, ALU.mult)); st.wait()
                st.did(v.scalar_tensor_tensor(a_dt[:], pq, 2.0, a_rx[:], ALU.mult, ALU.add)); st.wait()
                st.did(v.tensor_tensor(a_a[:], a_dt[:], aneg[:, k], ALU.mult)); st.wait()
                v.tensor_tensor(a_dtm[:], bc(a_dt[:], 3, B4), bc(bc(w("maskb"), 1, NH), 1, J), ALU.mult)
                v.tensor_tensor(a_R[:], bc(w("tri32"), 1, J * NH), bc(a_a[:].rearrange("p j h -> p (j h)"), 2, TT), ALU.mult)\
                    .then_inc(sem("a_R"), 1)
                yield s0 + 9
                dve.wait_ge(sem("a_S"), n)
                dve.wait_ge(sem("a_ex"), n)
                xs = a_S[:, :, ZD:ZD + DI].rearrange("p j (h d) -> p j h d", h=NH)
                st.did(v.scalar_tensor_tensor(a_de[:], a_dt[:], 0.5, a_ex[:, EXS], ALU.mult, ALU.mult)); st.wait()
                v.tensor_tensor(a_xe[:], xs, bc(a_de[:], 3, HD), ALU.mult).then_inc(sem("a_xe"), 1)
                yield s0 + 10
                dve.wait_ge(sem("a_G"), n)
                for b in range(B4):
                    r = slice(TT * b, TT * b + TT)
                    last = v.tensor_tensor(a_G[r], psA[r, 0, 0:2 * P].rearrange("p (j t) -> p j t", j=J)[:, :, TT * b:TT * b + TT], bc(w("tri32")[r], 1, J), ALU.mult)
                last.then_inc(sem("a_Gm"), 1)
                dve.wait_ge(sem("a_Gm"), n)
                v.tensor_tensor(a_M[:].rearrange("p (j h) t -> p j h t", j=J), a_E[:].rearrange("p (j h) t -> p j h t", j=J),
                                bc(a_G[:], 2, NH), ALU.mult).then_inc(sem("a_M"), 1)
                yield s0 + 11
                dve.wait_ge(sem("a_off"), n)
                yv = a_y[:].rearrange("p j (h d) -> p j h d", h=NH)
                v.tensor_tensor(yv, psA[:, 1, 0:256].rearrange("p (j h d) -> p j h d", j=J, h=NH), bc(a_ex[:, EXC], 3, HD), ALU.mult)
                dve.wait_ge(sem("a_st"), n)
                dve.wait_ge(sem("a_sd"), n)
                v.tensor_tensor(state[:, k], a_sd[:], psA[0:64, 0, 0:256].rearrange("p (j d) -> p j d", j=J), ALU.add).then_inc(sem("a_yo"), 1)
                yield s0 + 12
                dve.wait_ge(sem("a_yo"), n)
                dve.wait_ge(sem("a_xd"), n)
                yf = a_y[:].rearrange("p j d -> p (j d)")
                st.did(v.tensor_tensor(yf, yf, a_xd[:].rearrange("p j d -> p (j d)"), ALU.add)); st.wait()
                yield s0 + 13
                dve.wait_ge(sem("a_yi"), n)
                st.did(v.tensor_tensor(yf, yf, a_yi[:].rearrange("p j d -> p (j d)"), ALU.add)); st.wait()
                v.tensor_tensor(a_y[:], a_y[:], a_S[:, :, 0:DI], ALU.mult).then_inc(sem("a_y"), 1)
                yield s0 + 15
                dve.wait_ge(sem("a_r2"), n)
                for j in range(J):
                    last = v.tensor_scalar(a_y[:, j], a_y[:, j], a_r2[:, j:j + 1], None, ALU.mult)
                last.then_inc(sem("a_yn"), 1)
                st.end()
                yield s0 + 17
            dve.wait_ge(sem("a_mo"), i + 1)
            nc.vector.tensor_tensor(X[:, i], X[:, i], psA[:, 1, 0:P].rearrange("p (j c) -> p j c", j=J), ALU.add)\
                .then_inc(sem("x1_done"), 1)

        def mamba_pool(pool, i):
            for k in range(NB):
                n = i * 2 + (k + 1)
                s0 = 16 * k
                g = nc.gpsimd
                yield s0 + 5
                pool.wait_ge(sem("a_S"), n)
                for j in range(J):
                    last = g.tensor_tensor(a_bc[:, j], bc(bc(w("maskb"), 1, 2), 3, DS),
                                           bc(a_S[:, j, ZD + DI:PROJ].rearrange("p (q n) -> p q n", q=2), 2, B4), ALU.mult)
                last.then_inc(sem("a_bc"), 1)
                yield s0 + 8
                pool.wait_ge(sem("a_ex"), n)
                g.tensor_tensor(a_sd[:].rearrange("p j (h d) -> p j h d", h=NH), state[:, k].rearrange("p j (h d) -> p j h d", h=NH),
                                bc(a_ex[0:64, EXT], 3, HD), ALU.mult).then_inc(sem("a_sd"), 1)
                xs = a_S[:, :, ZD:ZD + DI].rearrange("p j (h d) -> p j h d", h=NH)
                for j in range(J):
                    last = g.tensor_tensor(a_xw[:, j], bc(xs[:, j], 2, B4), bc(a_dtm[:, j], 3, HD), ALU.mult)
                last.then_inc(sem("a_xw"), 1)
                g.tensor_tensor(a_xd[:].rearrange("p j (h d) -> p j h d", h=NH), xs, bc(dhalf[:, k], 3, HD), ALU.mult)\
                    .then_inc(sem("a_xd"), 1)
                yield s0 + 14
                pool.wait_ge(sem("a_ss"), n)
                settle(pool)
                g.tensor_scalar(a_r2[:], a_ss[:], 1.0 / DI, 4e-5, ALU.mult, ALU.add).then_inc(sem("a_r2e"), 1)
                pool.wait_ge(sem("a_r2e"), n)
                g.tensor_tensor(a_r2[:], a_r2[:], pow_m, ALU.pow).then_inc(sem("a_r2"), 1)

        def ffn0_pe(pe, i):
            i1 = i + 1
            yield 2
            pe.wait_ge(sem("f_xn"), i1)
            pe.wait_ge(sem("x3_done"), i1)
            settle(pe)
            for j in range(J):
                last = nc.tensor.transpose(psB[0:64, 0, j * P:(j + 1) * P], f_ln["xn"][:, j], ident)
            last.then_inc(sem("f_xT"), 1)
            yield 4
            pe.wait_ge(sem("f_xTs"), i1)
            for q in range(4):
                yield 4 + q // 2
                nc.tensor.matmul(psB[:, q // 2, (q % 2) * 256:(q % 2 + 1) * 256], w("f0w1", q * P, (q + 1) * P),
                                 f_xT[:].rearrange("p b t -> p (b t)"), start=True, stop=True).then_inc(sem("f_mm1"), 1)
            for q in range(4):
                yield 13 + q // 2
                pe.wait_ge(sem("f_h1"), i1)
                nc.tensor.matmul(psB[:, q // 2, (q % 2) * 256:(q % 2 + 1) * 256], w("f0w2", q * P, (q + 1) * P), f_h1[:, q],
                                 start=True, stop=True).then_inc(sem("f_mm2"), 1)
            yield 16
            pe.wait_ge(sem("f_feat"), i1)
            pe.wait_ge(sem("f_h2"), i1)
            nc.tensor.matmul(psB[:, 0, 0:E], ones3[:], wb("br"), start=True, stop=False)
            nc.tensor.matmul(psB[:, 0, 0:E], f_fr[:].rearrange("p b t -> p (b t)"), wr8[:], start=False, stop=True).then_inc(sem("f_lg"), 1)
            yield 20
            pe.wait_ge(sem("f_w"), i1)
            for j in range(J):
                nc.tensor.matmul(psB[:, j, :], ones3[:], wb("f0bo"), start=True, stop=False)
                for q in range(4):
                    yield 20 + j
                    last = nc.tensor.matmul(psB[:, j, q * P:(q + 1) * P], f_h2[:, q, j * P:(j + 1) * P], w("f0wo", q * P, (q + 1) * P),
                                            start=False, stop=(q == 3))
            last.then_inc(sem("f_y"), 1)

        def ffn0_act(act, i):
            i1 = i + 1
            yield 3
            act.wait_ge(sem("f_xT"), i1)
            nc.scalar.activation(f_xT[:].rearrange("p b t -> p (b t)"), psB[0:64, 0, 0:256], ACT.Copy).then_inc(sem("f_xTs"), 1)
            yield 5
            act.wait_ge(sem("f_mm1"), i * 4 + 4)
            for q in range(4):
                last = nc.scalar.activation(f_h1[:, q], psB[:, q // 2, (q % 2) * 256:(q % 2 + 1) * 256], ACT.Relu,
                                            bias=bn0b[:, 0, q:q + 1], scale=bn0s[:, 0, q:q + 1])
            last.then_inc(sem("f_h1"), 1)
            yield 15
            act.wait_ge(sem("f_mm2"), i * 4 + 4)
            for q in range(4):
                last = nc.scalar.activation(f_h2[:, q], psB[:, q // 2, (q % 2) * 256:(q % 2 + 1) * 256], ACT.Relu,
                                            bias=bn0b[:, 1, q:q + 1], scale=bn0s[:, 1, q:q + 1])
            last.then_inc(sem("f_h2"), 1)
            yield 17
            act.wait_ge(sem("f_ld"), i1)
            nc.scalar.activation(f_w[:, 1], f_w[:, 0], ACT.Exp, accum_out=f_s[:, 1:2]).then_inc(sem("f_le"), 1)

        def ffn0_dve(dve, i):
            i1 = i + 1
            v = nc.vector
            dve.wait_ge(sem("x1_done"), i + 2)
            yield from ln_vector(dve, "f", f_ln, X[:, i], i1, 0)
            yield 4
            dve.wait_ge(sem("f_xTs"), i1)
            st = Steps(dve, sem("f_steps"), i, 5)
            st.did(v.tensor_reduce(f_ft[:], f_xT[:].rearrange("p b t -> p t b"), AX, ALU.add)); st.wait()
            v.tensor_copy(f_fr[:], bc(f_ft[:], 1, B4)).then_inc(sem("f_feat"), 1)
            yield 17
            dve.wait_ge(sem("f_lg"), i1)
            st.did(v.tensor_reduce(f_s[:, 0:1], psB[:, 0, 0:E], AX, ALU.max)); st.wait()
            v.tensor_scalar(f_w[:, 0], psB[:, 0, 0:E], f_s[:, 0:1], None, ALU.subtract).then_inc(sem("f_ld"), 1)
            dve.wait_ge(sem("f_le"), i1)
            st.did(v.reciprocal(f_s[:, 2:3], f_s[:, 1:2])); st.wait()
            v.tensor_scalar(f_w[:, 2], f_w[:, 1], f_s[:, 2:3], None, ALU.mult).then_inc(sem("f_w"), 1)
            yield 23
            dve.wait_ge(sem("f_y"), i1)
            st.did(v.tensor_tensor(f_big[:], psB[:].rearrange("p j (e c) -> p j e c", e=E), bc(bc(f_w[:, 2], 1, J), 3, C), ALU.mult)); st.wait()
            yield 24
            st.did(v.tensor_reduce(f_red[:], f_big[:].rearrange("p j e c -> p j c e"), AX, ALU.add)); st.wait()
            st.end()
            v.tensor_tensor(X[:, i], X[:, i], f_red[:], ALU.add).then_inc(sem("x2_done"), 1)

        def prod_pe(pe, i, k, ps, s0):
            i1, c = i + 1, f"c{k}"
            yield s0 + 3
            pe.wait_ge(sem(c + "_e"), i1)
            if k == 1:
                pe.wait_ge(sem("x4_done"), i + 2)
            else:
                pe.wait_ge(sem("x2_done"), i1)
            for j in range(J):
                last = nc.tensor.transpose(ps[:, 0, j * P:(j + 1) * P], c_e[k][:, j].rearrange("p d c -> p (d c)"), ident)
            last.then_inc(sem(c + "_et"), 1)
            yield s0 + 5
            pe.wait_ge(sem(c + "_ets"), i1)
            pe.wait_ge(sem(c + "_acc"), i * 16 + 16)
            settle(pe)
            for t in range(16):
                if t % 8 == 0:
                    yield s0 + (5 + t // 8 * (1 + k))
                last = nc.tensor.matmul(ps[0:64, 0, 0:288].rearrange("p (h b t) -> p h b t", h=2, t=16)[:, :, :, t],
                                        accb[k][:, t], c_eT[k][:, :, :, t], start=True, stop=True)
            last.then_inc(sem(c + "_mm"), 1)
            yield (31, 32)[1 - k]
            pe.wait_ge(sem(c + "_q"), i1)
            settle(pe)
            for j in range(J):
                last = nc.tensor.transpose(ps[:, 0, j * C:(j + 1) * C],
                                           c_q[k][:, j * B4:(j + 1) * B4].rearrange("p b t -> p (b t)"), ident[0:64, 0:64])
            last.then_inc(sem(c + "_qT"), 1)

        def prod_act(act, i, k, ps, s0):
            i1, c = i + 1, f"c{k}"
            yield s0 + 2
            act.wait_ge(sem(c + "_mx"), i1)
            for j in range(J):
                last = nc.scalar.activation(c_e[k][:, j], bc(c_ln[k]["xn"][:, j], 1, 2), ACT.Exp, bias=c_mx[k][:, 1, j:j + 1])
            last.then_inc(sem(c + "_e"), 1)
            yield s0 + 4
            act.wait_ge(sem(c + "_et"), i1)
            for h in range(2):
                r = slice(64 * h, 64 * h + 64)
                last = nc.scalar.activation(c_eT[k][r, h, 0:B], ps[r, 0, 0:256].rearrange("p (b h t) -> p h b t", h=2, t=16)[:, h], ACT.Copy)
            last.then_inc(sem(c + "_ets"), 1)
            yield 33
            act.wait_ge(sem(c + "_qT"), i1)
            nc.scalar.activation(c_l[k][:].rearrange("p j c -> p (j c)"), ps[:, 0, 0:P], ACT.Ln).then_inc(sem(c + "_l"), 1)

        def prod_dve(dve, i, k, ps, s0, before, done):
            i1, c = i + 1, f"c{k}"
            v = nc.vector
            yield s0
            dve.wait_ge(sem(before), i + (1 + k))
            yield from ln_vector(dve, c, c_ln[k], X[:, i], i1, s0)
            dve.wait_ge(sem(c + "_xn"), i1)
            st = Steps(dve, sem(c + "_steps"), i, 2)
            st.did(v.tensor_reduce(c_mx[k][:, 0], c_ln[k]["xn"][:], AX, ALU.max)); st.wait()
            v.tensor_scalar(c_mx[k][:, 1], c_mx[k][:, 0], -1.0, None, ALU.mult).then_inc(sem(c + "_mx"), 1)
            yield s0 + (7 + 2 * k)
            dve.wait_ge(sem(c + "_mm"), i1)
            pv = ps[0:64, 0, 0:288].rearrange("p (h b t) -> p h b t", h=2, b=B + 1)
            st.did(v.reciprocal(c_r[k][:], pv[:, :, B])); st.wait()
            st.end()
            v.tensor_tensor(c_q[k][:].rearrange("p b (h t) -> p h b t", h=2), pv[:, :, 0:B], bc(c_r[k][:], 2, B), ALU.mult)\
                .then_inc(sem(c + "_q"), 1)
            yield 34
            dve.wait_ge(sem(c + "_l"), i1)
            for j in range(J):
                last = v.scalar_tensor_tensor(X[:, i, j], c_l[k][:, j], c_mx[k][:, 0, j:j + 1], X[:, i, j], ALU.add, ALU.add)
            last.then_inc(sem(done), 1)

        def x6_store(sp, i):
            yield 23
            sp.wait_ge(sem("x6_done"), i + 1)
            for j in range(J):
                sp.dma_start(x6d[j * B4:(j + 1) * B4, bass.ts(i, TT), :], X[:, i, j]).then_inc(sem("x6_out"), 16)

        def acc_load(sp, i, k, src):
            sp.dma_start(accb[k][:], src[i]).then_inc(sem(f"c{k}_acc"), 16)

        def acc_next(sp, i, k, src):
            yield 28
            if not (isinstance(i, int) and i == NT - 1):
                sp.wait_ge(sem(f"c{k}_mm"), i + 1)
                acc_load(sp, i + 1, k, src)

        def moe_pe(pe, i, m, u, ps, nch, names, before):
            i1 = i + 1
            gate, gateb, w1, w2, b2 = names
            hw = 512 // nch
            yield 4
            pe.wait_ge(sem(m + "_xn"), i1)
            pe.wait_ge(*before)
            settle(pe)
            for j in range(J):
                last = nc.tensor.transpose(ps[0:64, 0, j * P:(j + 1) * P], u["ln"]["xn"][:, j], ident)
            last.then_inc(sem(m + "_xT"), 1)
            yield 6
            pe.wait_ge(sem(m + "_xTs"), i1)
            for j in range(J):
                nc.tensor.matmul(ps[:, 1, j * E:(j + 1) * E], ones3[:], wb(gateb), start=True, stop=False)
                last = nc.tensor.matmul(ps[:, 1, j * E:(j + 1) * E], u["xT"][:, j * P:(j + 1) * P], w(gate), start=False, stop=True)
            last.then_inc(sem(m + "_lg"), 1)
            yield 7
            pe.wait_ge(sem(m + "_ld"), i1)
            for r in range(nch // 4):
                yield 7 + 4 * r
                if r:
                    pe.wait_ge(sem(m + "_h"), i * (nch // 4) + r)
                for q in range(4):
                    yield 7 + 4 * r + q // 2
                    e = r * 4 + q
                    last = nc.tensor.matmul(ps[:, q // 2, (q % 2) * 256:(q % 2 + 1) * 256], w(w1, e * P, (e + 1) * P), u["xT"][:],
                                            start=True, stop=True)
                last.then_inc(sem(m + "_mm1"), 1)
            yield 14
            pe.wait_ge(sem(m + "_h"), (i + 1) * (nch // 4))
            for j in range(J):
                nc.tensor.matmul(ps[:, j, :], ones3[:], wb(b2), start=True, stop=False)
                for e in range(nch):
                    if e * 2 % nch == 0:
                        yield 14 + 2 * j + e * 2 // nch
                    last = nc.tensor.matmul(ps[:, j, e * hw:(e + 1) * hw], u["h"][:, e, j * P:(j + 1) * P], w(w2, e * hw, (e + 1) * hw),
                                            start=False, stop=(e == nch - 1))
            last.then_inc(sem(m + "_y"), 1)

        def moe_act(act, i, m, u, ps, nch, b1):
            i1 = i + 1
            yield 5
            act.wait_ge(sem(m + "_xT"), i1)
            nc.scalar.activation(u["xT"][:], ps[0:64, 0, 0:256], ACT.Copy).then_inc(sem(m + "_xTs"), 1)
            yield 7
            act.wait_ge(sem(m + "_ld"), i1)
            nc.scalar.activation(u["g"][:, :, 0:E], u["d"][:], ACT.Exp).then_inc(sem(m + "_p"), 1)
            for r in range(nch // 4):
                yield 10 + 3 * r
                act.wait_ge(sem(m + "_mm1"), i * (nch // 4) + (r + 1))
                for q in range(4):
                    e = r * 4 + q
                    last = nc.scalar.activation(u["h"][:, e], ps[:, q // 2, (q % 2) * 256:(q % 2 + 1) * 256], ACT.Gelu, bias=w(b1, e, e + 1))
                last.then_inc(sem(m + "_h"), 1)

        def moe_dve(dve, i, m, u, ps, x, before, done, renorm):
            i1 = i + 1
            v = nc.vector
            yield 2
            if before:
                dve.wait_ge(*before)
            yield from ln_vector(dve, m, u["ln"], x, i1, 2)
            yield 6
            dve.wait_ge(sem(m + "_lg"), i1)
            st = Steps(dve, sem(m + "_steps"), i, 15 if renorm else 10)
            lg = ps[:, 1, 0:J * E].rearrange("p (j e) -> p j e", j=J)
            st.did(v.tensor_reduce(u["mx"][:], lg, AX, ALU.max)); st.wait()
            v.tensor_tensor(u["d"][:], lg, bc(u["mx"][:], 2, E), ALU.subtract).then_inc(sem(m + "_ld"), 1)
            yield 8
            dve.wait_ge(sem(m + "_p"), i1)
            p_ = u["g"][:, :, 0:E]
            st.did(v.tensor_reduce(u["sm"][:], p_, AX, ALU.add)); st.wait()
            st.did(v.reciprocal(u["sm"][:], u["sm"][:])); st.wait()
            st.did(v.tensor_tensor(p_, p_, bc(u["sm"][:], 2, E), ALU.mult)); st.wait()
            settle(dve)
            for j in range(J):
                last = v.max(u["top"][:, j], u["g"][:, j])
            st.did(last); st.wait()
            st.did(v.tensor_copy(u["rep"][:, :, 0:2], u["top"][:, :, 0:2])); st.wait()
            settle(dve)
            for j in range(J):
                last = v.match_replace(u["rest"][:, j], u["rep"][:, j], u["g"][:, j], 0.0)
            st.did(last); st.wait()
            st.did(v.tensor_tensor(u["cw"][:], p_, u["rest"][:, :, 0:E], ALU.subtract)); st.wait()
            if renorm:
                st.did(v.tensor_reduce(u["sm"][:], u["cw"][:], AX, ALU.add)); st.wait()
                st.did(v.tensor_scalar(u["sm"][:], u["sm"][:], 1e-12, None, ALU.max)); st.wait()
                st.did(v.reciprocal(u["mx"][:], u["sm"][:])); st.wait()
                st.did(v.tensor_tensor(u["cw"][:], u["cw"][:], bc(u["mx"][:], 2, E), ALU.mult)); st.wait()
            yield 19
            dve.wait_ge(sem(m + "_y"), i1)
            st.did(v.tensor_tensor(u["big"][:], ps[:].rearrange("p j (e c) -> p j e c", e=E), bc(u["cw"][:], 3, C), ALU.mult)); st.wait()
            yield 20
            st.did(v.tensor_reduce(u["red"][:], u["big"][:].rearrange("p j e c -> p j c e"), AX, ALU.add)); st.wait()
            if renorm:
                st.did(v.tensor_tensor(u["red"][:], u["red"][:], u["ln"]["xn"][:], ALU.add)); st.wait()
            st.end()
            v.tensor_tensor(x, x, u["red"][:], ALU.add).then_inc(sem(done), 1)

        def xproj_pe(pe, i, mixed):
            yield 21
            pe.wait_ge(sem("r_xn"), i + 1)
            pe.wait_ge(sem("x4_done"), mixed)
            settle(pe)
            for j in range(J):
                last = nc.tensor.transpose(psC[0:64, 1, j * P:(j + 1) * P], r_ln["xn"][:, j], ident)
            last.then_inc(sem("r_xT"), 1)
            yield 25
            pe.wait_ge(sem("r_xTs"), i + 1)
            settle(pe)
            yield 32
            pe.wait_ge(sem("r_hr"), i * TT + 1)
            ps = psL[:, 0, :].rearrange("p (t q b) -> p t q b", q=2, b=LB)
            xv = r_xT[:].rearrange("p b t -> p t b")
            nc.tensor.matmul(ps[:, :, 0], lwgo[:], xv, start=True, stop=False, skip_group_check=True)
            nc.tensor.matmul(ps[0:64, :, 1], lwi[:], xv, start=False, stop=False, skip_group_check=True).then_inc(sem("r_xp"), 1)

        def xproj_act(act, i):
            yield 22
            act.wait_ge(sem("r_xT"), i + 1)
            nc.scalar.activation(r_xT[0:64].rearrange("p b t -> p (b t)"), psC[0:64, 1, 0:256], ACT.Copy).then_inc(sem("r_xTs"), 1)

        def xproj_dve(dve, i):
            dve.wait_ge(sem("x5_done"), i + 2)
            yield from ln_vector(dve, "r", r_ln, X[:, i], i + 1, 18)

        TO = r_wk[:, 58:82:3]
        QT = TT // 4

        def lstm_pe(pe, i):
            pe.wait_ge(sem("r_xp"), i + 1)
            for t in range(TT):
                pe.wait_ge(sem("r_hr"), i * TT + (t + 1))
                h = r_h[:, t if t else TT]
                c = t * 2 * LB
                nc.tensor.matmul(psL[:, 0, c:c + LB], lvgo[:], h, start=False, stop=False, skip_group_check=True)
                nc.tensor.matmul(psL[0:64, 0, c + LB:c + 2 * LB], lvi[:], h, start=False, stop=False, skip_group_check=True)\
                    .then_inc(sem("r_z"), 1)
                yield t + 1

        def lstm_act(act, i):
            for t in range(TT):
                n = i * TT + (t + 1)
                c = t * 2 * LB
                act.wait_ge(sem("r_z"), n)
                o = r_wk[:, 2:2 + 84].rearrange("p (g x) -> p g x", x=28)[:, 0:2, 0:24:3]
                nc.scalar.activation(o, psL[0:64, 0, c:c + 2 * LB].rearrange("p (g b) -> p g b", b=LB), ACT.Tanh).then_inc(sem("r_gi"), 1)
                nc.scalar.activation(TO, psL[64:128, 0, c:c + LB], ACT.Tanh)
                act.wait_ge(sem("r_c"), n)
                nc.scalar.activation(r_tc[:], r_c3[:, t % 2, 2::3], ACT.Tanh, scale=0.5).then_inc(sem("r_tc"), 1)
                yield t + 1

        def lstm_dve(dve, i):
            v = nc.vector
            for t in range(TT):
                n = i * TT + (t + 1)
                dve.wait_ge(sem("r_hc"), n)
                dve.wait_ge(sem("r_gi"), n)
                v.tensor_tensor_scan(r_c3[:, t % 2, :], r_wk[:, 0:24], r_wk[:, 30:54], 0.0, ALU.mult, ALU.add).then_inc(sem("r_c"), 1)
                if t % QT == 0:
                    dve.wait_ge(sem("r_hT"), i * 4 + (t // QT + 1))
                dve.wait_ge(sem("r_tc"), n)
                v.scalar_tensor_tensor(r_h[:, t + 1], TO, 1.0, r_tc[:], ALU.add, ALU.mult).then_inc(sem("r_hr"), 1)
                dve.wait_ge(sem("r_hr"), n + 1)
                v.scalar_tensor_tensor(r_wk[:, 32:56:3], r_h[:, t + 1], 0.5, r_c3[:, t % 2, 2::3], ALU.mult, ALU.mult).then_inc(sem("r_hc"), 1)
                yield t + 1

        def lstm_pool(pool, i):
            for q in range(4):
                yield (22, 23, 26, 33)[q]
                pool.wait_ge(sem("r_hr"), i * TT + (QT * q + QT + 1))
                if q == 0:
                    pool.wait_ge(sem("p_hT"), i + 1)
                settle(pool)
                nc.gpsimd.tensor_copy(r_hT[:, :, QT * q:QT * q + QT].rearrange("p b t -> p t b"), r_h[:, QT * q + 1:QT * q + QT + 1])\
                    .then_inc(sem("r_hT"), 1)

        def post_pe(pe, i, mixed):
            yield 21
            pe.wait_ge(sem("r_hT"), i * 4 + 8)
            pe.wait_ge(sem("x4_done"), mixed)
            settle(pe)
            for j in range(J):
                last = nc.tensor.transpose(psC[:, 0, j * C:(j + 1) * C], r_hT[:, j * B4:(j + 1) * B4].rearrange("p b t -> p (b t)"),
                                           ident[0:64, 0:64])
            last.then_inc(sem("p_hT"), 1)
            yield 24
            pe.wait_ge(sem("p_xn"), i + 1)
            nc.tensor.transpose(psC[:, 1, 2 * P:3 * P], p_ln["xn"][:].rearrange("p j c -> p (j c)"), ident).then_inc(sem("p_xT"), 1)
            yield 25
            pe.wait_ge(sem("x6_free"), i + 1)
            settle(pe)

        def post_dve(dve, i):
            yield 22
            dve.wait_ge(sem("p_hT"), i + 2)
            for j in range(J):
                last = nc.vector.scalar_tensor_tensor(X[:, i, j], psC[:, 0, j * C:(j + 1) * C], 0.5, X[:, i, j], ALU.mult, ALU.add)
            last.then_inc(sem("x6_done"), 1)
            dve.wait_ge(sem("x6_done"), i + 1)
            yield from ln_vector(dve, "p", p_ln, X[:, i], i + 1, 22)

        def post_act(act, i):
            yield 24
            act.wait_ge(sem("p_xT"), i + 1)
            nc.scalar.activation(img[:, :, i + 3, 3:3 + IMG], psC[:, 1, 2 * P:3 * P].rearrange("p (b t) -> p b t", b=B4), ACT.Copy)\
                .then_inc(sem("x6_free"), 1)

        def at_slot(slot, step, *args):
            yield slot
            step(*args)

        def weave(parts):
            slots = [(0, g) for g in parts]
            slot = 0
            while slots:
                left = []
                for due, g in slots:
                    while due <= slot:
                        due = next(g, None)
                        if due is None:
                            break
                    if due is not None:
                        left.append((due, g))
                slots = left
                slot += 1

        CREDITS = dict(x1_done=1, x3_done=1, x4_done=1, x5_done=1, r_hr=1, r_hc=1, r_hT=4, p_hT=1, a_halo=2)
        M1 = ("m1gate", "m1gateb", "m1w1", "m1w2", "m1b2")
        LAG = dict(post=-1, lstm=0, xproj=1, mix=2, ffn=3, mamba=4, norm=5)
        FIRST_FULL, LAST_FULL = 1, NT - 1 - LAG["norm"]

        def turns(eng, parts_of):
            def turn(i):
                has = (lambda k: 0 <= i + LAG[k] < NT) if isinstance(i, int) else (lambda k: True)
                weave([part(i + LAG[k] if LAG[k] else i) for k, part in parts_of(i) if has(k)])

            for i in range(-LAG["norm"], FIRST_FULL):
                turn(i)
            with eng.Fori(FIRST_FULL, LAST_FULL + 1) as i:
                turn(i)
            for i in range(LAST_FULL + 1, NT + 1):
                turn(i)

        @block.sync
        def _(sp):
            sp.dma_start(W[:], pack_in).then_inc(sem("w_in"), 16)
            sp.dma_start(X[:], x_in).then_inc(sem("x_in"), 16)
            sp.wait_ge(sem("setup"), 1)
            acc_load(sp, 0, 0, acc1_in)
            acc_load(sp, 0, 1, acc2_in)
            turns(sp, lambda i: [
                ("post", lambda n: x6_store(sp, n)),
                ("mix", lambda n: acc_next(sp, n, 1, acc2_in)),
                ("ffn", lambda n: acc_next(sp, n, 0, acc1_in))])
            sp.wait_ge(sem("x6_out"), NT * 32)

        @block.gpsimd
        def _(pool):
            g = nc.gpsimd
            pool.wait_ge(sem("zeroed"), 2)
            pool.wait_ge(sem("w_in"), 16)
            for l in (1, 2):
                g.tensor_scalar(bn0s[:, l - 1], w(f"f0v{l}"), 1.0, 1e-3, ALU.mult, ALU.add)
            g.tensor_scalar(bn3s[:], w("bnv"), 1.0, 1e-5, ALU.mult, ALU.add).then_inc(sem("pool_bn"), 1)
            pool.wait_ge(sem("pool_bn"), 1)
            for l in (1, 2):
                g.tensor_tensor(bn0s[:, l - 1], bn0s[:, l - 1], epst[:, 0:4], ALU.pow)
            g.tensor_tensor(bn3s[:], bn3s[:], epst[:, 0:1], ALU.pow).then_inc(sem("pool_bn"), 1)

            def ln_at(slot, k, buf, eps, i):
                return at_slot(slot, ln_pool, pool, k, buf, eps, i + 1)

            turns(pool, lambda i: [
                ("lstm", lambda n: lstm_pool(pool, n)),
                ("post", lambda n: ln_at(22, "p", p_ln, 1e-6, n)),
                ("xproj", lambda n: ln_at(18, "r", r_ln, 1e-5, n)),
                ("mix", lambda n: ln_at(2, "m0", mix1["ln"], 1e-5, n)),
                ("mix", lambda n: ln_at(21, "c1", c_ln[1], 1e-6, n)),
                ("ffn", lambda n: ln_at(0, "f", f_ln, 1e-5, n)),
                ("ffn", lambda n: ln_at(25, "c0", c_ln[0], 1e-6, n)),
                ("mamba", lambda n: mamba_pool(pool, n)),
                ("norm", lambda n: ln_at(28, "a", a_ln, 1e-6, n))])

        @block.scalar
        def _(act):
            act.wait_ge(sem("w_in"), 16)
            for k in range(NB):
                for j in range(J):
                    nc.scalar.activation(aneg[:, k, j], w(f"alog{k}"), ACT.Exp)
            nc.scalar.activation(tmp0[:, 0:1], w("normw0"), ACT.Copy).then_inc(sem("act_setup"), 1)
            act.wait_ge(sem("setup"), 1)
            turns(act, lambda i: [
                ("lstm", lambda n: lstm_act(act, n)),
                ("post", lambda n: post_act(act, n)),
                ("xproj", lambda n: xproj_act(act, n)),
                ("mix", lambda n: moe_act(act, n, "m0", mix1, psC, 8, "m1b1")),
                ("mix", lambda n: prod_act(act, n, 1, psC, 21)),
                ("ffn", lambda n: ffn0_act(act, n)),
                ("ffn", lambda n: prod_act(act, n, 0, psB, 25)),
                ("mamba", lambda n: mamba_act(act, n))])

        @block.vector
        def _(dve):
            v = nc.vector
            v.memset(epst[:], -0.5)
            v.memset(ones3[:], 1.0)
            v.memset(bias3[:], 0.0)
            v.memset(epss[:, :, 0], 1e-5)
            v.memset(epss[:, :, 1], 1e-6)
            v.memset(hb[:], 0.0)
            v.memset(hh[:], 0.0)
            v.memset(state[:], 0.0)
            for k in (0, 1):
                v.memset(c_eT[k][:], 0.0)
            v.memset(r_xT[64:65], 1.0)
            v.memset(mix1["g"][:], NEG)
            v.memset(mix1["rep"][:], NEG)
            v.memset(r_c3[:], 0.0)
            v.memset(r_h[:], 0.0)
            v.memset(img[:], 0.0)
            v.memset(r_wk[:], 0.0).then_inc(sem("zeroed"), 1)
            dve.wait_ge(sem("zeroed"), 1)
            v.memset(r_wk[:, 1:24:3], 1.0)
            for k in (0, 1):
                for h in range(2):
                    v.memset(c_eT[k][64 * h:64 * h + 64, h, B], 1.0)
            v.memset(r_wk[:, 31:54:3], 1.0).then_inc(sem("zeroed"), 1)
            dve.wait_ge(sem("zeroed"), 2)
            dve.wait_ge(sem("w_in"), 16)
            dve.wait_ge(sem("x_in"), 16)
            dve.wait_ge(sem("act_setup"), 1)
            dve.wait_ge(sem("pool_bn"), 2)
            bias = W[0:1, BIAS0:NPACK]
            st = Steps(dve, sem("bias_steps"), 0, 7)
            for n in range(3):
                st.did(v.tensor_copy(bpart[:, n], bias if n == 0 else brest[:])); st.wait()
                if n:
                    v.tensor_copy(bias3[32 * n:32 * n + 1], bpart[:, n])
                else:
                    v.tensor_copy(bias3[0:1], bpart[:, 0])
                if n < 2:
                    st.did(v.tensor_tensor(brest[:], bias if n == 0 else brest[:], bpart[:, n], ALU.subtract)); st.wait()
            st.did(v.tensor_copy(tmp0[:, 1:2], tmp0[:, 0:1])); st.wait()
            st.did(v.tensor_copy(tmp0[:, 2:3], tmp0[:, 0:1]))
            st.end()
            for k in range(NB):
                for q in range(2):
                    v.tensor_tensor(wpair[:, k, q], w(f"wxbc{k}"), w(f"taps{k}", q * XBC, (q + 1) * XBC), ALU.mult)
                v.tensor_scalar(wout[:, k], w(f"wout{k}"), w(f"normw{k}"), None, ALU.mult)
                for j in range(J):
                    v.tensor_scalar(dhalf[:, k, j], w(f"dskip{k}"), 0.5, None, ALU.mult)
            v.tensor_scalar(aneg[:].rearrange("p k j h -> p (k j h)"), aneg[:].rearrange("p k j h -> p (k j h)"), -1.0, None, ALU.mult)
            v.tensor_scalar(wr8[:], w("wr"), 1.0 / B, None, ALU.mult)
            for l in (0, 1):
                v.tensor_tensor(bn0s[:, l], bn0s[:, l], w(f"f0g{l + 1}"), ALU.mult)
                v.tensor_tensor(bn0b[:, l], w(f"f0b{l + 1}"), w(f"f0m{l + 1}"), ALU.subtract)
            v.tensor_tensor(bn3s[:], bn3s[:], w("bng"), ALU.mult).then_inc(sem("dve_setup"), 1)
            dve.wait_ge(sem("dve_setup"), 1)
            v.tensor_tensor(bn0b[:].rearrange("p l q -> p (l q)"), bn0b[:].rearrange("p l q -> p (l q)"),
                            bn0s[:].rearrange("p l q -> p (l q)"), ALU.mult)
            v.tensor_tensor(bn3b[:], bn3s[:], w("bnm"), ALU.mult).then_inc(sem("dve_setup"), 1)
            dve.wait_ge(sem("dve_setup"), 2)
            for l in (0, 1):
                v.tensor_tensor(bn0b[:, l], bn0b[:, l], w(f"f0be{l + 1}"), ALU.add)
            v.tensor_tensor(bn3b[:], w("bnb"), bn3b[:], ALU.subtract)
            v.tensor_copy(lwgo[:, 0:64], w("ugo", 0, 64))
            v.tensor_scalar(lwgo[:, 64:128], w("ugo", 64, 128), 0.5, None, ALU.mult)
            v.tensor_scalar(lwi[:], w("ui"), 0.5, None, ALU.mult)
            v.tensor_scalar(lvgo[:, 0:64], w("vgo", 0, 64), 0.5, None, ALU.mult)
            v.tensor_scalar(lvgo[:, 64:128], w("vgo", 64, 128), 0.25, None, ALU.mult)
            v.tensor_scalar(lvi[:], w("vi"), 0.25, None, ALU.mult)
            v.tensor_scalar(wqs[:], w("wq"), w("ascale")[0:64], None, ALU.mult).then_inc(sem("dve_setup"), 1)
            dve.wait_ge(sem("dve_setup"), 3)
            for name, count in CREDITS.items():
                dve.sem_inc(sem(name), count)
            dve.sem_inc(sem("setup"), 1)
            turns(dve, lambda i: [
                ("lstm", lambda n: lstm_dve(dve, n)),
                ("post", lambda n: post_dve(dve, n)),
                ("xproj", lambda n: xproj_dve(dve, n)),
                ("mix", lambda n: moe_dve(dve, n, "m0", mix1, psC, X[:, n], (sem("x3_done"), n + 2), "x4_done", False)),
                ("mix", lambda n: prod_dve(dve, n, 1, psC, 21, "x4_done", "x5_done")),
                ("ffn", lambda n: ffn0_dve(dve, n)),
                ("ffn", lambda n: prod_dve(dve, n, 0, psB, 25, "x2_done", "x3_done")),
                ("mamba", lambda n: mamba_dve(dve, n)),
                ("norm", lambda n: norm_dve(dve, n))])

        @block.tensor
        def _(pe):
            def mixed(i):
                last = i + LAG["mix"]
                return (min(last, NT - 1) if isinstance(i, int) else last) + 2

            pe.wait_ge(sem("setup"), 1)
            turns(pe, lambda i: [
                ("lstm", lambda n: lstm_pe(pe, n)),
                ("post", lambda n: post_pe(pe, n, mixed(i))),
                ("xproj", lambda n: xproj_pe(pe, n, mixed(i))),
                ("mix", lambda n: moe_pe(pe, n, "m0", mix1, psC, 8, M1, (sem("x5_done"), n + 1))),
                ("mix", lambda n: prod_pe(pe, n, 1, psC, 21)),
                ("ffn", lambda n: ffn0_pe(pe, n)),
                ("ffn", lambda n: prod_pe(pe, n, 0, psB, 25)),
                ("mamba", lambda n: mamba_pe(pe, n))])

        block_ctx.__exit__(None, None, None)
        next_phase()
        phase1.close()

        NU = IMG * IMG // P
        XN = X[:].rearrange("p i j c -> p (i j) c")
        HALF = IMG * IMG // 2
        Y3 = resident("Y3", P, B4, IMG * IMG)
        conv = ExitStack()
        dg = conv.enter_context(nc.sbuf_tensor("dg", [P, KT * KT, P], F32))
        DVE_CHUNKS, PE_CHUNKS = range(0, 5), range(5, 8)

        def chunk(q):
            return Y3[:, q // 2, (q % 2) * HALF:(q % 2 + 1) * HALF]

        def window(q, ky, kx):
            r0 = (q % 2) * 16
            return img[:, q // 2, r0 + ky:r0 + ky + 16, kx:kx + IMG] if isinstance(ky, int) else \
                img[:, q // 2, bass.ds(ky + r0, 16), kx:kx + IMG]

        with nc.Block() as block:
            @block.sync
            def _(sp):
                sp.dma_start(XN, x6d[:, :, :].rearrange("b (u p) c -> p (b u) c", p=P)).then_inc(sem("xn_in"), 16)
                sp.wait_ge(sem("xn_in"), 16)

            @block.vector
            def _(dve):
                v = nc.vector
                v.tensor_tensor(dg[:], bc(ident, 1, KT * KT), bc(w("dw"), 2, P), ALU.mult).then_inc(sem("diag"), 1)
                nd = len(DVE_CHUNKS)
                for q in DVE_CHUNKS:
                    last = v.memset(chunk(q), 0.0)
                last.then_inc(sem("dw_zero"), 1)
                dve.wait_ge(sem("dw_zero"), 1)
                dve.wait_ge(sem("diag"), 1)
                with dve.Fori(0, KT) as ky:
                    for kx in range(KT):
                        if kx:
                            dve.wait_ge(sem("dw_tap"), ky * KT + kx)
                        for q in DVE_CHUNKS:
                            o = chunk(q).rearrange("p (r t) -> p r t", r=16)
                            last = v.scalar_tensor_tensor(o, window(q, ky, kx), w("dw")[:, bass.ds(ky * KT + kx, 1)], o, ALU.mult, ALU.add)
                        last.then_inc(sem("dw_tap"), 1)
                    dve.wait_ge(sem("dw_tap"), (ky + 1) * KT)
                for n, q in enumerate(DVE_CHUNKS):
                    v.tensor_scalar(chunk(q), chunk(q), 0.0, None, ALU.max).then_inc(sem("dw_relu"), 1)
                for n, q in enumerate(DVE_CHUNKS):
                    dve.wait_ge(sem("dw_relu"), n + 1)
                    v.tensor_scalar(chunk(q), chunk(q), bn3s[:], bn3b[:], ALU.mult, ALU.add).then_inc(sem("y3"), 1)
                for n, q in enumerate(PE_CHUNKS):
                    dve.wait_ge(sem("dw_pr"), n + 1)
                    v.tensor_scalar(chunk(q), chunk(q), bn3s[:], bn3b[:], ALU.mult, ALU.add).then_inc(sem("y3"), 1)

            @block.scalar
            def _(act):
                for n, q in enumerate(PE_CHUNKS):
                    act.wait_ge(sem("dw_mm"), n + 1)
                    nc.scalar.activation(chunk(q), psA[:, n % 2, :], ACT.Relu).then_inc(sem("dw_pr"), 1)
                act.wait_ge(sem("wvo"), 1)
                nc.scalar.activation(wvo[:], psB[0:64, 0, 0:64], ACT.Copy).then_inc(sem("wvos"), 1)

            @block.tensor
            def _(pe):
                pe.wait_ge(sem("diag"), 1)
                nc.tensor.matmul(psB[0:64, 0, 0:64], w("wvT"), w("wo3"), start=True, stop=True).then_inc(sem("wvo"), 1)
                for n, q in enumerate(PE_CHUNKS):
                    if n >= 2:
                        pe.wait_ge(sem("dw_pr"), n - 1)
                    for t in range(KT * KT):
                        last = nc.tensor.matmul(psA[:, n % 2, :].rearrange("p (r t) -> p r t", r=16), dg[:, t], window(q, t // KT, t % KT),
                                                start=(t == 0), stop=(t == KT * KT - 1))
                    last.then_inc(sem("dw_mm"), 1)

        next_phase()
        conv.close()

        def sb2(name, *shape):
            return ctx.enter_context(nc.sbuf_tensor(name, list(shape), F32))

        ys = sb2("ys", 64, 2, IMG * IMG)
        qs = sb2("qs", 64, 2, IMG * IMG); ks = sb2("ks", 64, 2, IMG * IMG); vs = sb2("vs", P, 2, NU, C)
        nmax = sb2("nmax", P, 2); rsum = sb2("rsum", P, 2); rinv = sb2("rinv", P, 2)
        at = sb2("at", P, 2, IMG * IMG); atT = sb2("atT", P, 2, NU, P)
        pss = [psA, psB]

        with nc.Block() as block:
            @block.sync
            def _(sp):
                for n in range(2):
                    sp.dma_start(ys[:, n], Y3[64 * n:64 * n + 64, 0, :]).then_inc(sem(f"ys{n}"), 16)
                with sp.Fori(1, B4) as b:
                    for n in range(2):
                        sp.wait_ge(sem("v_mm"), b * 2 + (n - 1))
                        sp.dma_start(ys[:, n], Y3[64 * n:64 * n + 64, b, :]).then_inc(sem(f"ys{n}"), 16)

            @block.tensor
            def _(pe):
                with pe.Fori(0, B4) as b:
                    for n in range(2):
                        m = b * 2 + (n + 1)
                        g0 = b * (2 * NU) + n * NU
                        pe.wait_ge(sem(f"ys{n}"), b * 16 + 16)
                        pe.wait_ge(sem("a_exp"), g0 + 2)
                        settle(pe)
                        for h in range(2):
                            nc.tensor.matmul(psA[0:64, h, :], wqs[:], ys[:, n, h * 512:(h + 1) * 512], start=True, stop=True)
                            last = nc.tensor.matmul(psB[0:64, h, :], w("wk"), ys[:, n, h * 512:(h + 1) * 512], start=True, stop=True)
                        last.then_inc(sem("qk_mm"), 1)
                        pe.wait_ge(sem("at_c0"), g0 + 2)
                        settle(pe)
                        for u in range(NU):
                            last = nc.tensor.matmul(psC[:, 0, u * C:(u + 1) * C], ys[:, n, u * P:(u + 1) * P], wvo[:], start=True, stop=True)
                        last.then_inc(sem("v_mm"), 1)
                        pe.wait_ge(sem("q_s"), m)
                        pe.wait_ge(sem("k_s"), m)

                        def scores(u):
                            pe.wait_ge(sem("a_exp"), g0 + (u + 1))
                            for h in range(2):
                                last = nc.tensor.matmul(pss[u % 2][:, h, :], qs[:, n, u * P:(u + 1) * P], ks[:, n, h * 512:(h + 1) * 512],
                                                        start=True, stop=True)
                            last.then_inc(sem("sc"), 1)

                        scores(0)
                        for u in range(NU):
                            if u + 1 < NU:
                                scores(u + 1)
                            pe.wait_ge(sem("a_exp"), g0 + (u + 3))
                            if u == 0:
                                pe.wait_ge(sem("v_s"), m)
                            for c in range(NU):
                                if c == 0:
                                    pe.wait_ge(sem("at_c0"), g0 + (u + 2))
                                if c == 4:
                                    pe.wait_ge(sem("at_c1"), g0 + (u + 2))
                                last = nc.tensor.transpose(psC[:, c // 4, (c % 4) * P:(c % 4 + 1) * P], at[:, u % 2, c * P:(c + 1) * P], ident)
                                if c == 3:
                                    last.then_inc(sem("aT0"), 1)
                            last.then_inc(sem("aT1"), 1)
                            pe.wait_ge(sem("xo"), g0 + (u + 1))
                            for c in range(NU):
                                if c == 0:
                                    pe.wait_ge(sem("at_c0"), g0 + (u + 3))
                                if c == 4:
                                    pe.wait_ge(sem("at_c1"), g0 + (u + 3))
                                last = nc.tensor.matmul(psL[:, u % 2, 0:C], atT[:, u % 2, c], vs[:, n, c], start=(c == 0), stop=(c == NU - 1))
                            last.then_inc(sem("av"), 1)

            @block.scalar
            def _(act):
                with act.Fori(0, B4) as b:
                    for n in range(2):
                        m = b * 2 + (n + 1)
                        g0 = b * (2 * NU) + n * NU
                        act.wait_ge(sem("qk_mm"), m)
                        nc.scalar.activation(qs[:, n].rearrange("p (h t) -> p h t", h=2), psA[0:64, :, :], ACT.Copy).then_inc(sem("q_s"), 1)
                        act.wait_ge(sem("v_mm"), m)
                        nc.scalar.activation(vs[:, n].rearrange("p u c -> p (u c)"), psC[:, 0, :], ACT.Copy).then_inc(sem("v_s"), 1)
                        for u in range(NU):
                            act.wait_ge(sem("nmax"), g0 + (u + 1))
                            act.wait_ge(sem("aT1"), g0 + (u + 1))
                            nc.scalar.activation(at[:, u % 2].rearrange("p (h t) -> p h t", h=2), pss[u % 2][:], ACT.Exp,
                                                 bias=nmax[:, u % 2:u % 2 + 1], accum_out=rsum[:, u % 2:u % 2 + 1]).then_inc(sem("a_exp"), 1)
                            act.wait_ge(sem("aT0"), g0 + (u + 1))
                            act.wait_ge(sem("av"), g0 + (u + 1))
                            nc.scalar.activation(atT[:, u % 2, 0:4].rearrange("p c q -> p (c q)"), psC[:, 0, :], ACT.Copy).then_inc(sem("at_c0"), 1)

            @block.vector
            def _(dve):
                v = nc.vector
                for name in ("a_exp", "at_c0", "at_c1", "aT1", "av", "xo"):
                    dve.sem_inc(sem(name), 2)
                with dve.Fori(0, B4) as b:
                    for n in range(2):
                        m = b * 2 + (n + 1)
                        g0 = b * (2 * NU) + n * NU
                        dve.wait_ge(sem("qk_mm"), m)
                        v.tensor_scalar(ks[:, n].rearrange("p (h t) -> p h t", h=2), psB[0:64, :, :], 0.0, None, ALU.max).then_inc(sem("k_s"), 1)
                        for u in range(NU + 1):
                            if u < NU:
                                dve.wait_ge(sem("sc"), g0 + (u + 1))
                                dve.wait_ge(sem("a_exp"), g0 + (u + 1))
                                v.tensor_reduce(nmax[:, u % 2:u % 2 + 1], pss[u % 2][:].rearrange("p h t -> p (h t)"), AX, ALU.max, negate=True)\
                                    .then_inc(sem("nmax"), 1)
                            if u:
                                r = (u - 1) % 2
                                dve.wait_ge(sem("aT1"), g0 + (u + 2))
                                dve.wait_ge(sem("av"), g0 + u)
                                v.tensor_copy(atT[:, r, 4:8].rearrange("p c q -> p (c q)"), psC[:, 1, :]).then_inc(sem("at_c1"), 1)
                                v.reciprocal(rinv[:, r:r + 1], rsum[:, r:r + 1]).then_inc(sem("rinv"), 1)
                                dve.wait_ge(sem("rinv"), g0 + u)
                                dve.wait_ge(sem("av"), g0 + (u + 2))
                                xo = XN[:, bass.ds(n * B4 * NU + b * NU + (u - 1), 1), :].rearrange("p o c -> p (o c)")
                                v.scalar_tensor_tensor(xo, psL[:, r, 0:C], rinv[:, r:r + 1], xo, ALU.mult, ALU.add).then_inc(sem("xo"), 1)

        next_phase()

        LANES = 4
        mixes = [moe_bufs(f"mix{k}", sb2, 4) for k in range(LANES)]
        banks = [psA, psB, psC, psL]
        M2 = ("m2gate", "m2gateb", "m2w1", "m2w2", "m2b2")
        o_v = out.rearrange("b (u p) c -> p (b u) c", p=P)
        XT = X[:]

        with nc.Block() as block:
            @block.sync
            def _(sp):
                with sp.Fori(0, NT // LANES) as i:
                    for k in range(LANES):
                        sp.wait_ge(sem(f"done{k}"), i + 2)
                        sp.dma_start(o_v[:, bass.ds(i * (2 * LANES) + 2 * k, 2), :], XN[:, bass.ds(i * (2 * LANES) + 2 * k, 2), :])\
                            .then_inc(sem("out"), 16)
                sp.wait_ge(sem("out"), NT * 16)

            @block.gpsimd
            def _(pool):
                with pool.Fori(0, NT // LANES) as i:
                    for k in range(LANES):
                        ln_pool(pool, f"m{k}", mixes[k]["ln"], 1e-5, i + 1)

            @block.scalar
            def _(act):
                with act.Fori(0, NT // LANES) as i:
                    weave([moe_act(act, i, f"m{k}", mixes[k], banks[k], 4, "m2b1") for k in range(LANES)])

            @block.vector
            def _(dve):
                for k in range(LANES):
                    nc.vector.memset(mixes[k]["g"][:], NEG)
                    last = nc.vector.memset(mixes[k]["rep"][:], NEG)
                last.then_inc(sem("pad"), 1)
                dve.wait_ge(sem("pad"), 1)
                for k in range(LANES):
                    dve.sem_inc(sem(f"done{k}"), 1)
                with dve.Fori(0, NT // LANES) as i:
                    weave([moe_dve(dve, i, f"m{k}", mixes[k], banks[k], XT[:, bass.ds(i * LANES + k, 1)].rearrange("p o j c -> p (o j) c"),
                                          None, f"done{k}", True) for k in range(LANES)])

            @block.tensor
            def _(pe):
                with pe.Fori(0, NT // LANES) as i:
                    weave([moe_pe(pe, i, f"m{k}", mixes[k], banks[k], 4, M2, (sem(f"done{k}"), i + 1)) for k in range(LANES)])


def kernel(**inputs):
    import concourse.bacc as bacc
    from concourse.bass_utils import run_bass_kernel_spmd

    a = {k: np.asarray(v) for k, v in inputs.items()}
    pack = np.zeros((P, NPACK), np.float32)

    def put(name, v):
        r, at, c = COL[name]
        pack[0:r, at:at + c] = np.asarray(v).reshape(r, c)

    def rows(v, n=P):
        return np.tile(np.asarray(v).reshape(1, -1), (n, 1))

    def pairs(v):
        o = np.zeros((P, 4, 2, v.shape[2]), np.float32)
        for e in range(E):
            o[64 * (e % 2):64 * (e % 2) + 64, e // 2, e % 2] = v[e]
        return o

    def pairv(v):
        return v.reshape(4, 2 * 64).T

    p = np.arange(P)
    same = (p[:, None] // TT) == (p[None, :] // TT)
    put("ident", np.eye(P))
    put("triblk", same & (p[:, None] <= p[None, :]))
    put("strictblk", same & (p[:, None] > p[None, :]))
    put("indblk", (p[:, None] // TT) == (p[None, :] // DS) % B4)
    put("tri32", (p[:, None] % TT) <= np.arange(TT)[None, :])
    put("maskb", 0.5 * ((p[:, None] // TT) == np.arange(B4)[None, :]))
    for k in range(NB):
        wi, cw = a["L0_conv_in_proj_w"][k], a["L0_conv_conv_w"][k][:, 0]
        put(f"wzd{k}", np.concatenate([wi[0:DI], wi[DI + XBC:]]).T)
        put(f"wxbc{k}", np.concatenate([wi[DI:DI + XBC].T] * 2))
        taps = np.concatenate([rows(cw[:, 3], 64), rows(cw[:, 2], 64)]), np.concatenate([rows(cw[:, 1], 64), rows(cw[:, 0], 64)])
        put(f"taps{k}", np.concatenate(taps, 1))
        put(f"bias{k}", np.concatenate([np.zeros(DI, np.float32), a["L0_conv_dt_bias"][k], a["L0_conv_conv_b"][k]]))
        put(f"alog{k}", rows(a["L0_conv_A_log"][k]))
        put(f"dskip{k}", rows(a["L0_conv_D"][k]))
        put(f"normw{k}", a["L0_conv_norm_w"][k])
        put(f"wout{k}", np.concatenate([a["L0_conv_out_proj_w"][k].T] * 2, 1))
    put("wr", a["L0_ffn_Wr"]); put("br", a["L0_ffn_br"])
    put("f0w1", a["L0_ffn_W1"].transpose(1, 0, 2)); put("f0w2", pairs(a["L0_ffn_W2"])); put("f0wo", pairs(a["L0_ffn_Wo"]))
    put("f0bo", a["L0_ffn_bo"])
    for l in (1, 2):
        for n, k in (("b", "b"), ("g", "g"), ("be", "be"), ("m", "m"), ("v", "v")):
            put(f"f0{n}{l}", pairv(a[f"L0_ffn_{k}{l}"]))
    put("m1gate", a["L1_ffn_gate_w"]); put("m1gateb", a["L1_ffn_gate_b"]); put("m1w1", a["L1_ffn_W1"].transpose(1, 0, 2))
    put("m1b1", a["L1_ffn_b1"].T); put("m1w2", a["L1_ffn_W2"].transpose(1, 0, 2)); put("m1b2", a["L1_ffn_b2"])
    u, v, bb = ({g: a[f"L2_ffn_{n}_{g}"] for g in "cio"} for n in "UVb")
    put("ugo", np.concatenate([np.concatenate([u["c"], bb["c"][None]]), np.concatenate([u["o"], bb["o"][None]])], 1))
    put("ui", np.concatenate([u["i"], bb["i"][None]]))
    put("vgo", np.concatenate([v["c"], v["o"]], 1)); put("vi", v["i"])
    put("dw", np.tile(a["L3_conv_dw_kernel"].reshape(KT * KT, C).T, (2, 1)))
    for n, k in (("bng", "gamma"), ("bnb", "beta"), ("bnm", "mean"), ("bnv", "var")):
        put(n, np.tile(a[f"L3_conv_bn_{k}"], 2))
    put("wq", a["L3_conv_wq"]); put("wk", a["L3_conv_wk"]); put("wvT", a["L3_conv_wv"].T); put("wo3", a["L3_conv_wo"])
    put("ascale", np.full(P, a["L3_conv_attn_scale"]))
    put("m2gate", a["L3_ffn_router_w"].T); put("m2gateb", np.zeros(E)); put("m2w1", a["L3_ffn_w1"].transpose(1, 0, 2))
    put("m2b1", pairv(a["L3_ffn_b1"])); put("m2w2", pairs(a["L3_ffn_w2"])); put("m2b2", a["L3_ffn_b2"])

    x = a["x"].reshape(J, B4, NT, TT, C).transpose(1, 3, 2, 0, 4).reshape(P, NT, J, C)
    accs = [a[f"L{l}_conv_accumulators"].reshape(NT, 2, 16, C, C).transpose(0, 1, 3, 2, 4).reshape(NT, P, 16, C) for l in (1, 2)]
    arrays = {"x_in": x, "pack_in": pack, "acc1_in": accs[0], "acc2_in": accs[1]}
    arrays = {k: np.ascontiguousarray(v) for k, v in arrays.items()}

    nc = bacc.Bacc("TRN2", target_bir_lowering=False, num_devices=1)
    args = [nc.dram_tensor(k, v.shape, F32, kind="ExternalInput").ap() for k, v in arrays.items()]
    o = nc.dram_tensor("out_x", (B, IMG * IMG, C), F32, kind="ExternalOutput").ap()
    build(nc, *args, o)
    r = run_bass_kernel_spmd(nc, [arrays], core_ids=[0]).results[0]["out_x"]
    return np.asarray(r).reshape(B, IMG, IMG, C)
```

```python
from contextlib import ExitStack

import numpy as np

import concourse.bass as bass
from concourse import mybir

P = 128
B, IMG, C = 8, 32, 64
NT = IMG
TT = IMG
J, B4 = 2, 4
NB, DI, DS, NH, HD = 2, 128, 16, 8, 16
ZD = DI + NH
XBC = DI + 2 * DS
PROJ = ZD + XBC
E = 8
KT = 7
PADI = IMG + KT - 1
LB = 8
NEG = -1.0

F32 = mybir.dt.float32
BF16 = mybir.dt.bfloat16
ALU = mybir.AluOpType
ACT = mybir.ActivationFunctionType
AX = mybir.AxisListType.X


PACK = [
    ("ident", 128, 128), ("triblk", 128, 128), ("strictblk", 128, 128), ("indblk", 128, 128),
    ("tri32", 128, 32), ("maskb", 128, 4),
]
for _b in range(NB):
    PACK += [(f"wzd{_b}", 64, ZD), (f"wxbc{_b}", 128, XBC), (f"taps{_b}", 128, 2 * XBC), 
             (f"alog{_b}", 128, NH), (f"dskip{_b}", 128, NH), (f"normw{_b}", 128, 1), (f"wout{_b}", 128, 2 * C)]
BIASES = [(f"bias{_b}", 1, PROJ) for _b in range(NB)]
PACK += BIASES
FIRST = "wr"
PACK += [("wr", 64, E), ("f0w1", 64, E * 64), ("f0w2", 128, 512), ("f0wo", 128, 512)]
PACK += [(f"f0{_n}{_l}", 128, 4) for _l in (1, 2) for _n in ("b", "g", "be", "m", "v")]
PACK += [("m1gate", 64, E), ("m1w1", 64, E * 128), ("m1b1", 128, 8), ("m1w2", 128, 512)]
RM = 96
PACK += [("ua", 65, RM), ("ub", 65, RM), ("vab", 128, RM)]
PACK += [("dw", 128, KT * KT), ("bng", 128, 1), ("bnb", 128, 1), ("bnm", 128, 1), ("bnv", 128, 1),
         ("wq", 64, 64), ("wk", 64, 64), ("wvT", 64, 64), ("wo3", 64, 64), ("ascale", 128, 1)]
PACK += [("m2gate", 64, E), ("m2w1", 64, E * 64), ("m2b1", 128, 4), ("m2w2", 128, 512)]
LATE_BIASES = [("br", 1, E), ("f0bo", 1, 512), ("m1gateb", 1, E), ("m1b2", 1, 512), ("m2gateb", 1, E), ("m2b2", 1, 512)]
PACK += LATE_BIASES
COL = {}
_at = 0
for _n, _r, _c in PACK:
    COL[_n] = (_r, _at, _c)
    _at += _c
NPACK = _at
NFIRST = COL[FIRST][1]
NBIAS0 = sum(_c for _, _, _c in BIASES)
NBIAS = NBIAS0 + sum(_c for _, _, _c in LATE_BIASES)
BCOL = {}
_at = 0
for _n, _r, _c in BIASES + LATE_BIASES:
    BCOL[_n] = _at
    _at += _c

DVE_A = 12


class Steps:

    def __init__(self, eng, sem, tile, per_tile):
        self.eng, self.sem, self.base, self.per, self.n = eng, sem, tile * per_tile, per_tile, 0

    def did(self, ins):
        ins.then_inc(self.sem, 1)
        self.n += 1

    def wait(self):
        self.eng.wait_ge(self.sem, self.base + self.n)

    def end(self):
        assert self.n == self.per, (self.sem, self.n, self.per)


def bc(ap, axis, n):
    ap = ap.unsqueeze(axis)
    shape = list(ap.shape)
    shape[axis] = n
    return ap.broadcast_to(shape)


def build(nc, x_in, pack_in, acc1_in, acc2_in, out):
    with ExitStack() as ctx:
        def resident(name, *shape):
            return ctx.enter_context(nc.sbuf_tensor(name, list(shape), F32))

        sems = {}
        phase = [""]

        def sem(name):
            if name not in sems:
                sems[name] = nc.alloc_semaphore(name=f"{phase[0]}{name}")
            return sems[name]

        def next_phase():
            nc.all_engine_barrier()
            nc.clear_and_free_semaphores(list(sems.values()))
            nc.all_engine_barrier()
            sems.clear()
            phase[0] += "n_"

        X = resident("X", P, NT, J, C)
        W = resident("W", P, NPACK)
        ident = W[:, COL["ident"][1]:COL["ident"][1] + 128]

        def w(name, c0=0, c1=None):
            r, at, c = COL[name]
            return W[0:r, at + c0:at + (c if c1 is None else c1)]

        def wb(name):
            r, at, c = COL[name]
            return bias3[:, BCOL[name]:BCOL[name] + c]

        bias3 = ctx.enter_context(nc.sbuf_tensor("bias3", [65, NBIAS], BF16))
        ones3 = ctx.enter_context(nc.sbuf_tensor("ones3", [65, P], BF16))
        wpair = resident("wpair", P, NB, 2, XBC)
        aneg = resident("aneg", P, NB, J, NH)
        dhalf = resident("dhalf", P, NB, J, NH)
        wout = resident("wout", P, NB, 2 * C)
        bn0s = resident("bn0s", P, 2, 4)
        bn0b = resident("bn0b", P, 2, 4)
        lua = resident("lua", 65, RM)
        lub = resident("lub", 65, RM)
        lvab = resident("lvab", P, RM)
        wr8 = resident("wr8", 64, E)
        bn3s = resident("bn3s", P, 1)
        bn3b = resident("bn3b", P, 1)
        wqs = resident("wqs", 64, 64)
        wvo = resident("wvo", 64, 64)
        epst = resident("epst", P, 4)
        decay_read = resident("decay_read", P, 1)
        epss = resident("epss", P, J, 2)

        psA = ctx.enter_context(nc.psum_tensor("psA", [P, 2, 512], F32))
        psB = ctx.enter_context(nc.psum_tensor("psB", [P, 2, 512], F32))
        psC = ctx.enter_context(nc.psum_tensor("psC", [P, 2, 512], F32))
        psL = ctx.enter_context(nc.psum_tensor("psL", [P, 2, 512], F32))

        img = resident("img", P, B4, PADI, PADI)
        x6d = nc.dram_tensor("x6d", [B, IMG * IMG, C], F32)
        phase1 = ctx.enter_context(ExitStack())

        def sb(name, *shape):
            return phase1.enter_context(nc.sbuf_tensor(name, list(shape), F32))

        bpart = phase1.enter_context(nc.sbuf_tensor("bpart", [1, 3, NBIAS], BF16))
        brest = sb("brest", 1, NBIAS)
        a_st = sb("a_st", P, J, 6); a_mv = sb("a_mv", P, J, 2); a_rs = sb("a_rs", P, J)
        a_xn = sb("a_xn", P, J, 2, C)
        hb = sb("hb", P, NB, 2, B, TT)
        hh = sb("hh", P, NB, B, 3)
        a_abs = sb("a_abs", P, J, NH); a_rx = sb("a_rx", P, J, NH); a_u = sb("a_u", P, J, NH)
        a_t = sb("a_t", P, 3, J, NH)
        NSER = 7
        a_h0 = sb("a_h0", P, J * NH, NSER); a_h1 = sb("a_h1", P, J * NH, NSER); a_h2 = sb("a_h2", P, J * NH, NSER)
        a_dt = sb("a_dt", P, J, NH); a_a = sb("a_a", P, J, NH);
        a_T = sb("a_T", P, J, PROJ); a_S = sb("a_S", P, J, PROJ)
        a_bc = sb("a_bc", P, J, 2, B4, DS)
        a_xd = sb("a_xd", P, J, DI)
        a_R = sb("a_R", P, J * NH, TT); a_E = sb("a_E", P, J * NH, TT); a_ex = sb("a_ex", P, 3, J, NH)
        a_bct = sb("a_bct", 64, 2, J, P)
        a_xe = sb("a_xe", P, J, NH, HD)
        a_dtm = sb("a_dtm", P, J, NH, B4); a_de = sb("a_de", P, J, NH)
        a_xw = sb("a_xw", P, J, NH, B4, HD)
        a_G = sb("a_G", P, J, TT)
        a_M = sb("a_M", P, J * NH, TT)
        a_yi = sb("a_yi", P, J, DI)
        state = sb("state", 64, NB, J, DI); a_sd = sb("a_sd", 64, J, DI)
        a_y = sb("a_y", P, J, DI); a_sq = sb("a_sq", P, J, DI); a_ss = sb("a_ss", P, J); a_r2 = sb("a_r2", P, J)
        a_yT = sb("a_yT", P, J * P)

        def lnbuf(k):
            return dict(st=sb(f"{k}_st", P, J, 6), mv=sb(f"{k}_mv", P, J, 2), rs=sb(f"{k}_rs", P, J),
                        xn=sb(f"{k}_xn", P, J, C))

        f_ln = lnbuf("f"); f_xT = sb("f_xT", 64, B, TT); f_ft = sb("f_ft", 64, TT); f_fr = sb("f_fr", 64, B4, TT)
        f_w = sb("f_w", P, 5, E); f_s = sb("f_s", P, 4)
        f_h1 = sb("f_h1", P, 4, 256); f_h2 = sb("f_h2", P, 4, 256)
        f_big = sb("f_big", P, J, E, C);
        c_ln = [lnbuf("c1"), lnbuf("c2")]
        c_mx = [sb(f"c_mx{k}", P, 2, J) for k in (0, 1)]
        c_e = [sb(f"c_e{k}", P, J, 2, C) for k in (0, 1)]
        c_eT = [sb(f"c_eT{k}", P, 2, B + 1, 16) for k in (0, 1)]
        c_r = [sb(f"c_r{k}", 64, J, 16) for k in (0, 1)]
        c_q = [sb(f"c_q{k}", 64, B, TT) for k in (0, 1)]
        c_l = [sb(f"c_l{k}", P, J, C) for k in (0, 1)]
        accb = [sb(f"accb{k}", P, 16, C) for k in (0, 1)]
        def moe_bufs(m, make, nch):
            return dict(ln={n: make(f"{m}_{n}", *sh) for n, sh in (("st", (P, J, 6)), ("mv", (P, J, 2)), ("rs", (P, J)), ("xn", (P, J, C)))},
                        xT=make(f"{m}_xT", 64, J * P), g=make(f"{m}_g", P, J, 14), mx=make(f"{m}_mx", P, J), sm=make(f"{m}_sm", P, J),
                        d=make(f"{m}_d", P, J, E), top=make(f"{m}_top", P, J, 8), rep=make(f"{m}_rep", P, J, 8),
                        rest=make(f"{m}_rest", P, J, 14), cw=make(f"{m}_cw", P, J, E), h=make(f"{m}_h", P, nch, 256),
                        big=make(f"{m}_big", P, J, E, C), red=make(f"{m}_red", P, J, C))

        mix1 = moe_bufs("m0", sb, 8)
        r_ln = lnbuf("r"); r_xT = sb("r_xT", 65, B, TT)
        r_wk = sb("r_wk", 64, 96); r_c3 = sb("r_c3", 64, 2, 24); r_tc = sb("r_tc", 64, LB)
        r_h = sb("r_h", P, TT + 1, 2, LB)
        r_hT = sb("r_hT", 64, B, TT)
        p_ln = lnbuf("p")

        pow_m = epst[:, 0:2]
        EPS = {1e-5: 0, 1e-6: 1}

        block_ctx = nc.Block()
        block = block_ctx.__enter__()


        def settle(eng):
            eng.sem_inc(sem("apart"), 1)

        def ln_vector(dve, k, buf, src, i1, s0, dup=False, out=None, gap=1):
            yield s0
            settle(dve)
            for j in range(J):
                last = nc.vector.bn_stats(buf["st"][:, j, :], src[:, j, :])
            last.then_inc(sem(k + "_stats"), 1)
            dve.wait_ge(sem(k + "_stats"), i1)
            settle(dve)
            for j in range(J):
                last = nc.vector.bn_aggr(buf["mv"][:, j, :], buf["st"][:, j, :])
            last.then_inc(sem(k + "_var"), 1)
            yield s0 + gap
            dve.wait_ge(sem(k + "_rstd"), i1)
            for j in range(J):
                o = buf["xn"][:, j] if out is None else out[:, j]
                s = src[:, j, :]
                if dup:
                    s = bc(s, 1, 2)
                last = nc.vector.tensor_scalar(o, s, buf["mv"][:, j, 0:1], buf["rs"][:, j:j + 1], ALU.subtract, ALU.mult)
            last.then_inc(sem(k + "_xn"), 1)

        def ln_pool(pool, k, buf, eps, i1):
            pool.wait_ge(sem(k + "_var"), i1)
            nc.gpsimd.tensor_tensor(buf["rs"][:, :], buf["mv"][:, :, 1], epss[:, :, EPS[eps]], ALU.add).then_inc(sem(k + "_vare"), 1)
            pool.wait_ge(sem(k + "_vare"), i1)
            nc.gpsimd.tensor_tensor(buf["rs"][:, :], buf["rs"][:, :], pow_m, ALU.pow).then_inc(sem(k + "_rstd"), 1)

        a_ln = dict(st=a_st, mv=a_mv, rs=a_rs)
        EXC, EXS, EXT = 0, 1, 2

        def mamba_pe(pe, i):
            for k in range(NB):
                n = i * 2 + (k + 1)
                s0 = 16 * k
                if k == 0:
                    pe.wait_ge(sem("a_xn"), i + 1)
                    pe.wait_ge(sem("x1_done"), i + 1)
                    for j in range(J):
                        last = nc.tensor.transpose(psA[:, 0, j * P:(j + 1) * P], a_xn[:, j].rearrange("p d c -> p (d c)"), ident)
                    last.then_inc(sem("a_feed"), 1)
                yield s0 + 2
                pe.wait_ge(sem("a_htop"), n)
                pe.wait_ge(sem("a_hbot"), n)
                pe.wait_ge(sem("a_halo"), n)
                pe.wait_ge(sem("a_hh"), n)
                for j in range(J):
                    if j:
                        yield s0 + 3
                    hfl = hb[:, k].rearrange("p s b t -> p s (b t)")
                    nc.tensor.matmul(psA[:, j, 0:PROJ], ones3[:], wb(f"bias{k}"), start=True, stop=False)
                    nc.tensor.matmul(psA[:, j, 0:ZD], hfl[0:64, 0, j * P:(j + 1) * P], w(f"wzd{k}"), start=False, stop=False)
                    nc.tensor.matmul(psA[:, j, ZD:PROJ], hfl[:, 0, j * P:(j + 1) * P], wpair[:, k, 0, :], start=False, stop=False)
                    last = nc.tensor.matmul(psA[:, j, ZD:PROJ], hfl[:, 1, j * P:(j + 1) * P], wpair[:, k, 1, :], start=False, stop=True)
                last.then_inc(sem("a_zx"), 1)
                yield s0 + 6
                pe.wait_ge(sem("a_S"), n)
                pe.wait_ge(sem("a_bc"), n)
                for j in range(J):
                    last = nc.tensor.transpose(psA[:, 1, j * P:(j + 1) * P], a_bc[:, j].rearrange("p q b n -> p (q b n)"), ident)
                last.then_inc(sem("a_bct"), 1)
                yield s0 + (7, 6)[k]
                pe.wait_ge(sem("a_R"), n)
                nc.tensor.matmul(psA[:, 0, :], w("strictblk"), a_R[:].rearrange("p h t -> p (h t)"), start=True, stop=True)\
                    .then_inc(sem("a_seg"), 1)
                yield s0 + 8
                pe.wait_ge(sem("a_bcts"), n)
                av = a_a[:].rearrange("p j h -> p (j h)")
                nc.tensor.matmul(psA[:, 1, 0:16], w("triblk"), av, start=True, stop=True)
                nc.tensor.matmul(psA[:, 1, 16:32], w("strictblk"), av, start=True, stop=True)
                nc.tensor.matmul(psA[:, 1, 32:48], w("indblk"), av, start=True, stop=True).then_inc(sem("a_sum"), 1)
                yield s0 + 9
                pe.wait_ge(sem("a_ex"), n)
                for j in range(J):
                    last = nc.tensor.matmul(psA[:, 0, j * P:(j + 1) * P], a_bct[:, 0, j], a_bct[:, 1, j], start=True, stop=True)
                last.then_inc(sem("a_G"), 1)
                for j in range(J):
                    last = nc.tensor.matmul(psA[:, 1, j * P:(j + 1) * P], a_bct[:, 1, j], state[:, k, j], start=True, stop=True)
                last.then_inc(sem("a_off"), 1)
                yield s0 + 10
                pe.wait_ge(sem("a_xe"), n)
                pe.wait_ge(sem("a_Gm"), n)
                for j in range(J):
                    last = nc.tensor.matmul(psA[0:64, 0, j * P:(j + 1) * P], a_bc[:, j, 0].rearrange("p b n -> p (b n)"),
                                            a_xe[:, j].rearrange("p h d -> p (h d)"), start=True, stop=True)
                last.then_inc(sem("a_st"), 1)
                yield s0 + 11
                pe.wait_ge(sem("a_M"), n)
                pe.wait_ge(sem("a_xw"), n)
                pe.wait_ge(sem("a_yo"), n)
                for j in range(J):
                    if j:
                        yield s0 + (13, 12)[k]
                    for h in range(NH):
                        last = nc.tensor.matmul(psA[0:TT, j, h * B4 * HD:(h + 1) * B4 * HD], a_M[:, j * NH + h],
                                                a_xw[:, j, h].rearrange("p b d -> p (b d)"), start=True, stop=True)
                last.then_inc(sem("a_Y"), 1)
                yield s0 + 15
                pe.wait_ge(sem("a_yn"), n)
                for j in range(J):
                    last = nc.tensor.transpose(psA[:, 0, j * P:(j + 1) * P], a_y[:, j], ident)
                last.then_inc(sem("a_yT"), 1)
                yield s0 + 16
                pe.wait_ge(sem("a_yTs"), n)
                if k == 0:
                    nc.tensor.matmul(psA[:, 1, 0:256], wout[:, k], a_yT[:], start=True, stop=True).then_inc(sem("a_feed"), 1)
                else:
                    for j in range(J):
                        last = nc.tensor.matmul(psA[:, 1, j * C:(j + 1) * C], a_yT[:, j * P:(j + 1) * P], wout[:, k, 0:C],
                                                start=True, stop=True)
                    last.then_inc(sem("a_mo"), 1)
                yield s0 + 16

        def mamba_act(act, i):
            for k in range(NB):
                n = i * 2 + (k + 1)
                s0 = 16 * k
                yield s0 + 1
                act.wait_ge(sem("a_feed"), n)
                fd = psA[0:64, k, 0:256].rearrange("p (b t) -> p b t", b=B)
                nc.scalar.activation(hb[0:64, k, 0], fd, ACT.Copy)
                nc.scalar.activation(hb[0:64, k, 1, :, 2:TT], fd[:, :, 0:TT - 2], ACT.Copy).then_inc(sem("a_htop"), 1)
                yield s0 + 4
                act.wait_ge(sem("a_rx"), n)
                nc.scalar.activation(a_u[:], a_abs[:], ACT.Exp).then_inc(sem("a_u"), 1)
                nc.scalar.activation(a_T[:], psA[:, :, 0:PROJ], ACT.Tanh, scale=0.5).then_inc(sem("a_T"), 1)
                yield s0 + (7, 6)[k]
                act.wait_ge(sem("a_bct"), n)
                for q in range(2):
                    last = nc.scalar.activation(a_bct[:, q].rearrange("p j t -> p (j t)"), psA[64 * q:64 * q + 64, 1, 0:2 * P], ACT.Copy)
                last.then_inc(sem("a_bcts"), 1)
                yield s0 + (8, 7.5)[k]
                act.wait_ge(sem("a_seg"), n)
                nc.scalar.activation(a_E[:].rearrange("p h t -> p (h t)"), psA[:, 0, :], ACT.Exp)
                act.wait_ge(sem("a_sum"), n)
                nc.scalar.activation(a_ex[:].rearrange("p s j h -> p (s j h)"), psA[:, 1, 0:48], ACT.Exp).then_inc(sem("a_ex"), 1)
                yield s0 + (13, 12)[k]
                act.wait_ge(sem("a_Y"), n)
                for b in range(B4):
                    last = nc.scalar.activation(a_yi[TT * b:TT * b + TT].rearrange("p j (h d) -> p (j h) d", h=NH),
                                                psA[0:TT].rearrange("p j (h b d) -> p (j h) b d", h=NH, b=B4)[:, :, b], ACT.Copy)
                last.then_inc(sem("a_yi"), 1)
                yield s0 + 14
                act.wait_ge(sem("a_y"), n)
                for j in range(J):
                    last = nc.scalar.activation(a_sq[:, j], a_y[:, j], ACT.Square, accum_out=a_ss[:, j:j + 1])
                last.then_inc(sem("a_ss"), 1)
                yield s0 + (15.5, 15)[k]
                act.wait_ge(sem("a_yT"), n)
                nc.scalar.activation(a_yT[:], psA[:, 0, 0:256], ACT.Copy).then_inc(sem("a_yTs"), 1)
                yield s0 + 16

        def norm_dve(dve, i):
            yield 28
            if not (isinstance(i, int) and i == 0):
                dve.wait_ge(sem("a_feed"), i * 2)
            yield from ln_vector(dve, "a", a_ln, X[:, i], i + 1, 27.5, gap=1.5, dup=True, out=a_xn)

        def mamba_dve(dve, i):
            for k in range(NB):
                n = i * 2 + (k + 1)
                s0 = 16 * k
                st = Steps(dve, sem("a_steps"), i * 2 + k, DVE_A)
                v = nc.vector
                yield s0 + 1
                dve.wait_ge(sem("a_feed"), n)
                dve.wait_ge(sem("a_halo"), n)
                fd = psA[:, k, 0:256].rearrange("p (b t) -> p b t", b=B)
                v.tensor_copy(hb[64:128, k, 0, :, 1:TT], fd[64:128, :, 0:TT - 1])
                v.tensor_copy(hb[64:128, k, 1, :, 3:TT], fd[64:128, :, 0:TT - 3]).then_inc(sem("a_hbot"), 1)
                dve.wait_ge(sem("a_htop"), n)
                v.tensor_copy(hh[:, k], fd[:, :, TT - 3:TT]).then_inc(sem("a_hh"), 1)
                yield s0 + 4
                dve.wait_ge(sem("a_zx"), n)
                raw = psA[:, :, DI:ZD]
                st.did(v.tensor_scalar(a_rx[:], raw, 0.0, None, ALU.max)); st.wait()
                v.scalar_tensor_tensor(a_abs[:], a_rx[:], -2.0, raw, ALU.mult, ALU.add).then_inc(sem("a_rx"), 1)
                dve.wait_ge(sem("a_hh"), n)
                v.tensor_copy(hb[64:128, k, 0, :, 0:1], hh[64:128, k, :, 2:3])
                v.tensor_copy(hb[0:64, k, 1, :, 0:2], hh[0:64, k, :, 1:3])
                v.tensor_copy(hb[64:128, k, 1, :, 0:3], hh[64:128, k, :, 0:3]).then_inc(sem("a_halo"), 1)
                yield s0 + (5, 4.5)[k]
                dve.wait_ge(sem("a_T"), n)
                v.scalar_tensor_tensor(a_S[:], a_T[:], 1.0, psA[:, :, 0:PROJ], ALU.add, ALU.mult).then_inc(sem("a_S"), 1)
                dve.wait_ge(sem("a_u"), n)
                s_, pq = a_t[:, 0], a_t[:, 1]
                st.did(v.tensor_scalar(pq, a_u[:], 2.0, None, ALU.add)); st.wait()
                st.did(v.reciprocal(a_t[:, 2], pq)); st.wait()
                st.did(v.tensor_tensor(s_, a_u[:], a_t[:, 2], ALU.mult)); st.wait()
                s1 = s_.rearrange("p j h -> p (j h)")
                st.did(v.tensor_tensor(a_h0[:, :, 1:], bc(s1, 2, NSER - 1), bc(s1, 2, NSER - 1), ALU.mult)); st.wait()
                yield s0 + (6, 5.5)[k]
                flat = lambda t: t[:].rearrange("p a n -> p (a n)")
                st.did(v.tensor_tensor_scan(flat(a_h2), flat(a_h0), flat(a_h1), 0.0, ALU.mult, ALU.add)); st.wait()
                st.did(v.tensor_tensor(pq.rearrange("p j h -> p (j h)"), a_h2[:, :, NSER - 1], s1, ALU.mult)); st.wait()
                st.did(v.scalar_tensor_tensor(a_dt[:], pq, 2.0, a_rx[:], ALU.mult, ALU.add)); st.wait()
                st.did(v.tensor_tensor(a_a[:], a_dt[:], aneg[:, k], ALU.mult)); st.wait()
                v.tensor_tensor(a_dtm[:], bc(a_dt[:], 3, B4), bc(bc(w("maskb"), 1, NH), 1, J), ALU.mult)
                v.tensor_tensor(a_R[:], bc(w("tri32"), 1, J * NH), bc(a_a[:].rearrange("p j h -> p (j h)"), 2, TT), ALU.mult)\
                    .then_inc(sem("a_R"), 1)
                yield s0 + 9
                dve.wait_ge(sem("a_S"), n)
                dve.wait_ge(sem("a_ex"), n)
                xs = a_S[:, :, ZD:ZD + DI].rearrange("p j (h d) -> p j h d", h=NH)
                st.did(v.scalar_tensor_tensor(a_de[:], a_dt[:], 0.5, a_ex[:, EXS], ALU.mult, ALU.mult)); st.wait()
                v.tensor_tensor(a_xe[:], xs, bc(a_de[:], 3, HD), ALU.mult).then_inc(sem("a_xe"), 1)
                yield s0 + 10
                dve.wait_ge(sem("a_G"), n)
                for b in range(B4):
                    r = slice(TT * b, TT * b + TT)
                    last = v.tensor_tensor(a_G[r], psA[r, 0, 0:2 * P].rearrange("p (j t) -> p j t", j=J)[:, :, TT * b:TT * b + TT], bc(w("tri32")[r], 1, J), ALU.mult)
                last.then_inc(sem("a_Gm"), 1)
                dve.wait_ge(sem("a_Gm"), n)
                v.tensor_tensor(a_M[:].rearrange("p (j h) t -> p j h t", j=J), a_E[:].rearrange("p (j h) t -> p j h t", j=J),
                                bc(a_G[:], 2, NH), ALU.mult).then_inc(sem("a_M"), 1)
                yield s0 + 11
                dve.wait_ge(sem("a_off"), n)
                yv = a_y[:].rearrange("p j (h d) -> p j h d", h=NH)
                v.tensor_tensor(yv, psA[:, 1, 0:256].rearrange("p (j h d) -> p j h d", j=J, h=NH), bc(a_ex[:, EXC], 3, HD), ALU.mult)
                dve.wait_ge(sem("a_st"), n)
                dve.wait_ge(sem("a_sd"), n)
                v.tensor_tensor(state[:, k], a_sd[:], psA[0:64, 0, 0:256].rearrange("p (j d) -> p j d", j=J), ALU.add).then_inc(sem("a_yo"), 1)
                yield s0 + (12.5, 12)[k]
                dve.wait_ge(sem("a_yo"), n)
                dve.wait_ge(sem("a_xd"), n)
                yf = a_y[:].rearrange("p j d -> p (j d)")
                st.did(v.tensor_tensor(yf, yf, a_xd[:].rearrange("p j d -> p (j d)"), ALU.add)); st.wait()
                yield s0 + 13
                dve.wait_ge(sem("a_yi"), n)
                st.did(v.tensor_tensor(yf, yf, a_yi[:].rearrange("p j d -> p (j d)"), ALU.add)); st.wait()
                v.tensor_tensor(a_y[:], a_y[:], a_S[:, :, 0:DI], ALU.mult).then_inc(sem("a_y"), 1)
                yield s0 + 15
                dve.wait_ge(sem("a_r2"), n)
                for j in range(J):
                    last = v.tensor_scalar(a_y[:, j], a_y[:, j], a_r2[:, j:j + 1], None, ALU.mult)
                last.then_inc(sem("a_yn"), 1)
                st.end()
                yield s0 + 17
            dve.wait_ge(sem("a_mo"), i + 1)
            nc.vector.tensor_tensor(X[:, i], X[:, i], psA[:, 1, 0:P].rearrange("p (j c) -> p j c", j=J), ALU.add)\
                .then_inc(sem("x1_done"), 1)

        def mamba_pool(pool, i):
            for k in range(NB):
                n = i * 2 + (k + 1)
                s0 = 16 * k
                g = nc.gpsimd
                yield s0 + (5, 4.5)[k]
                pool.wait_ge(sem("a_S"), n)
                for j in range(J):
                    last = g.tensor_tensor(a_bc[:, j], bc(bc(w("maskb"), 1, 2), 3, DS),
                                           bc(a_S[:, j, ZD + DI:PROJ].rearrange("p (q n) -> p q n", q=2), 2, B4), ALU.mult)
                last.then_inc(sem("a_bc"), 1)
                yield s0 + (7, 6)[k]
                pool.wait_ge(sem("a_R"), n)
                xs = a_S[:, :, ZD:ZD + DI].rearrange("p j (h d) -> p j h d", h=NH)
                for j in range(J):
                    last = g.tensor_tensor(a_xw[:, j], bc(xs[:, j], 2, B4), bc(a_dtm[:, j], 3, HD), ALU.mult)
                last.then_inc(sem("a_xw"), 1)
                yield s0 + 8
                pool.wait_ge(sem("a_ex"), n)
                g.tensor_tensor(a_sd[:].rearrange("p j (h d) -> p j h d", h=NH), state[:, k].rearrange("p j (h d) -> p j h d", h=NH),
                                bc(a_ex[0:64, EXT], 3, HD), ALU.mult).then_inc(sem("a_sd"), 1)
                g.tensor_tensor(a_xd[:].rearrange("p j (h d) -> p j h d", h=NH), xs, bc(dhalf[:, k], 3, HD), ALU.mult)\
                    .then_inc(sem("a_xd"), 1)
                yield s0 + 14
                pool.wait_ge(sem("a_ss"), n)
                settle(pool)
                g.tensor_scalar(a_r2[:], a_ss[:], 1.0 / DI, 4e-5, ALU.mult, ALU.add).then_inc(sem("a_r2e"), 1)
                pool.wait_ge(sem("a_r2e"), n)
                g.tensor_tensor(a_r2[:], a_r2[:], pow_m, ALU.pow).then_inc(sem("a_r2"), 1)

        def ffn0_pe(pe, i):
            i1 = i + 1
            yield 1
            pe.wait_ge(sem("f_xn"), i1)
            pe.wait_ge(sem("x3_done"), i1)
            settle(pe)
            for j in range(J):
                last = nc.tensor.transpose(psB[0:64, 0, j * P:(j + 1) * P], f_ln["xn"][:, j], ident)
            last.then_inc(sem("f_xT"), 1)
            yield 4
            pe.wait_ge(sem("f_xTs"), i1)
            for q in range(4):
                yield 4 + q // 2
                nc.tensor.matmul(psB[:, q // 2, (q % 2) * 256:(q % 2 + 1) * 256], w("f0w1", q * P, (q + 1) * P),
                                 f_xT[:].rearrange("p b t -> p (b t)"), start=True, stop=True).then_inc(sem("f_mm1"), 1)
            for q in range(4):
                yield 13 + q // 2
                pe.wait_ge(sem("f_h1"), i1)
                nc.tensor.matmul(psB[:, q // 2, (q % 2) * 256:(q % 2 + 1) * 256], w("f0w2", q * P, (q + 1) * P), f_h1[:, q],
                                 start=True, stop=True).then_inc(sem("f_mm2"), 1)
            yield 16
            pe.wait_ge(sem("f_feat"), i1)
            pe.wait_ge(sem("f_h2"), i1)
            nc.tensor.matmul(psB[:, 0, 0:E], ones3[:], wb("br"), start=True, stop=False)
            nc.tensor.matmul(psB[:, 0, 0:E], f_fr[:].rearrange("p b t -> p (b t)"), wr8[:], start=False, stop=True).then_inc(sem("f_lg"), 1)
            yield 19.5
            pe.wait_ge(sem("f_w"), i1)
            for j in range(J):
                nc.tensor.matmul(psB[:, j, :], ones3[:], wb("f0bo"), start=True, stop=False)
                for q in range(4):
                    yield 19.5 + j
                    last = nc.tensor.matmul(psB[:, j, q * P:(q + 1) * P], f_h2[:, q, j * P:(j + 1) * P], w("f0wo", q * P, (q + 1) * P),
                                            start=False, stop=(q == 3))
            last.then_inc(sem("f_y"), 1)

        def ffn0_act(act, i):
            i1 = i + 1
            yield 3
            act.wait_ge(sem("f_xT"), i1)
            nc.scalar.activation(f_xT[:].rearrange("p b t -> p (b t)"), psB[0:64, 0, 0:256], ACT.Copy).then_inc(sem("f_xTs"), 1)
            yield 5
            act.wait_ge(sem("f_mm1"), i * 4 + 4)
            for q in range(4):
                last = nc.scalar.activation(f_h1[:, q], psB[:, q // 2, (q % 2) * 256:(q % 2 + 1) * 256], ACT.Relu,
                                            bias=bn0b[:, 0, q:q + 1], scale=bn0s[:, 0, q:q + 1])
            last.then_inc(sem("f_h1"), 1)
            yield 15
            act.wait_ge(sem("f_mm2"), i * 4 + 4)
            for q in range(4):
                last = nc.scalar.activation(f_h2[:, q], psB[:, q // 2, (q % 2) * 256:(q % 2 + 1) * 256], ACT.Relu,
                                            bias=bn0b[:, 1, q:q + 1], scale=bn0s[:, 1, q:q + 1])
            last.then_inc(sem("f_h2"), 1)
            yield 16.5
            act.wait_ge(sem("f_ld"), i1)
            nc.scalar.activation(f_w[:, 1], f_w[:, 0], ACT.Exp, accum_out=f_s[:, 1:2]).then_inc(sem("f_le"), 1)

        def ffn0_dve(dve, i):
            i1 = i + 1
            v = nc.vector
            dve.wait_ge(sem("x1_done"), i + 2)
            yield from ln_vector(dve, "f", f_ln, X[:, i], i1, 0)
            yield 4
            dve.wait_ge(sem("f_xTs"), i1)
            st = Steps(dve, sem("f_steps"), i, 3)
            st.did(v.tensor_reduce(f_ft[:], f_xT[:].rearrange("p b t -> p t b"), AX, ALU.add)); st.wait()
            v.tensor_copy(f_fr[:], bc(f_ft[:], 1, B4)).then_inc(sem("f_feat"), 1)
            yield 16.5
            dve.wait_ge(sem("f_lg"), i1)
            st.did(v.tensor_reduce(f_s[:, 0:1], psB[:, 0, 0:E], AX, ALU.max)); st.wait()
            v.tensor_scalar(f_w[:, 0], psB[:, 0, 0:E], f_s[:, 0:1], None, ALU.subtract).then_inc(sem("f_ld"), 1)
            dve.wait_ge(sem("f_le"), i1)
            st.did(v.reciprocal(f_s[:, 2:3], f_s[:, 1:2])); st.wait()
            v.tensor_scalar(f_w[:, 2], f_w[:, 1], f_s[:, 2:3], None, ALU.mult).then_inc(sem("f_w"), 1)
            yield 23
            dve.wait_ge(sem("f_y"), i1)
            v.tensor_tensor(f_big[:], psB[:].rearrange("p j (e c) -> p j e c", e=E), bc(bc(f_w[:, 2], 1, J), 3, C), ALU.mult)\
                .then_inc(sem("f_big"), 1)
            st.end()

        def experts_pool(pool, i, k, big, s0, done):
            g = nc.gpsimd
            yield s0
            pool.wait_ge(sem(k + "_big"), i + 1)
            st = Steps(pool, sem(k + "_halves"), i, 3)
            for n in (4, 2, 1):
                st.did(g.tensor_tensor(big[:, :, 0:n], big[:, :, 0:n], big[:, :, n:2 * n], ALU.add)); st.wait()
            st.end()
            g.tensor_tensor(X[:, i], X[:, i], big[:, :, 0], ALU.add).then_inc(sem(done), 1)

        def prod_pe(pe, i, k, ps, s0):
            i1, c = i + 1, f"c{k}"
            yield s0 + 3
            pe.wait_ge(sem(c + "_e"), i1)
            if k == 1:
                pe.wait_ge(sem("x4_done"), i + 2)
            else:
                pe.wait_ge(sem("x2_done"), i1)
            for j in range(J):
                last = nc.tensor.transpose(ps[:, 0, j * P:(j + 1) * P], c_e[k][:, j].rearrange("p d c -> p (d c)"), ident)
            last.then_inc(sem(c + "_et"), 1)
            yield s0 + 5
            pe.wait_ge(sem(c + "_ets"), i1)
            pe.wait_ge(sem(c + "_acc"), i * 16 + 16)
            settle(pe)
            for t in range(16):
                if t % 8 == 0:
                    yield s0 + (5 + t // 8 * (1 + k)) + (0, 0.5)[k]
                last = nc.tensor.matmul(ps[0:64, 0, 0:288].rearrange("p (h b t) -> p h b t", h=2, t=16)[:, :, :, t],
                                        accb[k][:, t], c_eT[k][:, :, :, t], start=True, stop=True)
            last.then_inc(sem(c + "_mm"), 1)
            yield (31, 32)[1 - k]
            pe.wait_ge(sem(c + "_q"), i1)
            settle(pe)
            for j in range(J):
                last = nc.tensor.transpose(ps[:, 0, j * C:(j + 1) * C],
                                           c_q[k][:, j * B4:(j + 1) * B4].rearrange("p b t -> p (b t)"), ident[0:64, 0:64])
            last.then_inc(sem(c + "_qT"), 1)

        def prod_act(act, i, k, ps, s0):
            i1, c = i + 1, f"c{k}"
            yield s0 + 2
            act.wait_ge(sem(c + "_mx"), i1)
            for j in range(J):
                last = nc.scalar.activation(c_e[k][:, j], bc(c_ln[k]["xn"][:, j], 1, 2), ACT.Exp, bias=c_mx[k][:, 1, j:j + 1])
            last.then_inc(sem(c + "_e"), 1)
            yield s0 + 4
            act.wait_ge(sem(c + "_et"), i1)
            for h in range(2):
                r = slice(64 * h, 64 * h + 64)
                last = nc.scalar.activation(c_eT[k][r, h, 0:B], ps[r, 0, 0:256].rearrange("p (b h t) -> p h b t", h=2, t=16)[:, h], ACT.Copy)
            last.then_inc(sem(c + "_ets"), 1)
            yield 33
            act.wait_ge(sem(c + "_qT"), i1)
            nc.scalar.activation(c_l[k][:].rearrange("p j c -> p (j c)"), ps[:, 0, 0:P], ACT.Ln).then_inc(sem(c + "_l"), 1)

        def prod_dve(dve, i, k, ps, s0, before, done):
            i1, c = i + 1, f"c{k}"
            v = nc.vector
            yield s0
            dve.wait_ge(sem(before), i + (1 + k))
            yield from ln_vector(dve, c, c_ln[k], X[:, i], i1, s0)
            dve.wait_ge(sem(c + "_xn"), i1)
            st = Steps(dve, sem(c + "_steps"), i, 2)
            st.did(v.tensor_reduce(c_mx[k][:, 0], c_ln[k]["xn"][:], AX, ALU.max)); st.wait()
            v.tensor_scalar(c_mx[k][:, 1], c_mx[k][:, 0], -1.0, None, ALU.mult).then_inc(sem(c + "_mx"), 1)
            yield s0 + (7 + 2 * k)
            dve.wait_ge(sem(c + "_mm"), i1)
            pv = ps[0:64, 0, 0:288].rearrange("p (h b t) -> p h b t", h=2, b=B + 1)
            st.did(v.reciprocal(c_r[k][:], pv[:, :, B])); st.wait()
            st.end()
            v.tensor_tensor(c_q[k][:].rearrange("p b (h t) -> p h b t", h=2), pv[:, :, 0:B], bc(c_r[k][:], 2, B), ALU.mult)\
                .then_inc(sem(c + "_q"), 1)
            yield 34
            dve.wait_ge(sem(c + "_l"), i1)
            for j in range(J):
                last = v.scalar_tensor_tensor(X[:, i, j], c_l[k][:, j], c_mx[k][:, 0, j:j + 1], X[:, i, j], ALU.add, ALU.add)
            last.then_inc(sem(done), 1)

        def x6_store(sp, i):
            yield 24
            sp.wait_ge(sem("x6_done"), i + 1)
            for j in range(J):
                sp.dma_start(x6d[j * B4:(j + 1) * B4, bass.ts(i, TT), :], X[:, i, j]).then_inc(sem("x6_out"), 16)

        def acc_load(sp, i, k, src):
            sp.dma_start(accb[k][:], src[i]).then_inc(sem(f"c{k}_acc"), 16)

        def acc_next(sp, i, k, src):
            yield 28.5
            if not (isinstance(i, int) and i == NT - 1):
                sp.wait_ge(sem(f"c{k}_mm"), i + 1)
                acc_load(sp, i + 1, k, src)

        def moe_pe(pe, i, m, u, ps, nch, names, before, s0=0):
            i1 = i + 1
            gate, gateb, w1, w2, b2 = names
            hw = 512 // nch
            yield 4
            pe.wait_ge(sem(m + "_xn"), i1)
            pe.wait_ge(*before)
            settle(pe)
            for j in range(J):
                last = nc.tensor.transpose(ps[0:64, 0, j * P:(j + 1) * P], u["ln"]["xn"][:, j], ident)
            last.then_inc(sem(m + "_xT"), 1)
            yield 6
            pe.wait_ge(sem(m + "_xTs"), i1)
            for j in range(J):
                nc.tensor.matmul(ps[:, 1, j * E:(j + 1) * E], ones3[:], wb(gateb), start=True, stop=False)
                last = nc.tensor.matmul(ps[:, 1, j * E:(j + 1) * E], u["xT"][:, j * P:(j + 1) * P], w(gate), start=False, stop=True)
            last.then_inc(sem(m + "_lg"), 1)
            yield s0 + 7
            pe.wait_ge(sem(m + "_ld"), i1)
            for r in range(nch // 4):
                yield s0 + 7 + 4 * r
                if r:
                    pe.wait_ge(sem(m + "_h"), i * (nch // 4) + r)
                for q in range(4):
                    yield s0 + 7 + 4 * r + q // 2
                    e = r * 4 + q
                    last = nc.tensor.matmul(ps[:, q // 2, (q % 2) * 256:(q % 2 + 1) * 256], w(w1, e * P, (e + 1) * P), u["xT"][:],
                                            start=True, stop=True)
                last.then_inc(sem(m + "_mm1"), 1)
            yield s0 + 13.5
            pe.wait_ge(sem(m + "_h"), (i + 1) * (nch // 4))
            for j in range(J):
                nc.tensor.matmul(ps[:, j, :], ones3[:], wb(b2), start=True, stop=False)
                for e in range(nch):
                    if e * 2 % nch == 0:
                        yield s0 + 13.5 + 2 * j + e * 2 // nch
                    last = nc.tensor.matmul(ps[:, j, e * hw:(e + 1) * hw], u["h"][:, e, j * P:(j + 1) * P], w(w2, e * hw, (e + 1) * hw),
                                            start=False, stop=(e == nch - 1))
            last.then_inc(sem(m + "_y"), 1)

        def moe_act(act, i, m, u, ps, nch, b1, s0=0):
            i1 = i + 1
            yield 5
            act.wait_ge(sem(m + "_xT"), i1)
            nc.scalar.activation(u["xT"][:], ps[0:64, 0, 0:256], ACT.Copy).then_inc(sem(m + "_xTs"), 1)
            yield 7
            act.wait_ge(sem(m + "_ld"), i1)
            nc.scalar.activation(u["g"][:, :, 0:E], u["d"][:], ACT.Exp).then_inc(sem(m + "_p"), 1)
            for r in range(nch // 4):
                yield s0 + 10 + 3 * r
                act.wait_ge(sem(m + "_mm1"), i * (nch // 4) + (r + 1))
                for q in range(4):
                    e = r * 4 + q
                    last = nc.scalar.activation(u["h"][:, e], ps[:, q // 2, (q % 2) * 256:(q % 2 + 1) * 256], ACT.Gelu, bias=w(b1, e, e + 1))
                last.then_inc(sem(m + "_h"), 1)

        def moe_dve(dve, i, m, u, ps, x, before, done, renorm, s0=0):
            i1 = i + 1
            v = nc.vector
            yield 2
            if before:
                dve.wait_ge(*before)
            yield from ln_vector(dve, m, u["ln"], x, i1, 2)
            yield 6
            dve.wait_ge(sem(m + "_lg"), i1)
            st = Steps(dve, sem(m + "_steps"), i, 15 if renorm else 8)
            lg = ps[:, 1, 0:J * E].rearrange("p (j e) -> p j e", j=J)
            st.did(v.tensor_reduce(u["mx"][:], lg, AX, ALU.max)); st.wait()
            v.tensor_tensor(u["d"][:], lg, bc(u["mx"][:], 2, E), ALU.subtract).then_inc(sem(m + "_ld"), 1)
            yield s0 + 8
            dve.wait_ge(sem(m + "_p"), i1)
            p_ = u["g"][:, :, 0:E]
            st.did(v.tensor_reduce(u["sm"][:], p_, AX, ALU.add)); st.wait()
            st.did(v.reciprocal(u["sm"][:], u["sm"][:])); st.wait()
            st.did(v.tensor_tensor(p_, p_, bc(u["sm"][:], 2, E), ALU.mult)); st.wait()
            settle(dve)
            for j in range(J):
                last = v.max(u["top"][:, j], u["g"][:, j])
            st.did(last); st.wait()
            st.did(v.tensor_copy(u["rep"][:, :, 0:2], u["top"][:, :, 0:2])); st.wait()
            settle(dve)
            for j in range(J):
                last = v.match_replace(u["rest"][:, j], u["rep"][:, j], u["g"][:, j], 0.0)
            st.did(last); st.wait()
            st.did(v.tensor_tensor(u["cw"][:], p_, u["rest"][:, :, 0:E], ALU.subtract)); st.wait()
            if renorm:
                st.did(v.tensor_reduce(u["sm"][:], u["cw"][:], AX, ALU.add)); st.wait()
                st.did(v.tensor_scalar(u["sm"][:], u["sm"][:], 1e-12, None, ALU.max)); st.wait()
                st.did(v.reciprocal(u["mx"][:], u["sm"][:])); st.wait()
                st.did(v.tensor_tensor(u["cw"][:], u["cw"][:], bc(u["mx"][:], 2, E), ALU.mult)); st.wait()
            yield s0 + 19
            dve.wait_ge(sem(m + "_y"), i1)
            big = v.tensor_tensor(u["big"][:], ps[:].rearrange("p j (e c) -> p j e c", e=E), bc(u["cw"][:], 3, C), ALU.mult)
            if not renorm:
                big.then_inc(sem(m + "_big"), 1)
                st.end()
                return
            st.did(big); st.wait()
            yield s0 + 20
            st.did(v.tensor_reduce(u["red"][:], u["big"][:].rearrange("p j e c -> p j c e"), AX, ALU.add)); st.wait()
            st.did(v.tensor_tensor(u["red"][:], u["red"][:], u["ln"]["xn"][:], ALU.add)); st.wait()
            st.end()
            v.tensor_tensor(x, x, u["red"][:], ALU.add).then_inc(sem(done), 1)

        def xproj_pe(pe, i, mixed):
            yield 21.5
            pe.wait_ge(sem("r_xn"), i + 1)
            pe.wait_ge(sem("x4_done"), mixed)
            settle(pe)
            for j in range(J):
                last = nc.tensor.transpose(psC[0:64, 1, j * P:(j + 1) * P], r_ln["xn"][:, j], ident)
            last.then_inc(sem("r_xT"), 1)
            yield 25
            pe.wait_ge(sem("r_xTs"), i + 1)
            settle(pe)
            yield 32
            pe.wait_ge(sem("r_hr"), i * TT + 1)
            ps = psL[:, 0, :].rearrange("p (t q b) -> p t q b", q=2, b=LB)
            xv = r_xT[:].rearrange("p b t -> p t b")
            nc.tensor.matmul(ps[0:RM, :, 0], lua[:], xv, start=True, stop=False, skip_group_check=True)
            nc.tensor.matmul(ps[0:RM, :, 1], lub[:], xv, start=False, stop=False, skip_group_check=True).then_inc(sem("r_xp"), 1)

        def xproj_act(act, i):
            yield 22
            act.wait_ge(sem("r_xT"), i + 1)
            nc.scalar.activation(r_xT[0:64].rearrange("p b t -> p (b t)"), psC[0:64, 1, 0:256], ACT.Copy).then_inc(sem("r_xTs"), 1)

        def xproj_dve(dve, i):
            dve.wait_ge(sem("x5_done"), i + 2)
            yield from ln_vector(dve, "r", r_ln, X[:, i], i + 1, 18)

        TO = r_wk[:, 58:82:3]
        QT = TT // 4

        def lstm_pe(pe, i):
            pe.wait_ge(sem("r_xp"), i + 1)
            for t in range(TT):
                yield t - 0.5
                pe.wait_ge(sem("r_hr"), i * TT + (t + 1))
                h = r_h[:, t if t else TT].rearrange("p s b -> p (s b)")
                c = t * 2 * LB
                nc.tensor.matmul(psL[0:RM, 0, c:c + 2 * LB], lvab[:], h, start=False, stop=False, skip_group_check=True).then_inc(sem("r_z"), 1)

        def lstm_act(act, i):
            for t in range(TT):
                yield t - 0.5
                n = i * TT + (t + 1)
                c = t * 2 * LB
                act.wait_ge(sem("r_z"), n)
                o = r_wk[:, 2:2 + 84].rearrange("p (g x) -> p g x", x=28)[:, 0:2, 0:24:3]
                nc.scalar.activation(o, psL[0:64, 0, c:c + 2 * LB].rearrange("p (g b) -> p g b", b=LB), ACT.Tanh).then_inc(sem("r_gi"), 1)
                for s in range(2):
                    nc.scalar.activation(TO[32 * s:32 * s + 32], psL[64:RM, 0, c + s * LB:c + (s + 1) * LB], ACT.Tanh)
                yield t
                act.wait_ge(sem("r_c"), n)
                nc.scalar.activation(r_tc[:], r_c3[:, t % 2, 2::3], ACT.Tanh, scale=0.5).then_inc(sem("r_tc"), 1)

        def lstm_dve(dve, i):
            v = nc.vector
            for t in range(TT):
                yield t - 0.5
                n = i * TT + (t + 1)
                dve.wait_ge(sem("r_hc"), n)
                dve.wait_ge(sem("r_gi"), n)
                v.tensor_tensor_scan(r_c3[:, t % 2, :], r_wk[:, 0:24], r_wk[:, 30:54], 0.0, ALU.mult, ALU.add).then_inc(sem("r_c"), 1)
                yield t
                if t % QT == 0:
                    dve.wait_ge(sem("r_hT"), i * 4 + (t // QT + 1))
                dve.wait_ge(sem("r_tc"), n)
                for s in range(2):
                    last = v.scalar_tensor_tensor(r_h[64 * s:64 * s + 64, t + 1, s], TO, 1.0, r_tc[:], ALU.add, ALU.mult)
                last.then_inc(sem("r_hr"), 1)
                dve.wait_ge(sem("r_hr"), n + 1)
                v.scalar_tensor_tensor(r_wk[:, 32:56:3], r_h[0:64, t + 1, 0], 0.5, r_c3[:, t % 2, 2::3], ALU.mult, ALU.mult).then_inc(sem("r_hc"), 1)

        def lstm_pool(pool, i):
            for q in range(4):
                yield (22, 23, 26, 33)[q]
                pool.wait_ge(sem("r_hr"), i * TT + (QT * q + QT + 1))
                if q == 0:
                    pool.wait_ge(sem("p_hT"), i + 1)
                settle(pool)
                nc.gpsimd.tensor_copy(r_hT[:, :, QT * q:QT * q + QT].rearrange("p b t -> p t b"), r_h[0:64, QT * q + 1:QT * q + QT + 1, 0])\
                    .then_inc(sem("r_hT"), 1)

        def post_pe(pe, i, mixed):
            yield 21
            pe.wait_ge(sem("r_hT"), i * 4 + 8)
            pe.wait_ge(sem("x4_done"), mixed)
            settle(pe)
            for j in range(J):
                last = nc.tensor.transpose(psC[:, 0, j * C:(j + 1) * C], r_hT[:, j * B4:(j + 1) * B4].rearrange("p b t -> p (b t)"),
                                           ident[0:64, 0:64])
            last.then_inc(sem("p_hT"), 1)
            yield 24
            pe.wait_ge(sem("p_xn"), i + 1)
            nc.tensor.transpose(psC[:, 1, 2 * P:3 * P], p_ln["xn"][:].rearrange("p j c -> p (j c)"), ident).then_inc(sem("p_xT"), 1)
            yield 25
            pe.wait_ge(sem("x6_free"), i + 1)
            settle(pe)

        def post_dve(dve, i):
            yield 22
            dve.wait_ge(sem("p_hT"), i + 2)
            for j in range(J):
                last = nc.vector.scalar_tensor_tensor(X[:, i, j], psC[:, 0, j * C:(j + 1) * C], 0.5, X[:, i, j], ALU.mult, ALU.add)
            last.then_inc(sem("x6_done"), 1)
            dve.wait_ge(sem("x6_done"), i + 1)
            yield from ln_vector(dve, "p", p_ln, X[:, i], i + 1, 22)

        def post_act(act, i):
            yield 24
            act.wait_ge(sem("p_xT"), i + 1)
            nc.scalar.activation(img[:, :, i + 3, 3:3 + IMG], psC[:, 1, 2 * P:3 * P].rearrange("p (b t) -> p b t", b=B4), ACT.Copy)\
                .then_inc(sem("x6_free"), 1)

        def at_slot(slot, step, *args):
            yield slot
            step(*args)

        def weave(parts):
            slots = [(0, g) for g in parts]
            slot = 0
            while slots:
                left = []
                for due, g in slots:
                    while due <= slot:
                        due = next(g, None)
                        if due is None:
                            break
                    if due is not None:
                        left.append((due, g))
                slots = left
                slot += 0.5

        CREDITS = dict(x1_done=1, x3_done=1, x4_done=1, x5_done=1, r_hr=1, r_hc=1, r_hT=4, p_hT=1, a_halo=2)
        M1 = ("m1gate", "m1gateb", "m1w1", "m1w2", "m1b2")
        LAG = dict(post=-1, lstm=0, xproj=1, mix=2, ffn=3, mamba=4, norm=5)
        FIRST_FULL, LAST_FULL = 1, NT - 1 - LAG["norm"]

        def turns(eng, parts_of, late):
            def turn(i):
                has = (lambda k: 0 <= i + LAG[k] < NT) if isinstance(i, int) else (lambda k: True)
                weave([part(i + LAG[k] if LAG[k] else i) for k, part in parts_of(i) if has(k)])

            for i in range(-LAG["norm"], FIRST_FULL):
                if i == -LAG["ffn"]:
                    late()
                turn(i)
            with eng.Fori(FIRST_FULL, LAST_FULL + 1) as i:
                turn(i)
            for i in range(LAST_FULL + 1, NT + 1):
                turn(i)

        @block.sync
        def _(sp):
            sp.dma_start(W[:, 0:NFIRST], pack_in[:, 0:NFIRST]).then_inc(sem("w_in"), 16)
            sp.dma_start(X[:, 0:3], x_in[:, 0:3]).then_inc(sem("x_in"), 16)
            sp.dma_start(W[:, NFIRST:], pack_in[:, NFIRST:]).then_inc(sem("w_late"), 16)
            sp.dma_start(X[:, 3:], x_in[:, 3:]).then_inc(sem("x_late"), 16)
            acc_load(sp, 0, 0, acc1_in)
            acc_load(sp, 0, 1, acc2_in)
            turns(sp, lambda i: [
                ("post", lambda n: x6_store(sp, n)),
                ("mix", lambda n: acc_next(sp, n, 1, acc2_in)),
                ("ffn", lambda n: acc_next(sp, n, 0, acc1_in))], lambda: None)
            sp.wait_ge(sem("x6_out"), NT * 32)

        @block.gpsimd
        def _(pool):
            g = nc.gpsimd
            g.memset(img[:], 0.0).then_inc(sem("img_zeroed"), 1)

            def late():
                pool.wait_ge(sem("w_late"), 16)
                for l in (1, 2):
                    g.tensor_scalar(bn0s[:, l - 1], w(f"f0v{l}"), 1.0, 1e-3, ALU.mult, ALU.add)
                g.tensor_scalar(bn3s[:], w("bnv"), 1.0, 1e-5, ALU.mult, ALU.add).then_inc(sem("pool_bn"), 1)
                pool.wait_ge(sem("pool_bn"), 1)
                for l in (1, 2):
                    g.tensor_tensor(bn0s[:, l - 1], bn0s[:, l - 1], epst[:, 0:4], ALU.pow)
                g.tensor_tensor(bn3s[:], bn3s[:], epst[:, 0:1], ALU.pow).then_inc(sem("pool_bn"), 1)
                pool.wait_ge(sem("late"), 1)

            pool.wait_ge(sem("setup"), 1)

            def ln_at(slot, k, buf, eps, i):
                return at_slot(slot, ln_pool, pool, k, buf, eps, i + 1)

            turns(pool, lambda i: [
                ("lstm", lambda n: lstm_pool(pool, n)),
                ("post", lambda n: ln_at(22, "p", p_ln, 1e-6, n)),
                ("xproj", lambda n: ln_at(18, "r", r_ln, 1e-5, n)),
                ("mix", lambda n: ln_at(2, "m0", mix1["ln"], 1e-5, n)),
                ("mix", lambda n: experts_pool(pool, n, "m0", mix1["big"], 20, "x4_done")),
                ("mix", lambda n: ln_at(21, "c1", c_ln[1], 1e-6, n)),
                ("ffn", lambda n: ln_at(0, "f", f_ln, 1e-5, n)),
                ("ffn", lambda n: experts_pool(pool, n, "f", f_big, 24, "x2_done")),
                ("ffn", lambda n: ln_at(25, "c0", c_ln[0], 1e-6, n)),
                ("mamba", lambda n: mamba_pool(pool, n)),
                ("norm", lambda n: ln_at(28, "a", a_ln, 1e-6, n))], late)

        @block.scalar
        def _(act):
            act.wait_ge(sem("w_in"), 16)
            for k in range(NB):
                for j in range(J):
                    nc.scalar.activation(aneg[:, k, j], w(f"alog{k}"), ACT.Exp)
            nc.scalar.activation(decay_read[:], w("normw0"), ACT.Copy).then_inc(sem("act_setup"), 1)
            act.wait_ge(sem("setup"), 1)
            turns(act, lambda i: [
                ("lstm", lambda n: lstm_act(act, n)),
                ("post", lambda n: post_act(act, n)),
                ("xproj", lambda n: xproj_act(act, n)),
                ("mix", lambda n: moe_act(act, n, "m0", mix1, psC, 8, "m1b1")),
                ("mix", lambda n: prod_act(act, n, 1, psC, 21)),
                ("ffn", lambda n: ffn0_act(act, n)),
                ("ffn", lambda n: prod_act(act, n, 0, psB, 25)),
                ("mamba", lambda n: mamba_act(act, n))], lambda: act.wait_ge(sem("late"), 1))

        @block.vector
        def _(dve):
            v = nc.vector
            v.memset(epst[:], -0.5)
            v.memset(ones3[:], 1.0)
            v.memset(bias3[:], 0.0)
            v.memset(epss[:, :, 0], 1e-5)
            v.memset(epss[:, :, 1], 1e-6)
            v.memset(hb[:], 0.0)
            v.memset(hh[:], 0.0)
            v.memset(a_h0[:], 0.0)
            for n in range(NSER):
                v.memset(a_h1[:, :, n], 1.0 / (2 * (NSER - n) - 1))
            v.memset(state[:], 0.0)
            for k in (0, 1):
                v.memset(c_eT[k][:], 0.0)
            v.memset(r_xT[64:65], 1.0)
            v.memset(mix1["g"][:], NEG)
            v.memset(mix1["rep"][:], NEG)
            v.memset(r_c3[:], 0.0)
            v.memset(r_h[:], 0.0)
            v.memset(r_wk[:], 0.0).then_inc(sem("zeroed"), 1)
            dve.wait_ge(sem("zeroed"), 1)
            v.memset(r_wk[:, 1:24:3], 1.0)
            for k in (0, 1):
                for h in range(2):
                    v.memset(c_eT[k][64 * h:64 * h + 64, h, B], 1.0)
            v.memset(r_wk[:, 31:54:3], 1.0).then_inc(sem("zeroed"), 1)
            dve.wait_ge(sem("zeroed"), 2)
            dve.wait_ge(sem("img_zeroed"), 1)
            dve.wait_ge(sem("w_in"), 16)
            dve.wait_ge(sem("x_in"), 16)
            dve.wait_ge(sem("act_setup"), 1)

            def split_biases(names, c0, c1, base):
                bias = W[0:1, COL[names[0][0]][1]:COL[names[0][0]][1] + c1 - c0]
                part, rest = bpart[:, :, c0:c1], brest[:, c0:c1]
                st = Steps(dve, sem(f"bias_steps{base}"), 0, 5)
                for n in range(3):
                    st.did(v.tensor_copy(part[:, n], bias if n == 0 else rest)); st.wait()
                    v.tensor_copy(bias3[32 * n:32 * n + 1, c0:c1], part[:, n])
                    if n < 2:
                        st.did(v.tensor_tensor(rest, bias if n == 0 else rest, part[:, n], ALU.subtract)); st.wait()
                st.end()

            split_biases(BIASES, 0, NBIAS0, 0)
            for k in range(NB):
                for q in range(2):
                    v.tensor_tensor(wpair[:, k, q], w(f"wxbc{k}"), w(f"taps{k}", q * XBC, (q + 1) * XBC), ALU.mult)
                v.tensor_scalar(wout[:, k], w(f"wout{k}"), w(f"normw{k}"), None, ALU.mult)
                for j in range(J):
                    v.tensor_scalar(dhalf[:, k, j], w(f"dskip{k}"), 0.5, None, ALU.mult)
            v.tensor_scalar(aneg[:].rearrange("p k j h -> p (k j h)"), aneg[:].rearrange("p k j h -> p (k j h)"), -1.0, None, ALU.mult)\
                .then_inc(sem("dve_setup"), 1)
            dve.wait_ge(sem("dve_setup"), 1)
            for name, count in CREDITS.items():
                dve.sem_inc(sem(name), count)
            dve.sem_inc(sem("setup"), 1)

            def late():
                dve.wait_ge(sem("w_late"), 16)
                dve.wait_ge(sem("x_late"), 16)
                dve.wait_ge(sem("pool_bn"), 2)
                split_biases(LATE_BIASES, NBIAS0, NBIAS, 1)
                v.tensor_scalar(wr8[:], w("wr"), 1.0 / B, None, ALU.mult)
                for l in (0, 1):
                    v.tensor_tensor(bn0s[:, l], bn0s[:, l], w(f"f0g{l + 1}"), ALU.mult)
                    v.tensor_tensor(bn0b[:, l], w(f"f0b{l + 1}"), w(f"f0m{l + 1}"), ALU.subtract)
                v.tensor_tensor(bn3s[:], bn3s[:], w("bng"), ALU.mult).then_inc(sem("dve_setup"), 1)
                dve.wait_ge(sem("dve_setup"), 2)
                v.tensor_tensor(bn0b[:].rearrange("p l q -> p (l q)"), bn0b[:].rearrange("p l q -> p (l q)"),
                                bn0s[:].rearrange("p l q -> p (l q)"), ALU.mult)
                v.tensor_tensor(bn3b[:], bn3s[:], w("bnm"), ALU.mult).then_inc(sem("dve_setup"), 1)
                dve.wait_ge(sem("dve_setup"), 3)
                for l in (0, 1):
                    v.tensor_tensor(bn0b[:, l], bn0b[:, l], w(f"f0be{l + 1}"), ALU.add)
                v.tensor_tensor(bn3b[:], w("bnb"), bn3b[:], ALU.subtract)
                v.tensor_copy(lua[:, 0:64], w("ua", 0, 64))
                v.tensor_scalar(lua[:, 64:RM], w("ua", 64, RM), 0.5, None, ALU.mult)
                v.tensor_scalar(lub[:], w("ub"), 0.5, None, ALU.mult)
                v.tensor_scalar(lvab[0:64, 64:RM], w("vab", 64, RM)[0:64], 0.25, None, ALU.mult)
                v.tensor_scalar(lvab[64:P], w("vab")[64:P], 0.25, None, ALU.mult)
                v.tensor_scalar(lvab[0:64, 0:64], w("vab", 0, 64)[0:64], 0.5, None, ALU.mult)
                v.tensor_scalar(wqs[:], w("wq"), w("ascale")[0:64], None, ALU.mult).then_inc(sem("dve_setup"), 1)
                dve.wait_ge(sem("dve_setup"), 4)
                dve.sem_inc(sem("late"), 1)

            turns(dve, lambda i: [
                ("lstm", lambda n: lstm_dve(dve, n)),
                ("post", lambda n: post_dve(dve, n)),
                ("xproj", lambda n: xproj_dve(dve, n)),
                ("mix", lambda n: moe_dve(dve, n, "m0", mix1, psC, X[:, n], (sem("x3_done"), n + 2), "x4_done", False)),
                ("mix", lambda n: prod_dve(dve, n, 1, psC, 21, "x4_done", "x5_done")),
                ("ffn", lambda n: ffn0_dve(dve, n)),
                ("ffn", lambda n: prod_dve(dve, n, 0, psB, 25, "x2_done", "x3_done")),
                ("mamba", lambda n: mamba_dve(dve, n)),
                ("norm", lambda n: norm_dve(dve, n))], late)

        @block.tensor
        def _(pe):
            def mixed(i):
                last = i + LAG["mix"]
                return (min(last, NT - 1) if isinstance(i, int) else last) + 2

            pe.wait_ge(sem("setup"), 1)
            turns(pe, lambda i: [
                ("lstm", lambda n: lstm_pe(pe, n)),
                ("post", lambda n: post_pe(pe, n, mixed(i))),
                ("xproj", lambda n: xproj_pe(pe, n, mixed(i))),
                ("mix", lambda n: moe_pe(pe, n, "m0", mix1, psC, 8, M1, (sem("x5_done"), n + 1))),
                ("mix", lambda n: prod_pe(pe, n, 1, psC, 21)),
                ("ffn", lambda n: ffn0_pe(pe, n)),
                ("ffn", lambda n: prod_pe(pe, n, 0, psB, 25)),
                ("mamba", lambda n: mamba_pe(pe, n))], lambda: pe.wait_ge(sem("late"), 1))

        block_ctx.__exit__(None, None, None)
        next_phase()
        phase1.close()

        NU = IMG * IMG // P
        XN = X[:].rearrange("p i j c -> p (i j) c")
        HALF = IMG * IMG // 2
        Y3 = resident("Y3", P, B4, IMG * IMG)
        conv = ExitStack()
        dg = conv.enter_context(nc.sbuf_tensor("dg", [P, KT * KT, P], F32))
        DVE_CHUNKS, POOL_CHUNKS, PE_CHUNKS = range(0, 3), range(3, 5), range(5, 8)

        def chunk(q):
            return Y3[:, q // 2, (q % 2) * HALF:(q % 2 + 1) * HALF]

        prod = conv.enter_context(nc.sbuf_tensor("prod", [P, 4, HALF], F32))

        def window(q, ky, kx):
            r0 = (q % 2) * 16
            return img[:, q // 2, r0 + ky:r0 + ky + 16, kx:kx + IMG] if isinstance(ky, int) else \
                img[:, q // 2, bass.ds(ky + r0, 16), kx:kx + IMG]

        with nc.Block() as block:
            @block.sync
            def _(sp):
                sp.dma_start(XN, x6d[:, :, :].rearrange("b (u p) c -> p (b u) c", p=P)).then_inc(sem("xn_in"), 16)
                sp.wait_ge(sem("xn_in"), 16)

            @block.vector
            def _(dve):
                v = nc.vector
                for ky in range(KT):
                    v.tensor_tensor(dg[:, ky * KT:(ky + 1) * KT], bc(ident, 1, KT), bc(w("dw")[:, ky * KT:(ky + 1) * KT], 2, P), ALU.mult)\
                        .then_inc(sem("diag"), 1)
                for q in DVE_CHUNKS:
                    last = v.memset(chunk(q), 0.0)
                last.then_inc(sem("dve_tap"), 1)
                with dve.Fori(0, KT) as ky:
                    for kx in range(KT):
                        dve.wait_ge(sem("dve_tap"), ky * KT + (kx + 1))
                        for q in DVE_CHUNKS:
                            o = chunk(q).rearrange("p (r t) -> p r t", r=16)
                            last = v.scalar_tensor_tensor(o, window(q, ky, kx), w("dw")[:, bass.ds(ky * KT + kx, 1)], o, ALU.mult, ALU.add)
                        last.then_inc(sem("dve_tap"), 1)

            @block.gpsimd
            def _(pool):
                g = nc.gpsimd
                for n, q in enumerate(POOL_CHUNKS):
                    o = chunk(q)
                    for t in range(1, KT * KT):
                        m = n * (KT * KT - 1) + t
                        pool.wait_ge(sem("prod"), n * KT * KT + t + 1)
                        if m > 1:
                            pool.wait_ge(sem("pool_tap"), m - 1)
                        g.tensor_tensor(o, o, prod[:, t % 4], ALU.add).then_inc(sem("pool_tap"), 1)

            @block.scalar
            def _(act):
                def relu_norm(n, q, source):
                    nc.scalar.activation(chunk(q), source, ACT.Relu).then_inc(sem("relu"), 1)
                    act.wait_ge(sem("relu"), n + 1)
                    nc.scalar.activation(chunk(q), chunk(q), ACT.Identity, scale=bn3s[:], bias=bn3b[:]).then_inc(sem("y3"), 1)

                act.wait_ge(sem("wvo"), 1)
                nc.scalar.activation(wvo[:], psB[0:64, 0, 0:64], ACT.Copy).then_inc(sem("wvos"), 1)
                for n, q in enumerate(POOL_CHUNKS):
                    for t in range(KT * KT):
                        if n == 0 and t == 40:
                            act.wait_ge(sem("dw_mm"), 1)
                            relu_norm(0, PE_CHUNKS[0], psA[:, 0, :])
                        to = prod[:, t % 4] if t else chunk(q)
                        used = n * (KT * KT - 1) + t - 4
                        if t > 4:
                            act.wait_ge(sem("pool_tap"), used)
                        elif t and n:
                            act.wait_ge(sem("pool_tap"), n * (KT * KT - 1))
                        nc.scalar.activation(to.rearrange("p (r t) -> p r t", r=16), window(q, t // KT, t % KT), ACT.Copy, scale=w("dw")[:, t:t + 1])\
                            .then_inc(sem("prod"), 1)
                for n in (1, 2):
                    act.wait_ge(sem("dw_mm"), n + 1)
                    relu_norm(n, PE_CHUNKS[n], psA[:, n % 2, :])
                n = len(PE_CHUNKS)
                for chunks, done, count in ((POOL_CHUNKS, "pool_tap", len(POOL_CHUNKS) * (KT * KT - 1)), (DVE_CHUNKS, "dve_tap", KT * KT + 1)):
                    act.wait_ge(sem(done), count)
                    for q in chunks:
                        relu_norm(n, q, chunk(q))
                        n += 1

            @block.tensor
            def _(pe):
                nc.tensor.matmul(psB[0:64, 0, 0:64], w("wvT"), w("wo3"), start=True, stop=True).then_inc(sem("wvo"), 1)
                for n, q in enumerate(PE_CHUNKS):
                    if n >= 2:
                        pe.wait_ge(sem("relu"), n - 1)
                    for t in range(KT * KT):
                        if t % KT == 0 and n == 0:
                            pe.wait_ge(sem("diag"), t // KT + 1)
                        last = nc.tensor.matmul(psA[:, n % 2, :].rearrange("p (r t) -> p r t", r=16), dg[:, t], window(q, t // KT, t % KT),
                                                start=(t == 0), stop=(t == KT * KT - 1))
                    last.then_inc(sem("dw_mm"), 1)

        next_phase()
        conv.close()

        def sb2(name, *shape):
            return ctx.enter_context(nc.sbuf_tensor(name, list(shape), F32))

        ys = sb2("ys", 64, 2, IMG * IMG)
        qs = sb2("qs", 64, 2, IMG * IMG); ks = sb2("ks", 64, 2, IMG * IMG); vs = sb2("vs", P, 2, NU, C)
        nmax = sb2("nmax", P, 2); rsum = sb2("rsum", P, 2); rinv = sb2("rinv", P, 2)
        at = sb2("at", P, 2, IMG * IMG); atT = sb2("atT", P, 2, NU, P)
        oT = sb2("oT", C, 2, P)
        pss = [psA, psB]

        with nc.Block() as block:
            @block.sync
            def _(sp):
                for n in range(2):
                    sp.dma_start(ys[:, n], Y3[64 * n:64 * n + 64, 0, :]).then_inc(sem(f"ys{n}"), 16)
                with sp.Fori(1, B4) as b:
                    for n in range(2):
                        sp.wait_ge(sem("v_mm"), b * 2 + (n - 1))
                        sp.dma_start(ys[:, n], Y3[64 * n:64 * n + 64, b, :]).then_inc(sem(f"ys{n}"), 16)

            @block.tensor
            def _(pe):
                with pe.Fori(0, B4) as b:
                    for n in range(2):
                        m = b * 2 + (n + 1)
                        g0 = b * (2 * NU) + n * NU
                        pe.wait_ge(sem(f"ys{n}"), b * 16 + 16)
                        pe.wait_ge(sem("a_exp"), g0 + 2)
                        settle(pe)
                        for h in range(2):
                            nc.tensor.matmul(psA[0:64, h, :], wqs[:], ys[:, n, h * 512:(h + 1) * 512], start=True, stop=True)
                            last = nc.tensor.matmul(psB[0:64, h, :], w("wk"), ys[:, n, h * 512:(h + 1) * 512], start=True, stop=True)
                        last.then_inc(sem("qk_mm"), 1)
                        pe.wait_ge(sem("at_c0"), g0 + 2)
                        settle(pe)
                        for u in range(NU):
                            last = nc.tensor.matmul(psC[:, 0, u * C:(u + 1) * C], ys[:, n, u * P:(u + 1) * P], wvo[:], start=True, stop=True)
                        last.then_inc(sem("v_mm"), 1)
                        pe.wait_ge(sem("q_s"), m)
                        pe.wait_ge(sem("k_s"), m)

                        def scores(u):
                            pe.wait_ge(sem("a_exp"), g0 + (u + 1))
                            for h in range(2):
                                last = nc.tensor.matmul(pss[u % 2][:, h, :], qs[:, n, u * P:(u + 1) * P], ks[:, n, h * 512:(h + 1) * 512],
                                                        start=True, stop=True)
                            last.then_inc(sem("sc"), 1)

                        def turn_back(u):
                            pe.wait_ge(sem("oT"), g0 + (u + 1))
                            settle(pe)
                            nc.tensor.transpose(psL[:, u % 2, 2 * P:2 * P + C], oT[:, u % 2], ident[0:C, 0:C]).then_inc(sem("ob"), 1)

                        scores(0)
                        for u in range(NU):
                            if u + 1 < NU:
                                scores(u + 1)
                            if u:
                                turn_back(u - 1)
                            pe.wait_ge(sem("a_exp"), g0 + (u + 3))
                            if u == 0:
                                pe.wait_ge(sem("v_s"), m)
                            for c in range(NU):
                                if c == 0:
                                    pe.wait_ge(sem("at_c0"), g0 + (u + 2))
                                if c == 4:
                                    pe.wait_ge(sem("at_c1"), g0 + (u + 2))
                                last = nc.tensor.transpose(psC[:, c // 4, (c % 4) * P:(c % 4 + 1) * P], at[:, u % 2, c * P:(c + 1) * P], ident)
                                if c == 3:
                                    last.then_inc(sem("aT0"), 1)
                            last.then_inc(sem("aT1"), 1)
                            pe.wait_ge(sem("xo"), g0 + (u + 1))
                            for c in range(NU):
                                if c == 0:
                                    pe.wait_ge(sem("at_c0"), g0 + (u + 3))
                                if c == 4:
                                    pe.wait_ge(sem("at_c1"), g0 + (u + 3))
                                last = nc.tensor.matmul(psL[0:C, u % 2, 0:P], vs[:, n, c], atT[:, u % 2, c], start=(c == 0), stop=(c == NU - 1))
                            last.then_inc(sem("av"), 1)
                        turn_back(NU - 1)

            @block.scalar
            def _(act):
                with act.Fori(0, B4) as b:
                    for n in range(2):
                        m = b * 2 + (n + 1)
                        g0 = b * (2 * NU) + n * NU
                        act.wait_ge(sem("qk_mm"), m)
                        nc.scalar.activation(qs[:, n].rearrange("p (h t) -> p h t", h=2), psA[0:64, :, :], ACT.Copy).then_inc(sem("q_s"), 1)
                        act.wait_ge(sem("v_mm"), m)
                        nc.scalar.activation(vs[:, n].rearrange("p u c -> p (u c)"), psC[:, 0, :], ACT.Copy).then_inc(sem("v_s"), 1)
                        for u in range(NU):
                            act.wait_ge(sem("nmax"), g0 + (u + 1))
                            act.wait_ge(sem("aT1"), g0 + (u + 1))
                            nc.scalar.activation(at[:, u % 2].rearrange("p (h t) -> p h t", h=2), pss[u % 2][:], ACT.Exp,
                                                 bias=nmax[:, u % 2:u % 2 + 1], accum_out=rsum[:, u % 2:u % 2 + 1]).then_inc(sem("a_exp"), 1)
                            act.wait_ge(sem("aT0"), g0 + (u + 1))
                            act.wait_ge(sem("av"), g0 + (u + 1))
                            nc.scalar.activation(atT[:, u % 2, 0:4].rearrange("p c q -> p (c q)"), psC[:, 0, :], ACT.Copy).then_inc(sem("at_c0"), 1)

            @block.vector
            def _(dve):
                v = nc.vector
                for name in ("a_exp", "at_c0", "at_c1", "aT1", "av", "xo"):
                    dve.sem_inc(sem(name), 2)
                with dve.Fori(0, B4) as b:
                    for n in range(2):
                        m = b * 2 + (n + 1)
                        g0 = b * (2 * NU) + n * NU
                        dve.wait_ge(sem("qk_mm"), m)
                        v.tensor_scalar(ks[:, n].rearrange("p (h t) -> p h t", h=2), psB[0:64, :, :], 0.0, None, ALU.max).then_inc(sem("k_s"), 1)
                        for u in range(NU + 1):
                            if u < NU:
                                dve.wait_ge(sem("sc"), g0 + (u + 1))
                                dve.wait_ge(sem("a_exp"), g0 + (u + 1))
                                v.tensor_reduce(nmax[:, u % 2:u % 2 + 1], pss[u % 2][:].rearrange("p h t -> p (h t)"), AX, ALU.max, negate=True)\
                                    .then_inc(sem("nmax"), 1)
                            if u:
                                r = (u - 1) % 2
                                dve.wait_ge(sem("aT1"), g0 + (u + 2))
                                dve.wait_ge(sem("av"), g0 + u)
                                v.tensor_copy(atT[:, r, 4:8].rearrange("p c q -> p (c q)"), psC[:, 1, :]).then_inc(sem("at_c1"), 1)
                                v.reciprocal(rinv[:, r:r + 1], rsum[:, r:r + 1]).then_inc(sem("rinv"), 1)
                                dve.wait_ge(sem("av"), g0 + (u + 2))
                                v.tensor_copy(oT[:, r], psL[0:C, r, 0:P]).then_inc(sem("oT"), 1)
                                dve.wait_ge(sem("rinv"), g0 + u)
                                dve.wait_ge(sem("ob"), g0 + u)
                                xo = XN[:, bass.ds(n * B4 * NU + b * NU + (u - 1), 1), :].rearrange("p o c -> p (o c)")
                                v.scalar_tensor_tensor(xo, psL[:, r, 2 * P:2 * P + C], rinv[:, r:r + 1], xo, ALU.mult, ALU.add).then_inc(sem("xo"), 1)

        next_phase()

        LANES = 4
        SKEW = 5
        mixes = [moe_bufs(f"mix{k}", sb2, 4) for k in range(LANES)]
        banks = [psA, psB, psC, psL]
        M2 = ("m2gate", "m2gateb", "m2w1", "m2w2", "m2b2")
        o_v = out.rearrange("b (u p) c -> p (b u) c", p=P)
        XT = X[:]

        with nc.Block() as block:
            @block.sync
            def _(sp):
                with sp.Fori(0, NT // LANES) as i:
                    for k in range(LANES):
                        sp.wait_ge(sem(f"done{k}"), i + 2)
                        sp.dma_start(o_v[:, bass.ds(i * (2 * LANES) + 2 * k, 2), :], XN[:, bass.ds(i * (2 * LANES) + 2 * k, 2), :])\
                            .then_inc(sem("out"), 16)
                sp.wait_ge(sem("out"), NT * 16)

            @block.gpsimd
            def _(pool):
                with pool.Fori(0, NT // LANES) as i:
                    for k in range(LANES):
                        ln_pool(pool, f"m{k}", mixes[k]["ln"], 1e-5, i + 1)

            @block.scalar
            def _(act):
                with act.Fori(0, NT // LANES) as i:
                    weave([moe_act(act, i, f"m{k}", mixes[k], banks[k], 4, "m2b1", SKEW * k) for k in range(LANES)])

            @block.vector
            def _(dve):
                for k in range(LANES):
                    nc.vector.memset(mixes[k]["g"][:], NEG)
                    last = nc.vector.memset(mixes[k]["rep"][:], NEG)
                last.then_inc(sem("pad"), 1)
                dve.wait_ge(sem("pad"), 1)
                for k in range(LANES):
                    dve.sem_inc(sem(f"done{k}"), 1)
                with dve.Fori(0, NT // LANES) as i:
                    weave([moe_dve(dve, i, f"m{k}", mixes[k], banks[k], XT[:, bass.ds(i * LANES + k, 1)].rearrange("p o j c -> p (o j) c"),
                                          None, f"done{k}", True, SKEW * k) for k in range(LANES)])

            @block.tensor
            def _(pe):
                with pe.Fori(0, NT // LANES) as i:
                    weave([moe_pe(pe, i, f"m{k}", mixes[k], banks[k], 4, M2, (sem(f"done{k}"), i + 1), SKEW * k) for k in range(LANES)])


def kernel(**inputs):
    import concourse.bacc as bacc
    from concourse.bass_utils import run_bass_kernel_spmd

    a = {k: np.asarray(v) for k, v in inputs.items()}
    pack = np.zeros((P, NPACK), np.float32)

    def put(name, v):
        r, at, c = COL[name]
        pack[0:r, at:at + c] = np.asarray(v).reshape(r, c)

    def rows(v, n=P):
        return np.tile(np.asarray(v).reshape(1, -1), (n, 1))

    def pairs(v):
        o = np.zeros((P, 4, 2, v.shape[2]), np.float32)
        for e in range(E):
            o[64 * (e % 2):64 * (e % 2) + 64, e // 2, e % 2] = v[e]
        return o

    def pairv(v):
        return v.reshape(4, 2 * 64).T

    p = np.arange(P)
    same = (p[:, None] // TT) == (p[None, :] // TT)
    put("ident", np.eye(P))
    put("triblk", same & (p[:, None] <= p[None, :]))
    put("strictblk", same & (p[:, None] > p[None, :]))
    put("indblk", (p[:, None] // TT) == (p[None, :] // DS) % B4)
    put("tri32", (p[:, None] % TT) <= np.arange(TT)[None, :])
    put("maskb", 0.5 * ((p[:, None] // TT) == np.arange(B4)[None, :]))
    for k in range(NB):
        wi, cw = a["L0_conv_in_proj_w"][k], a["L0_conv_conv_w"][k][:, 0]
        put(f"wzd{k}", np.concatenate([wi[0:DI], wi[DI + XBC:]]).T)
        put(f"wxbc{k}", np.concatenate([wi[DI:DI + XBC].T] * 2))
        taps = np.concatenate([rows(cw[:, 3], 64), rows(cw[:, 2], 64)]), np.concatenate([rows(cw[:, 1], 64), rows(cw[:, 0], 64)])
        put(f"taps{k}", np.concatenate(taps, 1))
        put(f"bias{k}", np.concatenate([np.zeros(DI, np.float32), a["L0_conv_dt_bias"][k], a["L0_conv_conv_b"][k]]))
        put(f"alog{k}", rows(a["L0_conv_A_log"][k]))
        put(f"dskip{k}", rows(a["L0_conv_D"][k]))
        put(f"normw{k}", a["L0_conv_norm_w"][k])
        put(f"wout{k}", np.concatenate([a["L0_conv_out_proj_w"][k].T] * 2, 1))
    put("wr", a["L0_ffn_Wr"]); put("br", a["L0_ffn_br"])
    put("f0w1", a["L0_ffn_W1"].transpose(1, 0, 2)); put("f0w2", pairs(a["L0_ffn_W2"])); put("f0wo", pairs(a["L0_ffn_Wo"]))
    put("f0bo", a["L0_ffn_bo"])
    for l in (1, 2):
        for n, k in (("b", "b"), ("g", "g"), ("be", "be"), ("m", "m"), ("v", "v")):
            put(f"f0{n}{l}", pairv(a[f"L0_ffn_{k}{l}"]))
    put("m1gate", a["L1_ffn_gate_w"]); put("m1gateb", a["L1_ffn_gate_b"]); put("m1w1", a["L1_ffn_W1"].transpose(1, 0, 2))
    put("m1b1", a["L1_ffn_b1"].T); put("m1w2", a["L1_ffn_W2"].transpose(1, 0, 2)); put("m1b2", a["L1_ffn_b2"])
    u, v, bb = ({g: a[f"L2_ffn_{n}_{g}"] for g in "cio"} for n in "UVb")
    ub = {g: np.concatenate([u[g], bb[g][None]]) for g in "cio"}
    put("ua", np.concatenate([ub["c"], ub["o"][:, :32]], 1)); put("ub", np.concatenate([ub["i"], ub["o"][:, 32:]], 1))
    put("vab", np.concatenate([np.concatenate([v["c"], v["o"][:, :32]], 1), np.concatenate([v["i"], v["o"][:, 32:]], 1)]))
    put("dw", np.tile(a["L3_conv_dw_kernel"].reshape(KT * KT, C).T, (2, 1)))
    for n, k in (("bng", "gamma"), ("bnb", "beta"), ("bnm", "mean"), ("bnv", "var")):
        put(n, np.tile(a[f"L3_conv_bn_{k}"], 2))
    put("wq", a["L3_conv_wq"]); put("wk", a["L3_conv_wk"]); put("wvT", a["L3_conv_wv"].T); put("wo3", a["L3_conv_wo"])
    put("ascale", np.full(P, a["L3_conv_attn_scale"]))
    put("m2gate", a["L3_ffn_router_w"].T); put("m2gateb", np.zeros(E)); put("m2w1", a["L3_ffn_w1"].transpose(1, 0, 2))
    put("m2b1", pairv(a["L3_ffn_b1"])); put("m2w2", pairs(a["L3_ffn_w2"])); put("m2b2", a["L3_ffn_b2"])

    x = a["x"].reshape(J, B4, NT, TT, C).transpose(1, 3, 2, 0, 4).reshape(P, NT, J, C)
    accs = [a[f"L{l}_conv_accumulators"].reshape(NT, 2, 16, C, C).transpose(0, 1, 3, 2, 4).reshape(NT, P, 16, C) for l in (1, 2)]
    arrays = {"x_in": x, "pack_in": pack, "acc1_in": accs[0], "acc2_in": accs[1]}
    arrays = {k: np.ascontiguousarray(v) for k, v in arrays.items()}

    nc = bacc.Bacc("TRN2", target_bir_lowering=False, num_devices=1)
    args = [nc.dram_tensor(k, v.shape, F32, kind="ExternalInput").ap() for k, v in arrays.items()]
    o = nc.dram_tensor("out_x", (B, IMG * IMG, C), F32, kind="ExternalOutput").ap()
    build(nc, *args, o)
    r = run_bass_kernel_spmd(nc, [arrays], core_ids=[0]).results[0]["out_x"]
    return np.asarray(r).reshape(B, IMG, IMG, C)
```
